# Optimizing a Trainium2 kernel written in Bass

```python
import numpy as np
import jax
import jax.numpy as jnp

def _softmax(x, axis=-1):
    return jax.nn.softmax(x, axis=axis)

def _gelu(x):
    return jax.nn.gelu(x, approximate=True)

def _silu(x):
    return jax.nn.silu(x)

def _sigmoid(x):
    return jax.nn.sigmoid(x)

def _layernorm(x, axis=-1, eps=1e-05):
    m = jnp.mean(x, axis=axis, keepdims=True)
    v = jnp.var(x, axis=axis, keepdims=True)
    return (x - m) / jnp.sqrt(v + eps)

def _scatter_add(tgt, idx, src, axis=0):
    return tgt.at[idx].add(src)

def _segment_sum(src, seg, n):
    return jax.ops.segment_sum(src, seg, n)
kernel_name = 'mk_seq_postln_d1_jaxref_r8_484513'

def setup_inputs(seed: int=0):
    np.random.seed(seed)
    _w = jnp.asarray

    def _L0_attn_setup():
        import jax, jax.numpy as jnp
        import numpy as np
        D_MODEL, N_HEADS = (128, 16)
        D_H = D_MODEL // N_HEADS
        D_HR = D_H // 2
        D_LATENT = 32
        THETA = 10000.0

        def rope(x, theta=THETA):
            S, d = (x.shape[-2], x.shape[-1])
            inv = theta ** (-jnp.arange(0, d, 2, dtype=jnp.float32) / d)
            ang = jnp.arange(S, dtype=jnp.float32)[:, None] * inv
            cos, sin = (jnp.cos(ang), jnp.sin(ang))
            x1, x2 = (x[..., 0::2], x[..., 1::2])
            r1 = x1 * cos - x2 * sin
            r2 = x1 * sin + x2 * cos
            return jnp.stack([r1, r2], axis=-1).reshape(x.shape)
        key = jax.random.key(seed)
        ks = jax.random.split(key, 9)
        s = lambda fan_in: 1.0 / np.sqrt(fan_in)
        return {'x': jax.random.normal(ks[0], (4, 256, D_MODEL), jnp.float32), 'W_DQ': jax.random.normal(ks[1], (D_MODEL, D_LATENT), jnp.float32) * s(D_MODEL), 'W_UQ': jax.random.normal(ks[2], (D_LATENT, N_HEADS * D_H), jnp.float32) * s(D_LATENT), 'W_QR': jax.random.normal(ks[3], (D_LATENT, N_HEADS * D_HR), jnp.float32) * s(D_LATENT), 'W_DKV': jax.random.normal(ks[4], (D_MODEL, D_LATENT), jnp.float32) * s(D_MODEL), 'W_UK': jax.random.normal(ks[5], (D_LATENT, N_HEADS * D_H), jnp.float32) * s(D_LATENT), 'W_UV': jax.random.normal(ks[6], (D_LATENT, N_HEADS * D_H), jnp.float32) * s(D_LATENT), 'W_KR': jax.random.normal(ks[7], (D_MODEL, D_HR), jnp.float32) * s(D_MODEL), 'W_O': jax.random.normal(ks[8], (N_HEADS * D_H, D_MODEL), jnp.float32) * s(N_HEADS * D_H)}
    _L0_attn_in = _L0_attn_setup()

    def _L0_ffn_setup():
        import jax, jax.numpy as jnp
        import numpy as np
        D_MODEL = 128
        D_FF = 512
        NUM_EXPERTS = 8
        key = jax.random.key(seed)
        ks = jax.random.split(key, 8)
        scale_in = 1.0 / np.sqrt(D_MODEL)
        scale_ff = 1.0 / np.sqrt(D_FF)
        x = jax.random.normal(ks[0], (4, 256, D_MODEL), dtype=jnp.float32)
        gate_w = jax.random.uniform(ks[1], (NUM_EXPERTS, D_MODEL), jnp.float32, -scale_in, scale_in)
        gate_b = jax.random.uniform(ks[2], (NUM_EXPERTS,), jnp.float32, -scale_in, scale_in)
        expert_bias = jnp.zeros((NUM_EXPERTS,), dtype=jnp.float32)
        w1 = jax.random.uniform(ks[3], (NUM_EXPERTS, D_MODEL, D_FF), jnp.float32, -scale_in, scale_in)
        b1 = jax.random.uniform(ks[4], (NUM_EXPERTS, D_FF), jnp.float32, -scale_in, scale_in)
        w2 = jax.random.uniform(ks[5], (NUM_EXPERTS, D_FF, D_MODEL), jnp.float32, -scale_ff, scale_ff)
        b2 = jax.random.uniform(ks[6], (NUM_EXPERTS, D_MODEL), jnp.float32, -scale_ff, scale_ff)
        return {'x': x, 'gate_w': gate_w, 'gate_b': gate_b, 'expert_bias': expert_bias, 'w1': w1, 'b1': b1, 'w2': w2, 'b2': b2}
    _L0_ffn_in = _L0_ffn_setup()
    _d = {'L0_attn_x': _L0_attn_in['x'], 'L0_attn_W_DQ': _L0_attn_in['W_DQ'], 'L0_attn_W_UQ': _L0_attn_in['W_UQ'], 'L0_attn_W_QR': _L0_attn_in['W_QR'], 'L0_attn_W_DKV': _L0_attn_in['W_DKV'], 'L0_attn_W_UK': _L0_attn_in['W_UK'], 'L0_attn_W_UV': _L0_attn_in['W_UV'], 'L0_attn_W_KR': _L0_attn_in['W_KR'], 'L0_attn_W_O': _L0_attn_in['W_O'], 'L0_ffn_gate_w': _L0_ffn_in['gate_w'], 'L0_ffn_gate_b': _L0_ffn_in['gate_b'], 'L0_ffn_expert_bias': _L0_ffn_in['expert_bias'], 'L0_ffn_w1': _L0_ffn_in['w1'], 'L0_ffn_b1': _L0_ffn_in['b1'], 'L0_ffn_w2': _L0_ffn_in['w2'], 'L0_ffn_b2': _L0_ffn_in['b2']}
    _x0 = _d['L0_attn_x']
    _d['L0_attn_x'] = jax.random.normal(jax.random.fold_in(jax.random.key(seed), 1), (4, 1024, 128), dtype=_x0.dtype)
    del _x0
    return _d

def reference(L0_attn_x, L0_attn_W_DQ, L0_attn_W_UQ, L0_attn_W_QR, L0_attn_W_DKV, L0_attn_W_UK, L0_attn_W_UV, L0_attn_W_KR, L0_attn_W_O, L0_ffn_gate_w, L0_ffn_gate_b, L0_ffn_expert_bias, L0_ffn_w1, L0_ffn_b1, L0_ffn_w2, L0_ffn_b2):

    def _L0_attn_ref(x, W_DQ, W_UQ, W_QR, W_DKV, W_UK, W_UV, W_KR, W_O):
        import jax, jax.numpy as jnp
        import numpy as np
        D_MODEL, N_HEADS = (128, 16)
        D_H = D_MODEL // N_HEADS
        D_HR = D_H // 2
        D_LATENT = 32
        THETA = 10000.0

        def rope(x, theta=THETA):
            S, d = (x.shape[-2], x.shape[-1])
            inv = theta ** (-jnp.arange(0, d, 2, dtype=jnp.float32) / d)
            ang = jnp.arange(S, dtype=jnp.float32)[:, None] * inv
            cos, sin = (jnp.cos(ang), jnp.sin(ang))
            x1, x2 = (x[..., 0::2], x[..., 1::2])
            r1 = x1 * cos - x2 * sin
            r2 = x1 * sin + x2 * cos
            return jnp.stack([r1, r2], axis=-1).reshape(x.shape)
        B, S, _ = x.shape
        d_qk = D_H + D_HR
        c_q = x @ W_DQ
        Qc = (c_q @ W_UQ).reshape(B, S, N_HEADS, D_H).transpose(0, 2, 1, 3)
        Qr = (c_q @ W_QR).reshape(B, S, N_HEADS, D_HR).transpose(0, 2, 1, 3)
        Qr = rope(Qr)
        c_kv = x @ W_DKV
        Kc = (c_kv @ W_UK).reshape(B, S, N_HEADS, D_H).transpose(0, 2, 1, 3)
        Kr = rope((x @ W_KR)[:, None, :, :])
        Kr = jnp.broadcast_to(Kr, (B, N_HEADS, S, D_HR))
        V = (c_kv @ W_UV).reshape(B, S, N_HEADS, D_H).transpose(0, 2, 1, 3)
        Q = jnp.concatenate([Qc, Qr], axis=-1)
        K = jnp.concatenate([Kc, Kr], axis=-1)
        scores = jnp.einsum('bhqd,bhkd->bhqk', Q, K)
        scores = jnp.clip(scores, -80.0, 80.0)
        causal = jnp.tril(jnp.ones((S, S), dtype=bool))
        scores = jnp.where(causal, scores, -jnp.inf)
        weights = jax.nn.softmax(scores / jnp.sqrt(jnp.float32(d_qk)), axis=-1)
        attn = jnp.einsum('bhqk,bhkd->bhqd', weights, V)
        attn = attn.transpose(0, 2, 1, 3).reshape(B, S, N_HEADS * D_H)
        return attn @ W_O

    def _L0_ffn_ref(x, gate_w, gate_b, expert_bias, w1, b1, w2, b2):
        import jax, jax.numpy as jnp
        import numpy as np
        D_MODEL = 128
        D_FF = 512
        NUM_EXPERTS = 8
        gate_logits = jnp.einsum('bsd,ed->bse', x, gate_w) + gate_b + expert_bias
        top_idx = jnp.argmax(gate_logits, axis=-1)
        out = jnp.zeros_like(x)
        for e in range(NUM_EXPERTS):
            mask = (top_idx == e)[..., None].astype(x.dtype)
            h = jax.nn.relu(jnp.einsum('bsd,df->bsf', x, w1[e]) + b1[e])
            y = jnp.einsum('bsf,fd->bsd', h, w2[e]) + b2[e]
            out = out + mask * y
        return out
    x = L0_attn_x
    x = _layernorm(x + _L0_attn_ref(x, L0_attn_W_DQ, L0_attn_W_UQ, L0_attn_W_QR, L0_attn_W_DKV, L0_attn_W_UK, L0_attn_W_UV, L0_attn_W_KR, L0_attn_W_O), axis=-1)
    x = _layernorm(x + _L0_ffn_ref(x, L0_ffn_gate_w, L0_ffn_gate_b, L0_ffn_expert_bias, L0_ffn_w1, L0_ffn_b1, L0_ffn_w2, L0_ffn_b2), axis=-1)
    return x

_drawn_inputs = setup_inputs


def setup_inputs(seed=0):
    import zlib

    import numpy as np

    out = dict(_drawn_inputs(seed))
    spreads = {'L0_ffn_expert_bias': (0.0, 0.1)}
    factors = {'L0_ffn_b1': 2.796}
    for name, (base, spread) in spreads.items():
        noise = np.random.default_rng([zlib.crc32(name.encode()), seed]).standard_normal(out[name].shape)
        drawn = base * np.exp(spread * noise) if base else spread * noise
        out[name] = jnp.asarray(drawn.astype(out[name].dtype))
    for name, factor in factors.items():
        out[name] = (out[name] * factor).astype(out[name].dtype)
    return out
```

```python
from contextlib import ExitStack

import numpy as np

import concourse.bass as bass
from concourse import mybir

F32, BF16 = mybir.dt.float32, mybir.dt.bfloat16
I32, U32 = mybir.dt.int32, mybir.dt.uint32
ALU = mybir.AluOpType
ACT = mybir.ActivationFunctionType
AX = mybir.AxisListType

P = 128
B, S, D = 4, 1024, 128
HEADS, DH, DR, LATENT = 16, 8, 4, 32
THETA = 10000.0
CLIP = 80.0
EPS = 1e-5
E, DFF = 8, 512
N = B * S

HG = 4
NHG = HEADS // HG
QC = 512
NKT = S // P
SPLITS = 3
TERMS = SPLITS * SPLITS
ROWS = TERMS * (DH + DR)
VW = 32
CONTQ, ROPEQ, ROPEK, CONTK, ROT = 0, 32, 48, 64, 96
NROPE = HG * DR + DR
ROPE_END = ROPEQ + NROPE
FROWS = ROT
SCALE = 1.0 / float(np.sqrt(np.float32(DH + DR)))
P_LO, P_HI = float(np.exp(-CLIP * SCALE)), float(np.exp(CLIP * SCALE))


def unit_table():
    out = []
    for qc in range(S // QC):
        for kt in range((qc + 1) * QC // P):
            w = QC - max(0, kt * P - qc * QC)
            if w > QC // 2:
                out += [(qc, kt, (0, 1), w), (qc, kt, (2, 3), w)]
            else:
                out.append((qc, kt, (0, 1, 2, 3), w))
    return out


UNITS = unit_table()
NU = len(UNITS)
GROUPS = sorted({(qc, kt) for qc, kt, _, _ in UNITS})
NG = len(GROUPS)
GROUP_OF = [GROUPS.index((qc, kt)) for qc, kt, _, _ in UNITS]
LAST_UNIT = [max(n for n in range(NU) if GROUP_OF[n] == g) for g in range(NG)]
QC_GROUPS = [max(g for g in range(NG) if GROUPS[g][0] == qc) + 1 for qc in range(S // QC)]
UB, GB = NU * NHG, NG * NHG


def bank_table():
    out = []
    for n, (_, _, heads, w) in enumerate(UNITS):
        m = QC // w
        out += [(n, i, min(m, len(heads))) for i in range(0, len(heads), min(m, len(heads)))]
    return out


BANKS = bank_table()
NBK = len(BANKS)
BB = NBK * NHG
BANKS_OF = [[m for m in range(NBK) if BANKS[m][0] == n] for n in range(NU)]

SPILLS, STACKS = 3 * SPLITS, 3 * SPLITS - 1
SCORE_SLOTS = 4
P_SLOTS = 8
LAG = 4

Q = 2
QT = NKT // Q
ROW = D + 4
REGION = N + P
DUMMY = E * REGION
TILES = max(N // P + E - 1, 0)
RING = 6
HEAD = 3
ROUNDS = (TILES - 2 * HEAD) // RING
MLP_STEPS = range(TILES + HEAD)

CONST, CONST_W = {}, 0
for _name, _w in (("upper", P), ("descend", E), ("region", E), ("full_tiles", E * N // P), ("up_to", E * E),
                  ("tile", TILES), ("tile_row", TILES), ("partition", E), ("half", QT)):
    CONST[_name] = slice(CONST_W, CONST_W + _w)
    CONST_W += _w

STEPS = {
    "project0": (None, 2), "project1": (None, 6), "part0": (None, 9), "part1": (None, 11),
    "evac1": (None, 5), "turn1": (None, 7), "evac0": (None, 11), "turn0": (None, 17),
    "v0": (2, 10), "v1": (3, 10),
    "flip0": (0, 12), "flip1": (0, 14), "out0": (0, 18), "out1": (1, 3),
    "norm0": (1, 1), "norm1": (1, 8),
    "turnx0": (1, 11), "turnx1": (2, 1), "gate0": (1, 14), "gate1": (2, 14), "rank0": (1, 18), "rank1": (2, 18),
}
BANK_OF = {"project": 0, "v": 0, "turn": 1, "flip0": 1, "flip1": 0, "out0": 0, "out1": 1, "turnx0": 1, "turnx1": 1,
           "gate0": 0, "gate1": 0, "rank0": 0, "rank1": 0}


def bank_jobs(bank):
    jobs = []
    for hg in range(NHG):
        for u in range(NU):
            for name, (at, unit) in STEPS.items():
                kind, half = name[:-1], int(name[-1])
                if unit == u and at in (None, hg):
                    if kind in ("project", "v", "turn") and BANK_OF[kind] == bank:
                        jobs.append((kind, hg - 1 if name == "turn1" else hg, half))
                    elif BANK_OF.get(name) == bank:
                        jobs.append((kind, hg, half))
    return jobs


BANK_JOBS = [bank_jobs(bank) for bank in range(2)]
ROUTING = ("flip", "out", "turnx", "gate", "rank")
TAIL_JOBS = [[("turn", -1, 1) if j[0] == "turn" else j for j in BANK_JOBS[bank]
              if j[0] in ROUTING or j == ("turn", -1, 1)] for bank in range(2)]


def due(name, hg, u):
    at, unit = STEPS[name]
    return unit == u and at in (None, hg)


def counted(n):
    return not (isinstance(n, int) and n <= 0)


def tile_entry(table, r, c):
    return table[0:1, c:c + 1] if isinstance(r, int) else table[0:1, bass.ds(r * RING + c, 1)]


def mlp_loop(eng, step):
    for c in range(HEAD):
        step(0, c, lambda tile: 0 <= tile < TILES)
    with eng.Fori(0, ROUNDS) as r:
        for c in range(HEAD, HEAD + RING):
            step(r, c, lambda tile: True)
    for c in range(HEAD + ROUNDS * RING, TILES + HEAD):
        step(0, c, lambda tile: 0 <= tile < TILES)


def build(nc, io):
    ctx = ExitStack()
    with ctx:
        def sb(name, shape, dt=F32):
            return ctx.enter_context(nc.sbuf_tensor(name, shape, dt))

        def ps(name, shape, dt=F32):
            return ctx.enter_context(nc.psum_tensor(name, shape, dt))

        def sem(name):
            return ctx.enter_context(nc.semaphore(name))

        scores = [ps(f"scores{i}", [P, QC]) for i in range(SCORE_SLOTS)]
        o_acc = [ps(f"o_acc{i}", [P, QC]) for i in range(2)]
        misc = [ps(f"misc{i}", [P, QC]) for i in range(2)]

        ident = sb("ident", [P, P])
        mask_hi = sb("mask_hi", [P, P])
        rope_cs = sb("rope_table", [P, S])
        const = sb("const", [P, CONST_W])
        upper = sb("upper", [P, P], BF16)
        ones = sb("ones", [P, P], BF16)
        dqT = sb("dqT", [LATENT, D])
        dkvT = sb("dkvT", [LATENT, D])
        up = sb("up", [LATENT, 4, P])
        kr = sb("kr", [D, DR])
        w_hg = sb("w_hg", [D, NHG, P])
        w_v = sb("w_v", [D, P])
        w_o = sb("w_o", [HEADS * DH, D])
        xT = sb("xT", [D, S])
        full = sb("full", [FROWS, S])
        rope_b = sb("rope_b", [ROPE_END, S])
        parts = sb("parts", [FROWS, SPLITS, S], BF16)
        rest = sb("rest", [FROWS, S])
        q_stack = [sb(f"q_stack{i}", [ROWS, HG, S], BF16) for i in range(2)]
        k_stack = [sb(f"k_stack{i}", [ROWS, HG, S], BF16) for i in range(2)]
        v_tok = sb("v_tok", [P, NKT, HEADS, DH])
        v_stat = [sb(f"v_stat{i}", [P, NKT, HG, VW]) for i in range(2)]
        prob = [sb(f"prob{i}", [P, 2 * QC]) for i in range(P_SLOTS)]
        o_sb = [sb(f"o_sb{i}", [P, QC]) for i in range(2)]
        rsum = sb("rsum", [P, QC // P * HG])
        attn = sb("attn", [P, NKT, D])
        xrow = [sb(f"xrow{i}", [P, QT, ROW]) for i in range(Q)]
        flipped = [sb(f"flipped{i}", [P, QT * P]) for i in range(Q)]
        stats = [sb(f"stats{i}", [P, QT, 6]) for i in range(Q)]
        mean_var = [sb(f"mean_var{i}", [P, QT, 2]) for i in range(Q)]
        var_eps = [sb(f"var_eps{i}", [P, QT]) for i in range(Q)]
        rstd = [sb(f"rstd{i}", [P, QT]) for i in range(Q)]
        gate_wT = sb("gate_wT", [D, E])
        gate_bias = sb("gate_bias", [P, 2, E])
        logits = sb("logits", [P, QT, E])
        top = sb("top", [P, QT])
        reach = sb("reach", [P, QT, E])
        order = sb("order", [P, QT, E])
        first = sb("first", [P, QT])
        onehot = [sb(f"onehot{i}", [P, QT + 1, E], BF16) for i in range(Q)]
        place = sb("place", [P, QT, E])
        chosen = sb("chosen", [P, QT, E])
        place_of = sb("place_of", [P, QT])
        index = [sb(f"index{i}", [P, QT], U32) for i in range(Q)]
        next_row = sb("next_row", [P, E])
        pad_row = sb("pad_row", [P, ROW])
        pad_at = sb("pad_at", [P, E])
        pad_index = sb("pad_index", [P, E], U32)
        tokens_of = sb("tokens_of", [P, E])
        begun = sb("begun", [P, E, N // P])
        tiles_of = sb("tiles_of", [P, E])
        below = sb("below", [P, E, E])
        end_of = sb("end_of", [P, E])
        skip_rows = sb("skip_rows", [P, E])
        passed = sb("passed", [P, TILES, E])
        jump = sb("jump", [P, TILES, E])
        tile_e = sb("tile_e", [P, TILES])
        tile_at = sb("tile_at", [P, TILES])
        tile_sum = sb("tile_sum", [P, TILES])
        expert_tab = sb("expert_tab", [P, TILES], I32)
        row_tab = sb("row_tab", [P, TILES], I32)
        w1 = sb("w1", [D, E * DFF])
        w2 = sb("w2", [P, E * DFF // P, D])
        b1 = sb("b1", [P, E * DFF])
        b2 = sb("b2", [P, E * D])
        xs = [sb(f"xs{i}", [P, ROW]) for i in range(RING)]
        xsT = [sb(f"xsT{i}", [P, P]) for i in range(2)]
        hidden = [sb(f"hidden{i}", [P, DFF]) for i in range(2)]
        hiddenT = [sb(f"hiddenT{i}", [P, DFF]) for i in range(2)]
        x_b2 = [sb(f"x_b2{i}", [P, D]) for i in range(HEAD)]
        ys = [sb(f"ys{i}", [P, D]) for i in range(2)]
        zs = [sb(f"zs{i}", [P, D]) for i in range(RING)]
        y_stats = [sb(f"y_stats{i}", [P, 6]) for i in range(2)]
        y_mean = [sb(f"y_mean{i}", [P, 2]) for i in range(2)]
        y_var = [sb(f"y_var{i}", [P, 1]) for i in range(2)]
        y_rstd = [sb(f"y_rstd{i}", [P, 1]) for i in range(2)]

        q_spill = [nc.dram_tensor(f"q_spill{i}", (SPLITS, DH + DR, HG, S), BF16, kind="Internal").ap() for i in range(2)]
        k_spill = [nc.dram_tensor(f"k_spill{i}", (SPLITS, DH + DR, HG, S), BF16, kind="Internal").ap() for i in range(2)]
        by_expert = nc.dram_tensor("by_expert", (DUMMY + P, ROW), F32, kind="Internal").ap()

        weights_in, up_in, const_in, tables_in = sem("weights_in"), sem("up_in"), sem("const_in"), sem("tables_in")
        out_w_in, gate_in, mlp_in, pad_in = sem("out_w_in"), sem("gate_in"), sem("mlp_in"), sem("pad_in")
        ident_ready, mask_ready, w_zero = sem("ident_ready"), sem("mask_ready"), sem("w_zero")
        ones_ready, onehot_zero, upper_ready = sem("ones_ready"), sem("onehot_zero"), sem("upper_ready")
        bias_ready, carried = sem("bias_ready"), sem("carried")
        fused_mm, fused = sem("fused_mm"), sem("fused")
        xT_in = sem("xT_in")
        projected, content_out, partner_out = sem("projected"), sem("content_out"), sem("partner_out")
        rope_mul, rope_out = sem("rope_mul"), sem("rope_out")
        part_ready = [sem(f"part{i}_ready") for i in range(SPLITS)]
        rest_ready = sem("rest_ready")
        spilled = sem("spilled")
        stack_in = [sem(f"stack_in{i}") for i in range(2)]
        v_mm, v_out, v_pad, v_ready = sem("v_mm"), sem("v_out"), sem("v_pad"), sem("v_ready")
        scored, exped, clipped, weighted = sem("scored"), sem("exped"), sem("clipped"), sem("weighted")
        o_out, turned, rsum_ready, attn_ready = sem("o_out"), sem("turned"), sem("rsum_ready"), sem("attn_ready")
        flip_mm, flip_out, out_mm, x_rows_in = sem("flip_mm"), sem("flip_out"), sem("out_mm"), sem("x_rows_in")
        added, stats_ready, mean_ready, var_ready = sem("added"), sem("stats_ready"), sem("mean_ready"), sem("var_ready")
        rstd_ready, normed, turnx_mm, turnx_out = sem("rstd_ready"), sem("normed"), sem("turnx_mm"), sem("turnx_out")
        gate_mm, logits_out, top_ready, reach_ready = sem("gate_mm"), sem("logits_out"), sem("top_ready"), sem("reach_ready")
        biased = sem("biased")
        order_ready, first_ready, onehot_ready = sem("order_ready"), sem("first_ready"), sem("onehot_ready")
        rank_mm, placed, chosen_ready, place_ready = sem("rank_mm"), sem("placed"), sem("chosen_ready"), sem("place_ready")
        index_ready, routed = sem("index_ready"), sem("routed")
        pad_placed, pad_ready, padded, dummy_out = sem("pad_placed"), sem("pad_ready"), sem("padded"), sem("dummy_out")
        plan, planned = sem("plan"), sem("planned")
        xs_in = [sem(f"xs_in{i}") for i in range(RING)]
        xs_turned, xsT_ready, up_mm = sem("xs_turned"), sem("xsT_ready"), sem("up_mm")
        hidden_ready, h_turned, hiddenT_ready = sem("hidden_ready"), sem("h_turned"), sem("hiddenT_ready")
        down_mm, y_out, y_stat, y_meaned = sem("down_mm"), sem("y_out"), sem("y_stat"), sem("y_meaned")
        y_vared, y_rstd_ready, z_ready, x_b2_ready = sem("y_vared"), sem("y_rstd_ready"), sem("z_ready"), sem("x_b2_ready")
        written = [sem(f"written{i}") for i in range(RING)]

        pool_seen, dve_seen, sp_seen = sem("pool_seen"), sem("dve_seen"), sem("sp_seen")

        block = ctx.enter_context(nc.Block())

        def score_ap(m):
            unit, _, heads = BANKS[m % NBK]
            w = UNITS[unit][3]
            return scores[m % SCORE_SLOTS][:, 0:heads * w].rearrange("p (h w) -> p h w", w=w)

        def prob_ap(n):
            _, _, heads, w = UNITS[n % NU]
            return prob[n % P_SLOTS][:, 0:len(heads) * w].rearrange("p (h w) -> p h w", w=w)

        def banks_up_to(b, n):
            return b * BB + (n // NU * NBK + BANKS_OF[n % NU][-1] + 1)

        def groups_up_to(b, n):
            return b * GB + (n // NU * NG + GROUP_OF[n % NU] + 1)

        def halves(b, hg, half):
            return b * (2 * NHG) + (2 * hg + half + 1)

        def routed_groups(b, q):
            return b * Q + (q - Q + 1)

        def reader_done(b, job):
            kind, hg, half = job
            return {
                "project": (partner_out, halves(b, hg + 2, half)),
                "v": (v_out, b * 2 + (2 + half + 1)),
                "turn": (attn_ready, halves(b, hg, half)),
                "flip": (flip_out, routed_groups(b, half)),
                "out": (added, routed_groups(b, half)),
                "turnx": (turnx_out, routed_groups(b, half)),
                "gate": (logits_out, routed_groups(b, half)),
                "rank": (carried, routed_groups(b, half) + 1),
            }[kind]

        def before(b, job):
            bank = BANK_OF[job[0]] if job[0] in BANK_OF else BANK_OF[f"{job[0]}{job[2]}"]
            tail = isinstance(b, int) and b == B
            jobs = TAIL_JOBS[bank] if tail else BANK_JOBS[bank]
            if isinstance(b, int) and b == 0:
                jobs = [j for j in jobs if j[0] not in ROUTING and j != ("turn", -1, 1)]
            i = jobs.index(job)
            return reader_done(b, jobs[i - 1]) if i else reader_done(b - 1, BANK_JOBS[bank][-1])

        def misc_of(kind, half):
            return misc[BANK_OF[kind] if kind in BANK_OF else BANK_OF[f"{kind}{half}"]]

        @block.sync
        def _(sp):
            sp.dma_start(dqT[:], io["W_DQ_T"]).then_inc(weights_in, 16)
            sp.dma_start(dkvT[:], io["W_DKV_T"]).then_inc(weights_in, 16)
            sp.dma_start(up[:, 0, :], io["W_UQ"]).then_inc(up_in, 16)
            sp.dma_start(up[:, 1, 0:HEADS * DR], io["W_QR"]).then_inc(up_in, 16)
            sp.dma_start(up[:, 2, :], io["W_UK"]).then_inc(up_in, 16)
            sp.dma_start(up[:, 3, :], io["W_UV"]).then_inc(up_in, 16)
            sp.dma_start(kr[:], io["W_KR"]).then_inc(weights_in, 16)
            sp.dma_start(xT[:], io["x_T"][0]).then_inc(xT_in, 16)
            sp.dma_start(rope_cs[:], io["rope_cs"]).then_inc(const_in, 16)
            sp.dma_start(const[:], io["const"]).then_inc(tables_in, 16)

            def spill(par, part, stacked):
                if stacked is not None:
                    sp.wait_ge(stack_in[par], stacked)
                    sp.sem_inc(sp_seen, 1)
                for s in range(SPLITS):
                    sp.wait_ge(part_ready[s], part)
                    sp.dma_start(q_spill[par][s].rearrange("r h s -> (r h) s"),
                                 parts[CONTQ:ROPEK, s, :]).then_inc(spilled, 16)
                    sp.dma_start(k_spill[par][s, 0:DH].rearrange("r h s -> (r h) s"),
                                 parts[CONTK:CONTK + HG * DH, s, :]).then_inc(spilled, 16)
                    sp.dma_start(k_spill[par][s, DH:DH + DR],
                                 parts[ROPEK:ROPEK + DR, s, :].unsqueeze(1).to_broadcast([DR, HG, S])
                                 ).then_inc(spilled, 16)

            def stack(par):
                qs = q_spill[par].rearrange("s r h t -> (s r) (h t)")
                ks = k_spill[par].rearrange("s r h t -> (s r) (h t)")
                block_rows, head_rows = SPLITS * (DH + DR), DH + DR
                qd = q_stack[par][:].rearrange("r h t -> r (h t)")
                kd = k_stack[par][:].rearrange("r h t -> r (h t)")
                for g in range(SPLITS):
                    r0 = g * block_rows
                    mid = r0 + (SPLITS - g) * head_rows
                    sp.dma_start(qd[r0:r0 + block_rows], qs).then_inc(stack_in[par], 16)
                    sp.dma_start(kd[r0:mid], ks[g * head_rows:]).then_inc(stack_in[par], 16)
                    if g:
                        sp.dma_start(kd[mid:r0 + block_rows], ks[0:g * head_rows]).then_inc(stack_in[par], 16)

            def load_rows(group, sent):
                if counted(sent):
                    sp.wait_ge(routed, sent)
                for q in range(Q):
                    sp.dma_start(xrow[q][:], io["x_rows"][group[q]].rearrange("(t p) w -> p t w", p=P)
                                 ).then_inc(x_rows_in, 16)

            def value(n):
                return n if isinstance(n, int) else sp.snap(n)

            def batch(b):
                for hg in range(NHG):
                    n_spilled = value(b * (NHG * SPILLS * 16) + (hg + 2) * (SPILLS * 16))
                    n_scored = value(b * BB + (hg * NBK + 1))
                    n_part = value(b * NHG + (hg + 3))
                    n_stacked = value(b * (2 * STACKS * 16) + (hg // 2 + 1) * (STACKS * 16))
                    n_sent = value(b * (Q * QT * 16))
                    n_projected = value(halves(b, NHG - 1, 1))
                    group = [value(b * Q + q) for q in range(Q)]
                    next_batch = value(b + 1)
                    sp.wait_ge(spilled, n_spilled)
                    sp.sem_inc(sp_seen, 1)
                    sp.wait_ge(scored, n_scored)
                    stack((hg + 1) % 2)
                    if hg == 1:
                        sp.wait_ge(projected, n_projected)
                        sp.dma_start(xT[:], io["x_T"][next_batch]).then_inc(xT_in, 16)
                    spill(hg % 2, n_part, n_stacked)
                    if hg == NHG - 1:
                        load_rows(group, n_sent)
                    if isinstance(b, int):
                        load_later(hg)

            def load_later(hg):
                if hg == 0:
                    sp.dma_start(w_o[:], io["W_O"]).then_inc(out_w_in, 16)
                    sp.dma_start(gate_wT[:], io["gate_w_T"]).then_inc(gate_in, 16)
                    sp.dma_start(gate_bias[:, 0, :], io["gate_b"].to_broadcast([P, E])).then_inc(gate_in, 16)
                    sp.dma_start(gate_bias[:, 1, :], io["expert_bias"].to_broadcast([P, E])).then_inc(gate_in, 16)
                    sp.dma_start(pad_row[:], io["pad_rows"]).then_inc(pad_in, 16)
                    sp.wait_ge(pad_in, 16)
                    sp.dma_start(by_expert[DUMMY:DUMMY + P, :], pad_row[:]).then_inc(dummy_out, 16)
                    sp.dma_start(b2[:], io["b2"].to_broadcast([P, E * D])).then_inc(mlp_in, 16)
                if hg == 1:
                    sp.dma_start(w1[:].rearrange("d (e f) -> d e f", e=E),
                                 io["w1"].rearrange("e d f -> d e f")).then_inc(mlp_in, 16)
                if hg == 2:
                    sp.dma_start(w2[:].rearrange("p (e c) d -> p e c d", e=E),
                                 io["w2"].rearrange("e (c p) d -> p e c d", p=P)).then_inc(mlp_in, 16)
                if hg == 3:
                    sp.dma_start(b1[:], io["b1"].to_broadcast([P, E * DFF])).then_inc(mlp_in, 16)

            spill(0, 1, None)
            spill(1, 2, None)
            sp.wait_ge(spilled, SPILLS * 16)
            stack(0)
            batch(0)
            with sp.Fori(1, B) as b:
                batch(b)
            sp.wait_ge(spilled, (B * NHG + 2) * SPILLS * 16)
            sp.wait_ge(stack_in[0], (B * NHG // 2 + 1) * STACKS * 16)
            sp.wait_ge(stack_in[1], B * NHG // 2 * STACKS * 16)
            sp.wait_ge(xT_in, (B + 1) * 16)
            sp.wait_ge(dummy_out, 16)

            sp.wait_ge(routed, N // P * 16)
            sp.wait_ge(padded, E * 16)
            sp.wait_ge(planned, 2)

            def load_tile(r, c):
                used = value(r * 16 + c // RING * 16)
                row = sp.value_load(tile_entry(row_tab, r, c), min_val=0, max_val=DUMMY)
                if counted(used):
                    sp.wait_ge(written[c % RING], used)
                sp.dma_start(xs[c % RING][:], by_expert[bass.ds(row, P), :]).then_inc(xs_in[c % RING], 16)

            for c in range(RING):
                load_tile(0, c)
            with sp.Fori(0, ROUNDS) as r:
                for c in range(RING, 2 * RING):
                    load_tile(r, c)
            for c in range((ROUNDS + 1) * RING, TILES):
                load_tile(0, c)

        @block.gpsimd
        def _(pool):
            pool.memset(ident[:], 0.0).then_inc(ident_ready, 1)
            pool.memset(mask_hi[:], P_HI).then_inc(mask_ready, 1)
            pool.wait_ge(ident_ready, 1)
            pool.affine_select(out=ident[:], in_=ident[:], compare_op=ALU.not_equal, fill=1.0, base=0,
                               pattern=[[-1, P]], channel_multiplier=1).then_inc(ident_ready, 1)
            pool.wait_ge(mask_ready, 1)
            pool.affine_select(out=mask_hi[:], in_=mask_hi[:], compare_op=ALU.is_ge, fill=0.0, base=0,
                               pattern=[[1, P]], channel_multiplier=-1).then_inc(mask_ready, 1)
            for i in range(2):
                pool.memset(v_stat[i][:], 0.0).then_inc(v_pad, 1)
            pool.wait_ge(v_pad, 2)
            for i in range(2):
                pool.memset(v_stat[i][:, :, :, DH:DH + 1], 1.0).then_inc(v_pad, 1)

            def v_slice(hg, par):
                pool.sem_inc(pool_seen, 1)
                pool.tensor_copy(v_stat[par][:, :, :, 0:DH],
                                 v_tok[:, :, hg * HG:(hg + 1) * HG, :]).then_inc(v_ready, 1)

            def rope(b, hg, c):
                n = halves(b, hg, c)
                t = slice(c * QC, (c + 1) * QC)
                pool.wait_ge(content_out, n)
                pool.tensor_tensor(full[0:ROPE_END, t], full[0:ROPE_END, t], rope_cs[0:ROPE_END, t],
                                   ALU.mult).then_inc(rope_mul, 1)
                pool.wait_ge(partner_out, n)
                pool.wait_ge(rope_mul, n)
                pool.tensor_tensor(full[0:ROPE_END, t], full[0:ROPE_END, t], rope_b[0:ROPE_END, t],
                                   ALU.add).then_inc(rope_out, 1)

            def rest0(k):
                pool.wait_ge(part_ready[0], k + 1)
                pool.tensor_tensor(rest[:], full[:], parts[:, 0, :], ALU.subtract).then_inc(rest_ready, 1)

            def part2(k):
                pool.wait_ge(rest_ready, k + 1)
                pool.wait_ge(part_ready[1], k + 1)
                pool.tensor_tensor(parts[:, 2, :], rest[:], parts[:, 1, :], ALU.subtract).then_inc(part_ready[2], 1)

            def inverse_std(b, q):
                pool.wait_ge(var_ready, routed_groups(b, q))
                pool.tensor_tensor(rstd[q][:], var_eps[q][:], const[:, CONST["half"]], ALU.pow).then_inc(rstd_ready, 1)

            def route(b, q):
                pool.wait_ge(index_ready, routed_groups(b, q))
                pool.sem_inc(pool_seen, 1)
                for t in range(QT):
                    pool.indirect_dma_start(by_expert, bass.IndirectOffsetOnAxis(ap=index[q][:, t:t + 1], axis=0),
                                            xrow[q][:, t, :], None).then_inc(routed, 16)

            def batch(b):
                for hg in range(NHG):
                    k = b * NHG + (hg + 2)
                    if hg == 1 and not isinstance(b, int):
                        inverse_std(b, 0)
                    rope(b, hg + 2, 0)
                    if hg < NHG - 1:
                        if counted(b * GB + hg * NG):
                            pool.wait_ge(weighted, b * GB + hg * NG)
                        v_slice(hg + 1, (hg + 1) % 2)
                    if hg == 1 and not isinstance(b, int):
                        inverse_std(b, 1)
                    rope(b, hg + 2, 1)
                    rest0(k)
                    if hg >= 2 and not isinstance(b, int):
                        route(b, hg - 2)
                    part2(k)
                    if hg == NHG - 1:
                        pool.wait_ge(v_out, b * 2 + 4)
                        pool.wait_ge(weighted, b * GB + hg * NG)
                        v_slice(0, 0)

            pool.wait_ge(const_in, 16)
            pool.wait_ge(v_pad, 4)
            for k in range(2):
                rope(0, k, 0)
                rope(0, k, 1)
                rest0(k)
                part2(k)
            pool.wait_ge(v_out, 2)
            v_slice(0, 0)
            pool.wait_ge(tables_in, 16)
            batch(0)
            with pool.Fori(1, B) as b:
                batch(b)
            for q in range(Q):
                inverse_std(B, q)
            for q in range(Q):
                route(B, q)
            pool.wait_ge(pad_ready, 1)
            pool.wait_ge(pad_in, 16)
            for e in range(E):
                pool.indirect_dma_start(by_expert, bass.IndirectOffsetOnAxis(ap=pad_index[:, e:e + 1], axis=0),
                                        pad_row[:], None).then_inc(padded, 16)
            pool.wait_ge(planned, 2)
            pool.wait_ge(mlp_in, 4 * 16)

            def residual(r, c):
                e = pool.value_load(tile_entry(expert_tab, r, c), min_val=0, max_val=E - 1)
                if counted(r * RING + (c - 2)):
                    pool.wait_ge(y_out, r * RING + (c - 2))
                pool.wait_ge(xs_in[c % RING], r * 16 + (c // RING + 1) * 16)
                pool.tensor_tensor(x_b2[c % HEAD][:], xs[c % RING][:, 0:D], b2[:, bass.ds(e * D, D)],
                                   ALU.add).then_inc(x_b2_ready, 1)

            def y_inverse_std(r, c):
                pool.wait_ge(y_vared, r * RING + (c + 1))
                pool.tensor_tensor(y_rstd[c % 2][:], y_var[c % 2][:], const[:, CONST["half"]][:, 0:1],
                                   ALU.pow).then_inc(y_rstd_ready, 1)

            def write(r, c):
                pool.wait_ge(z_ready, r * RING + (c + 1))
                pool.sem_inc(pool_seen, 1)
                pool.indirect_dma_start(
                    io["out"], bass.IndirectOffsetOnAxis(ap=xs[c % RING][:, D:D + 1].bitcast(U32), axis=0),
                    zs[c % RING][:], None, bounds_check=N - 1, oob_is_err=False).then_inc(written[c % RING], 16)

            def step(r, c, live):
                if live(c):
                    residual(r, c)
                if live(c - 3):
                    write(r, c - 3)
                if live(c - 2):
                    y_inverse_std(r, c - 2)

            mlp_loop(pool, step)
            for i in range(RING):
                pool.wait_ge(written[i], len(range(i, TILES, RING)) * 16)

        @block.vector
        def _(dve):
            dve.memset(w_hg[:], 0.0).then_inc(w_zero, 1)
            dve.memset(ones[:], 1.0)
            dve.memset(rope_b[0:ROPEQ], 0.0)
            for q in range(Q):
                dve.memset(onehot[q][:], 0.0)
            dve.wait_ge(w_zero, 1)
            dve.wait_ge(fused_mm, 1)
            dve.wait_ge(weights_in, 48)

            def by_element(ap, per_head):
                return ap.rearrange("p (g h d) -> p g d h", g=NHG, d=per_head)

            def rows(start, n):
                return w_hg[:, :, start:start + n * HG].rearrange("p g (d h) -> p g d h", h=HG)

            qr = by_element(misc[0][:, 128:128 + HEADS * DR], DR)
            dve.tensor_copy(rows(CONTQ, DH), by_element(misc[0][:, 0:128], DH))
            dve.tensor_copy(rows(ROPEQ, DR), qr)
            dve.tensor_copy(rows(CONTK, DH), by_element(misc[0][:, 192:320], DH))
            for e in range(2):
                dve.tensor_copy(rows(ROT, DR)[:, :, e::2, :], qr[:, :, 1 - e::2, :])
            for hg in range(NHG):
                dve.tensor_copy(w_hg[:, hg, ROPEK:ROPEK + DR], kr[:])
                for e in range(2):
                    dve.tensor_copy(w_hg[:, hg, ROT + HG * DR + e:ROT + NROPE:2], kr[:, 1 - e::2])
            dve.tensor_copy(w_v[:], misc[0][:, 320:448]).then_inc(fused, 1)
            dve.wait_ge(const_in, 16)

            def take(b, hg, c):
                n = halves(b, hg, c)
                t = slice(c * QC, (c + 1) * QC)
                dve.wait_ge(projected, n)
                if counted(b * NHG + hg):
                    dve.wait_ge(rest_ready, b * NHG + hg)
                    dve.wait_ge(part_ready[1], b * NHG + hg)
                dve.tensor_copy(full[:, t], misc[0][0:FROWS]).then_inc(content_out, 1)
                dve.tensor_tensor(rope_b[ROPEQ:ROPE_END, t], misc[0][ROT:ROT + NROPE], rope_cs[ROT:ROT + NROPE, t],
                                  ALU.mult).then_inc(partner_out, 1)

            def part1(k):
                dve.wait_ge(part_ready[0], k + 1)
                dve.tensor_tensor(parts[:, 1, :], full[:], parts[:, 0, :], ALU.subtract).then_inc(part_ready[1], 1)

            def normalize(b, hg, qc):
                n = halves(b, hg, qc)
                dve.wait_ge(turned, n)
                o = misc_of("turn", qc)[:].rearrange("p (t c) -> p t c", c=VW)
                dve.reciprocal(rsum[:], o[:, :, DH]).then_inc(rsum_ready, 1)
                if hg == 0 and counted(routed_groups(b, qc)):
                    dve.wait_ge(flip_mm, routed_groups(b, qc))
                dve.wait_ge(rsum_ready, n)
                tiles = QC // P
                cols = hg % NHG * HG * DH
                out = attn[:, qc * tiles:(qc + 1) * tiles, cols:cols + HG * DH]
                dve.tensor_tensor(out.rearrange("p t (h d) -> p t h d", d=DH),
                                  o[:, :, 0:DH].rearrange("p (t h) d -> p t h d", h=HG),
                                  rsum[:].rearrange("p (t h) -> p t h", h=HG).unsqueeze(3)
                                  .to_broadcast([P, tiles, HG, DH]),
                                  ALU.mult).then_inc(attn_ready, 1)

            def clip(b, n):
                w = UNITS[n % NU][3]
                diag = UNITS[n % NU][1] * P >= UNITS[n % NU][0] * QC
                p = prob_ap(n)
                dve.wait_ge(exped, banks_up_to(b, n))
                if not diag or w > P:
                    rest_ = p[:, :, P if diag else 0:w]
                    last = dve.tensor_scalar(rest_, rest_, P_HI, P_LO, ALU.min, ALU.max)
                if diag:
                    d_ = p[:, :, 0:P]
                    last = dve.scalar_tensor_tensor(
                        out=d_, in0=d_, scalar=P_LO,
                        in1=mask_hi[:].unsqueeze(1).to_broadcast([P, len(UNITS[n % NU][2]), P]),
                        op0=ALU.max, op1=ALU.min)
                last.then_inc(clipped, 1)

            def moments(b, q):
                g = routed_groups(b, q)
                x = xrow[q][:, :, 0:D]
                dve.wait_ge(out_mm, g)
                dve.wait_ge(x_rows_in, b * (Q * 16))
                dve.tensor_tensor(x, misc_of("out", q)[:].rearrange("p (t d) -> p t d", d=D), x,
                                  ALU.add).then_inc(added, 1)
                dve.wait_ge(added, g)
                for t in range(QT):
                    last = dve.bn_stats(stats[q][:, t, :], x[:, t, :])
                last.then_inc(stats_ready, 1)
                dve.wait_ge(stats_ready, g)
                dve.sem_inc(dve_seen, 1)
                for t in range(QT):
                    last = dve.bn_aggr(mean_var[q][:, t, :], stats[q][:, t, :])
                last.then_inc(mean_ready, 1)
                dve.wait_ge(mean_ready, g)
                dve.tensor_scalar(var_eps[q][:], mean_var[q][:, :, 1], EPS, None, ALU.add).then_inc(var_ready, 1)

            def layernorm(b, q):
                g = routed_groups(b, q)
                dve.wait_ge(rstd_ready, g)
                for t in range(QT):
                    x = xrow[q][:, t, 0:D]
                    last = dve.tensor_scalar(x, x, mean_var[q][:, t, 0:1], rstd[q][:, t:t + 1],
                                             ALU.subtract, ALU.mult)
                last.then_inc(normed, 1)

            def choose(b, q):
                g = routed_groups(b, q)

                def wide(ap):
                    return ap.unsqueeze(2).to_broadcast([P, QT, E])

                dve.wait_ge(gate_mm, g)
                dve.tensor_tensor(logits[:], misc_of("gate", q)[:, 0:QT * E].rearrange("p (t e) -> p t e", e=E),
                                  gate_bias[:, 0, :].unsqueeze(1).to_broadcast([P, QT, E]),
                                  ALU.add).then_inc(logits_out, 1)
                dve.wait_ge(logits_out, g)
                dve.tensor_reduce(top[:], logits[:], AX.X, ALU.max).then_inc(top_ready, 1)
                dve.wait_ge(top_ready, g)
                dve.tensor_tensor(reach[:], logits[:], wide(top[:]), ALU.is_ge).then_inc(reach_ready, 1)
                dve.wait_ge(reach_ready, g)
                dve.tensor_tensor(order[:], reach[:],
                                  const[:, CONST["descend"]].unsqueeze(1).to_broadcast([P, QT, E]),
                                  ALU.mult).then_inc(order_ready, 1)
                dve.wait_ge(order_ready, g)
                dve.tensor_reduce(first[:], order[:], AX.X, ALU.max).then_inc(first_ready, 1)
                dve.wait_ge(first_ready, g)
                dve.tensor_tensor(onehot[q][:, 0:QT, :], order[:], wide(first[:]),
                                  ALU.is_equal).then_inc(onehot_ready, 1)

            def assign(b, q):
                g = routed_groups(b, q)
                rank = misc_of("rank", q)[:, 0:(QT + 1) * E].rearrange("p (t e) -> p t e", e=E)
                dve.wait_ge(rank_mm, g)
                dve.wait_ge(carried, g)
                dve.tensor_tensor(place[:], rank[:, 0:QT, :], next_row[:].unsqueeze(1).to_broadcast([P, QT, E]),
                                  ALU.add).then_inc(placed, 1)
                dve.wait_ge(placed, g)
                dve.tensor_tensor(next_row[:], next_row[:], rank[:, QT, :], ALU.add).then_inc(carried, 1)
                dve.tensor_tensor(chosen[:], place[:], onehot[q][:, 0:QT, :], ALU.mult).then_inc(chosen_ready, 1)
                dve.wait_ge(chosen_ready, g)
                dve.tensor_reduce(place_of[:], chosen[:], AX.X, ALU.add).then_inc(place_ready, 1)
                dve.wait_ge(place_ready, g)
                dve.tensor_copy(index[q][:], place_of[:]).then_inc(index_ready, 1)

            def batch(b):
                later = not isinstance(b, int)
                for hg in range(NHG):
                    k = b * NHG + (hg + 2)
                    for u in range(NU):
                        clip(b, hg * NU + u)
                        for c in range(2):
                            if due(f"project{c}", hg, u):
                                take(b, hg + 2, c)
                        if due("part1", hg, u):
                            part1(k)
                        if due("turn1", hg, u) and (hg or later):
                            normalize(b, hg - 1, 1)
                        if due("turn0", hg, u):
                            normalize(b, hg, 0)
                        for q in range(Q):
                            if later and due(f"out{q}", hg, u):
                                moments(b, q)
                            if later and due(f"norm{q}", hg, u):
                                layernorm(b, q)
                            if later and due(f"gate{q}", hg, u):
                                choose(b, q)
                            if later and due(f"rank{q}", hg, u):
                                assign(b, q)

            for k in range(2):
                take(0, k, 0)
                take(0, k, 1)
                part1(k)
            dve.wait_ge(tables_in, 16)
            dve.tensor_copy(upper[:], const[:, CONST["upper"]]).then_inc(upper_ready, 1)
            dve.tensor_copy(next_row[:], const[:, CONST["region"]]).then_inc(carried, 1)
            dve.wait_ge(mask_ready, 2)
            batch(0)
            dve.wait_ge(gate_in, 48)
            dve.tensor_tensor(gate_bias[:, 0, :], gate_bias[:, 0, :], gate_bias[:, 1, :], ALU.add).then_inc(bias_ready, 1)
            dve.wait_ge(bias_ready, 1)
            with dve.Fori(1, B) as b:
                batch(b)
            normalize(B, -1, 1)
            for q in range(Q):
                moments(B, q)
            for q in range(Q):
                layernorm(B, q)
            for q in range(Q):
                choose(B, q)
                assign(B, q)

            dve.wait_ge(carried, N // (P * QT) + 1)
            dve.tensor_tensor(pad_at[:], next_row[:], const[:, CONST["partition"]], ALU.add).then_inc(pad_placed, 1)
            dve.tensor_tensor(tokens_of[:], next_row[:], const[:, CONST["region"]], ALU.subtract).then_inc(plan, 1)
            dve.wait_ge(pad_placed, 1)
            dve.tensor_copy(pad_index[:], pad_at[:]).then_inc(pad_ready, 1)
            dve.wait_ge(plan, 1)
            dve.tensor_tensor(begun[:], tokens_of[:].unsqueeze(2).to_broadcast([P, E, N // P]),
                              const[:, CONST["full_tiles"]].rearrange("p (e k) -> p e k", e=E),
                              ALU.is_gt).then_inc(plan, 1)
            dve.wait_ge(plan, 2)
            dve.tensor_reduce(tiles_of[:], begun[:], AX.X, ALU.add).then_inc(plan, 1)
            dve.wait_ge(plan, 3)
            dve.tensor_tensor(below[:], const[:, CONST["up_to"]].rearrange("p (e f) -> p e f", e=E),
                              tiles_of[:].unsqueeze(1).to_broadcast([P, E, E]), ALU.mult).then_inc(plan, 1)
            dve.tensor_scalar(skip_rows[:], tiles_of[:], -float(P), float(REGION), ALU.mult, ALU.add).then_inc(plan, 1)
            dve.wait_ge(plan, 5)
            dve.tensor_reduce(end_of[:], below[:], AX.X, ALU.add).then_inc(plan, 1)
            dve.wait_ge(plan, 6)
            dve.tensor_tensor(passed[:], const[:, CONST["tile"]].unsqueeze(2).to_broadcast([P, TILES, E]),
                              end_of[:].unsqueeze(1).to_broadcast([P, TILES, E]), ALU.is_ge).then_inc(plan, 1)
            dve.wait_ge(plan, 7)
            dve.tensor_reduce(tile_e[:], passed[:], AX.X, ALU.add).then_inc(plan, 1)
            dve.tensor_tensor(jump[:], passed[:], skip_rows[:].unsqueeze(1).to_broadcast([P, TILES, E]),
                              ALU.mult).then_inc(plan, 1)
            dve.wait_ge(plan, 9)
            dve.tensor_scalar(expert_tab[:], tile_e[:], float(E - 1), None, ALU.min).then_inc(planned, 1)
            dve.tensor_reduce(tile_sum[:], jump[:], AX.X, ALU.add).then_inc(plan, 1)
            dve.wait_ge(plan, 10)
            dve.tensor_tensor(tile_at[:], tile_sum[:], const[:, CONST["tile_row"]], ALU.add).then_inc(plan, 1)
            dve.wait_ge(plan, 11)
            dve.tensor_scalar(row_tab[:], tile_at[:], float(DUMMY), None, ALU.min).then_inc(planned, 1)
            dve.wait_ge(planned, 2)
            dve.wait_ge(mlp_in, 4 * 16)

            def bias1(r, c):
                e = dve.value_load(tile_entry(expert_tab, r, c), min_val=0, max_val=E - 1)
                dve.wait_ge(up_mm, r * RING + (c + 1))
                if counted(r * RING + (c - 1)):
                    dve.wait_ge(h_turned, r * RING + (c - 1))
                dve.tensor_tensor(hidden[c % 2][:], scores[2 + c % 2][:], b1[:, bass.ds(e * DFF, DFF)],
                                  ALU.add).then_inc(hidden_ready, 1)

            def y_moments(r, c):
                n = r * RING + (c + 1)
                dve.wait_ge(down_mm, n)
                dve.wait_ge(x_b2_ready, n)
                dve.tensor_tensor(ys[c % 2][:], misc[c % 2][:, 0:D], x_b2[c % HEAD][:], ALU.add).then_inc(y_out, 1)
                dve.wait_ge(y_out, n)
                dve.bn_stats(y_stats[c % 2][:], ys[c % 2][:]).then_inc(y_stat, 1)
                dve.wait_ge(y_stat, n)
                dve.sem_inc(dve_seen, 1)
                dve.bn_aggr(y_mean[c % 2][:], y_stats[c % 2][:]).then_inc(y_meaned, 1)
                dve.wait_ge(y_meaned, n)
                dve.tensor_scalar(y_var[c % 2][:], y_mean[c % 2][:, 1:2], EPS, None, ALU.add).then_inc(y_vared, 1)

            def y_norm(r, c):
                dve.wait_ge(y_rstd_ready, r * RING + (c + 1))
                dve.tensor_scalar(zs[c % RING][:], ys[c % 2][:], y_mean[c % 2][:, 0:1], y_rstd[c % 2][:],
                                  ALU.subtract, ALU.mult).then_inc(z_ready, 1)

            def step(r, c, live):
                if live(c):
                    bias1(r, c)
                if live(c - 3):
                    y_norm(r, c - 3)
                if live(c - 2):
                    y_moments(r, c - 2)

            mlp_loop(dve, step)

        @block.scalar
        def _(act):
            def part0(k, busy):
                act.wait_ge(rope_out, k * 2 + 2)
                if busy:
                    act.wait_ge(spilled, k * (SPILLS * 16))
                act.activation(parts[:, 0, :], full[:], ACT.Copy).then_inc(part_ready[0], 1)

            def v_evac(b, c):
                act.wait_ge(v_mm, b * 2 + (2 + c + 1))
                half = v_tok[:, c * (NKT // 2):(c + 1) * (NKT // 2)]
                act.activation(half.rearrange("p t h d -> p (t h d)"), misc_of("v", c)[:], ACT.Copy).then_inc(v_out, 1)

            def exp(b, n, m):
                act.wait_ge(scored, b * BB + (m + 1))
                if counted(groups_up_to(b, n - P_SLOTS)):
                    act.wait_ge(weighted, groups_up_to(b, n - P_SLOTS))
                _, start, heads = BANKS[m % NBK]
                act.activation(prob_ap(n)[:, start:start + heads], score_ap(m), ACT.Exp,
                               scale=SCALE).then_inc(exped, 1)

            def o_evac(b, hg, qc):
                act.wait_ge(weighted, b * GB + (hg * NG + QC_GROUPS[qc]))
                if counted(halves(b, hg - 1, qc)):
                    act.wait_ge(turned, halves(b, hg - 1, qc))
                act.activation(o_sb[qc][:], o_acc[qc][:], ACT.Copy).then_inc(o_out, 1)

            def flip_evac(kind, b, q):
                ready, done = {"flip": (flip_mm, flip_out), "turnx": (turnx_mm, turnx_out)}[kind]
                act.wait_ge(ready, routed_groups(b, q))
                act.activation(flipped[q][:], misc_of(kind, q)[:], ACT.Copy).then_inc(done, 1)

            def batch(b):
                later = not isinstance(b, int)
                for hg in range(NHG):
                    for u in range(NU):
                        for m in BANKS_OF[u]:
                            exp(b, hg * NU + u, hg * NBK + m)
                        if due("evac1", hg, u) and (hg or later):
                            o_evac(b, hg - 1, 1)
                        if due("part0", hg, u):
                            part0(b * NHG + (hg + 2), True)
                        if due("evac0", hg, u):
                            o_evac(b, hg, 0)
                        for c in range(2):
                            if due(f"v{c}", hg, u):
                                act.wait_ge(v_ready, b * NHG + NHG)
                                v_evac(b, c)
                        for q in range(Q):
                            for kind in ("flip", "turnx"):
                                if later and due(f"{kind}{q}", hg, u):
                                    flip_evac(kind, b, q)

            part0(0, False)
            part0(1, True)
            v_evac(-1, 0)
            v_evac(-1, 1)
            batch(0)
            with act.Fori(1, B) as b:
                batch(b)
            o_evac(B, -1, 1)
            for kind in ("flip", "turnx"):
                for q in range(Q):
                    flip_evac(kind, B, q)

            def xT_evac(r, c):
                act.wait_ge(xs_turned, r * RING + (c + 1))
                if counted(r * RING + (c - 1)):
                    act.wait_ge(up_mm, r * RING + (c - 1))
                act.activation(xsT[c % 2][:], scores[c % 2][:, 0:P], ACT.Copy).then_inc(xsT_ready, 1)

            def relu(r, c):
                act.wait_ge(h_turned, r * RING + (c + 1))
                if counted(r * RING + (c - 1)):
                    act.wait_ge(down_mm, r * RING + (c - 1))
                act.activation(hiddenT[c % 2][:], o_acc[c % 2][:], ACT.Relu).then_inc(hiddenT_ready, 1)

            def step(r, c, live):
                if live(c + 1):
                    xT_evac(r, c + 1)
                if live(c - 1):
                    relu(r, c - 1)

            xT_evac(0, 0)
            mlp_loop(act, step)

        @block.tensor
        def _(pe):
            pe.wait_ge(weights_in, 48)
            pe.wait_ge(up_in, 64)
            pe.matmul(misc[0][:, 0:128], dqT[:], up[:, 0, :], start=True, stop=True)
            pe.matmul(misc[0][:, 128:192], dqT[:], up[:, 1, 0:64], start=True, stop=True)
            pe.matmul(misc[0][:, 192:320], dkvT[:], up[:, 2, :], start=True, stop=True)
            pe.matmul(misc[0][:, 320:448], dkvT[:], up[:, 3, :], start=True, stop=True).then_inc(fused_mm, 1)

            def project(c, hg):
                pe.matmul(misc_of("project", c)[:], w_hg[:, hg, :], xT[:, c * QC:(c + 1) * QC],
                          start=True, stop=True).then_inc(projected, 1)

            def v_rows(c):
                for t in range(QC // P):
                    last = pe.matmul(misc_of("v", c)[:, t * P:(t + 1) * P],
                                     xT[:, c * QC + t * P:c * QC + (t + 1) * P], w_v[:], start=True, stop=True)
                last.then_inc(v_mm, 1)

            def score(b, m):
                unit, start, count = BANKS[m % NBK]
                _, kt, heads, w = UNITS[unit]
                qc = UNITS[unit][0]
                par = m // NBK % 2
                old = m - SCORE_SLOTS if m >= SCORE_SLOTS else \
                    max(i for i in range(BB) if i % SCORE_SLOTS == m % SCORE_SLOTS) - BB
                if counted(b * BB + (old + 1)):
                    pe.wait_ge(exped, b * BB + (old + 1))
                out = score_ap(m)
                for i in range(count):
                    j = heads[start + i]
                    last = pe.matmul(out[:, i, :], k_stack[par][:, j, kt * P:(kt + 1) * P],
                                     q_stack[par][:, j, (qc + 1) * QC - w:(qc + 1) * QC], start=True, stop=True)
                last.then_inc(scored, 1)

            def weigh(b, n):
                if n % NU not in LAST_UNIT:
                    return
                g, hg = LAST_UNIT.index(n % NU), n // NU
                qc, kt = GROUPS[g]
                par = hg % 2
                pe.wait_ge(clipped, b * UB + (n + 1))
                if kt == 0:
                    if qc == 0:
                        pe.wait_ge(v_ready, b * NHG + (hg + 1))
                    if counted(halves(b, hg - 1, qc)):
                        pe.wait_ge(o_out, halves(b, hg - 1, qc))
                for u in range(NU):
                    if GROUP_OF[u] == g:
                        _, _, heads, w = UNITS[u]
                        p = prob_ap(hg * NU + u)
                        for i, j in enumerate(heads):
                            last = pe.matmul(o_acc[qc][j * VW:(j + 1) * VW, QC - w:QC], v_stat[par][:, kt, j, :],
                                             p[:, i, :], start=kt == 0, stop=g + 1 == QC_GROUPS[qc])
                last.then_inc(weighted, 1)

            def turn(b, hg, qc):
                pe.wait_ge(o_out, halves(b, hg, qc))
                free = before(b, ("turn", hg, qc))
                if counted(free[1]):
                    pe.wait_ge(*free)
                for t in range(QC // P):
                    last = pe.transpose(misc_of("turn", qc)[:, t * P:(t + 1) * P], o_sb[qc][:, t * P:(t + 1) * P],
                                        ident[:])
                last.then_inc(turned, 1)

            def routing(b, hg, kind, q):
                g = routed_groups(b, q)
                bank = misc_of(kind, q)
                pe.wait_ge(*before(b, (kind, hg, q)))
                if kind == "flip":
                    pe.wait_ge(attn_ready, halves(b, -1, 1))
                    for t in range(QT):
                        last = pe.transpose(bank[:, t * P:(t + 1) * P], attn[:, q * QT + t, :], ident[:])
                    last.then_inc(flip_mm, 1)
                elif kind == "out":
                    pe.wait_ge(flip_out, g)
                    pe.wait_ge(out_w_in, 16)
                    for t in range(QT):
                        last = pe.matmul(bank[:, t * D:(t + 1) * D], flipped[q][:, t * P:(t + 1) * P], w_o[:],
                                         start=True, stop=True)
                    last.then_inc(out_mm, 1)
                elif kind == "turnx":
                    pe.wait_ge(normed, g)
                    for t in range(QT):
                        last = pe.transpose(bank[:, t * P:(t + 1) * P], xrow[q][:, t, 0:D], ident[:])
                    last.then_inc(turnx_mm, 1)
                elif kind == "gate":
                    pe.wait_ge(turnx_out, g)
                    pe.wait_ge(gate_in, 48)
                    for t in range(QT):
                        last = pe.matmul(bank[:, t * E:(t + 1) * E], flipped[q][:, t * P:(t + 1) * P], gate_wT[:],
                                         start=True, stop=True)
                    last.then_inc(gate_mm, 1)
                else:
                    pe.wait_ge(onehot_ready, g)
                    pe.wait_ge(upper_ready, 1)
                    hot = onehot[q][:].rearrange("p t e -> p (t e)")
                    pe.matmul(bank[:, 0:(QT + 1) * E], upper[:], hot, start=True, stop=False, skip_group_check=True)
                    for s in range(1, QT + 1):
                        last = pe.matmul(bank[:, s * E:(QT + 1) * E], ones[:], hot[:, 0:(QT + 1 - s) * E],
                                         start=False, stop=s == QT, skip_group_check=True)
                    last.then_inc(rank_mm, 1)

            def batch(b):
                later = not isinstance(b, int)
                for hg in range(NHG):
                    n_stack = STACKS * 16
                    pe.wait_ge(stack_in[hg % 2], b * (2 * n_stack) + (hg // 2 + 1) * n_stack)
                    for u in range(NU):
                        n = hg * NU + u
                        for m in BANKS_OF[u]:
                            score(b, hg * NBK + m)
                        if n >= LAG or later:
                            weigh(b, n - LAG)
                        for c in range(2):
                            if due(f"project{c}", hg, u):
                                if hg == 2 and c == 0:
                                    pe.wait_ge(xT_in, b * 16 + 32)
                                pe.wait_ge(*before(b, ("project", hg, c)))
                                project(c, (hg + 2) % NHG)
                            if due(f"v{c}", hg, u):
                                pe.wait_ge(*before(b, ("v", hg, c)))
                                v_rows(c)
                        if due("turn1", hg, u) and (hg or later):
                            turn(b, hg - 1, 1)
                        if due("turn0", hg, u):
                            turn(b, hg, 0)
                        for q in range(Q):
                            for kind in ROUTING:
                                if later and due(f"{kind}{q}", hg, u):
                                    routing(b, hg, kind, q)

            pe.wait_ge(fused, 1)
            pe.wait_ge(xT_in, 16)
            for k in range(2):
                for c in range(2):
                    if k or c:
                        pe.wait_ge(partner_out, 2 * k + c)
                    project(c, k)
            pe.wait_ge(partner_out, 4)
            v_rows(0)
            pe.wait_ge(v_out, 1)
            v_rows(1)
            pe.wait_ge(ident_ready, 2)
            batch(0)
            with pe.Fori(1, B) as b:
                batch(b)
            for n in range(-LAG, 0):
                weigh(B, n)
            turn(B, -1, 1)
            for kind in ROUTING[0:3]:
                for q in range(Q):
                    routing(B, STEPS[f"{kind}{q}"][0], kind, q)
            for q in range(Q):
                for kind in ROUTING[3:]:
                    routing(B, STEPS[f"{kind}{q}"][0], kind, q)

            pe.wait_ge(exped, B * BB)
            pe.wait_ge(carried, N // (P * QT) + 1)
            pe.wait_ge(planned, 2)
            pe.wait_ge(mlp_in, 4 * 16)

            def turn_x(r, c):
                pe.wait_ge(xs_in[c % RING], r * 16 + (c // RING + 1) * 16)
                if counted(r * RING + (c - 1)):
                    pe.wait_ge(xsT_ready, r * RING + (c - 1))
                pe.transpose(scores[c % 2][:, 0:P], xs[c % RING][:, 0:D], ident[:]).then_inc(xs_turned, 1)

            def up_rows(r, c):
                e = pe.value_load(tile_entry(expert_tab, r, c), min_val=0, max_val=E - 1)
                pe.wait_ge(xsT_ready, r * RING + (c + 1))
                if counted(r * RING + (c - 1)):
                    pe.wait_ge(hidden_ready, r * RING + (c - 1))
                pe.matmul(scores[2 + c % 2][:], xsT[c % 2][:], w1[:, bass.ds(e * DFF, DFF)],
                          start=True, stop=True).then_inc(up_mm, 1)

            def turn_hidden(r, c):
                pe.wait_ge(hidden_ready, r * RING + (c + 1))
                if counted(r * RING + (c - 1)):
                    pe.wait_ge(hiddenT_ready, r * RING + (c - 1))
                for f in range(DFF // P):
                    last = pe.transpose(o_acc[c % 2][:, f * P:(f + 1) * P], hidden[c % 2][:, f * P:(f + 1) * P],
                                        ident[:])
                last.then_inc(h_turned, 1)

            def down_rows(r, c):
                e = pe.value_load(tile_entry(expert_tab, r, c), min_val=0, max_val=E - 1)
                pe.wait_ge(hiddenT_ready, r * RING + (c + 1))
                if counted(r * RING + (c - 1)):
                    pe.wait_ge(y_out, r * RING + (c - 1))
                w2_cols = w2[:].rearrange("p c d -> p (c d)")
                for f in range(DFF // P):
                    last = pe.matmul(misc[c % 2][:, 0:D], hiddenT[c % 2][:, f * P:(f + 1) * P],
                                     w2_cols[:, bass.ds(e * DFF + f * D, D)], start=f == 0, stop=f == DFF // P - 1)
                last.then_inc(down_mm, 1)

            def step(r, c, live):
                if live(c):
                    up_rows(r, c)
                if live(c - 1):
                    turn_hidden(r, c - 1)
                if live(c + 1):
                    turn_x(r, c + 1)
                if live(c - 2):
                    down_rows(r, c - 2)

            turn_x(0, 0)
            mlp_loop(pe, step)


def rope_table():
    inv = np.float32(THETA) ** (-np.arange(0, DR, 2, dtype=np.float32) / np.float32(DR))
    ang = np.arange(S, dtype=np.float32)[None, :] * inv.astype(np.float32)[:, None]
    table = np.zeros((P, S), np.float32)
    table[CONTQ:ROPEQ] = 1.0
    for r in range(NROPE):
        d = r // HG if r < HG * DR else r - HG * DR
        table[ROPEQ + r] = np.cos(ang[d // 2])
        table[ROT + r] = np.sin(ang[d // 2]) * (np.float32(1.0) if d % 2 else np.float32(-1.0))
    return table


def constants():
    p = np.arange(P, dtype=np.float32)
    table = np.zeros((P, CONST_W), np.float32)
    table[:, CONST["upper"]] = p[:, None] < p[None, :]
    table[:, CONST["descend"]] = E - np.arange(E)
    table[:, CONST["region"]] = REGION * np.arange(E)
    table[:, CONST["full_tiles"]] = np.tile(P * np.arange(N // P), E)
    table[:, CONST["up_to"]] = (np.arange(E)[:, None] >= np.arange(E)[None, :]).reshape(-1)
    table[:, CONST["tile"]] = np.arange(TILES)
    table[:, CONST["tile_row"]] = P * np.arange(TILES)
    table[:, CONST["partition"]] = p[:, None]
    table[:, CONST["half"]] = -0.5
    return table


def with_ids(rows, ids):
    out = np.zeros((rows.shape[0], ROW), np.int32)
    out[:, 0:D] = np.ascontiguousarray(rows).view(np.int32)
    out[:, D] = ids
    return out.view(np.float32)


def kernel(**inputs):
    import concourse.bacc as bacc
    from concourse.bass_utils import run_bass_kernel_spmd

    a = {k: np.asarray(v) for k, v in inputs.items()}
    x = a["L0_attn_x"]
    x_T = x.transpose(0, 2, 1)
    arrays = {
        "x_T": np.concatenate([x_T, x_T[:1]]),
        "x_rows": with_ids(x.reshape(N, D), np.arange(N)).reshape(2 * B, S // 2, ROW),
        "pad_rows": with_ids(np.zeros((P, D), np.float32), N + np.arange(P)),
        "W_DQ_T": np.ascontiguousarray(a["L0_attn_W_DQ"].T),
        "W_DKV_T": np.ascontiguousarray(a["L0_attn_W_DKV"].T),
        "W_UQ": a["L0_attn_W_UQ"], "W_QR": a["L0_attn_W_QR"], "W_UK": a["L0_attn_W_UK"],
        "W_UV": a["L0_attn_W_UV"], "W_KR": a["L0_attn_W_KR"], "W_O": a["L0_attn_W_O"],
        "gate_w_T": np.ascontiguousarray(a["L0_ffn_gate_w"].T),
        "gate_b": a["L0_ffn_gate_b"].reshape(1, E), "expert_bias": a["L0_ffn_expert_bias"].reshape(1, E),
        "w1": a["L0_ffn_w1"], "b1": a["L0_ffn_b1"].reshape(1, E * DFF),
        "w2": a["L0_ffn_w2"], "b2": a["L0_ffn_b2"].reshape(1, E * D),
        "rope_cs": rope_table(),
        "const": constants(),
    }
    nc = bacc.Bacc("TRN2", target_bir_lowering=False, num_devices=1)
    io = {k: nc.dram_tensor("in_" + k, v.shape, mybir.dt.from_np(v.dtype), kind="ExternalInput").ap()
          for k, v in arrays.items()}
    io["out"] = nc.dram_tensor("out", (N, D), F32, kind="ExternalOutput").ap()
    build(nc, io)
    r = run_bass_kernel_spmd(nc, [{"in_" + k: v for k, v in arrays.items()}], core_ids=[0])
    return r.results[0]["out"].reshape(B, S, D)
```

```python
from contextlib import ExitStack

import numpy as np

import concourse.bass as bass
from concourse import mybir

F32, BF16 = mybir.dt.float32, mybir.dt.bfloat16
I32, U32 = mybir.dt.int32, mybir.dt.uint32
ALU = mybir.AluOpType
ACT = mybir.ActivationFunctionType
AX = mybir.AxisListType

P = 128
B, S, D = 4, 1024, 128
HEADS, DH, DR, LATENT = 16, 8, 4, 32
THETA = 10000.0
CLIP = 80.0
EPS = 1e-5
E, DFF = 8, 512
N = B * S

HG = 4
NHG = HEADS // HG
QC = 512
NKT = S // P
SPLITS = 3
TERMS = SPLITS * SPLITS
ROWS = TERMS * (DH + DR)
VW = 32
CONTQ, ROPEQ, ROPEK, CONTK, ROT = 0, 32, 48, 64, 96
NROPE = HG * DR + DR
ROPE_END = ROPEQ + NROPE
FROWS = ROT
SCALE = 1.0 / float(np.sqrt(np.float32(DH + DR)))
P_LO, P_HI = float(np.exp(-CLIP * SCALE)), float(np.exp(CLIP * SCALE))


def unit_table():
    out = []
    for qc in range(S // QC):
        for kt in range((qc + 1) * QC // P):
            w = QC - max(0, kt * P - qc * QC)
            if w > QC // 2:
                out += [(qc, kt, (0, 1), w), (qc, kt, (2, 3), w)]
            else:
                out.append((qc, kt, (0, 1, 2, 3), w))
    return out


UNITS = unit_table()
NU = len(UNITS)
GROUPS = sorted({(qc, kt) for qc, kt, _, _ in UNITS})
NG = len(GROUPS)
GROUP_OF = [GROUPS.index((qc, kt)) for qc, kt, _, _ in UNITS]
LAST_UNIT = [max(n for n in range(NU) if GROUP_OF[n] == g) for g in range(NG)]
QC_GROUPS = [max(g for g in range(NG) if GROUPS[g][0] == qc) + 1 for qc in range(S // QC)]
UB, GB = NU * NHG, NG * NHG


def bank_table():
    out = []
    for n, (_, _, heads, w) in enumerate(UNITS):
        m = QC // w
        out += [(n, i, min(m, len(heads))) for i in range(0, len(heads), min(m, len(heads)))]
    return out


BANKS = bank_table()
NBK = len(BANKS)
BB = NBK * NHG
BANKS_OF = [[m for m in range(NBK) if BANKS[m][0] == n] for n in range(NU)]

SPILLS, STACKS = 3 * SPLITS, 3 * SPLITS - 1
SCORE_SLOTS = 4
P_SLOTS = 10
LAG = 6

Q = 2
QT = NKT // Q
ROW = D + 4
REGION = N + P
DUMMY = E * REGION
TILES = max(N // P + E - 1, 0)
RING = 6
STAGES = 3
HEAD = RING
ROUNDS = (TILES - HEAD - 1) // RING

CONST, CONST_W = {}, 0
for _name, _w in (("upper", P), ("descend", E), ("region", E), ("full_tiles", E * N // P), ("up_to", E * E),
                  ("tile", TILES), ("tile_row", TILES), ("half", QT)):
    CONST[_name] = slice(CONST_W, CONST_W + _w)
    CONST_W += _w

STEPS = {
    "project0": (None, 2), "project1": (None, 9), "part0": (None, 16),
    "evac1": (None, 6), "turn1": (None, 9), "evac0": (None, 12), "turn0": (None, 16),
    "v0": (2, 6), "v1": (3, 14),
    "flip0": (0, 16), "flip1": (0, 19), "out0": (1, 3), "out1": (1, 16),
    "moments0": (1, 4), "moments1": (1, 17), "norm0": (1, 8), "norm1": (2, 5),
    "turnx0": (2, 3), "turnx1": (2, 13), "gate0": (2, 17), "rank0": (3, 4),
}
BANK_OF = {"project": 0, "v0": 1, "v1": 0, "turn": 1, "flip0": 0, "flip1": 0, "out0": 1, "out1": 0,
           "turnx0": 1, "turnx1": 1, "gate0": 0, "rank0": 1}


def bank_jobs(bank):
    jobs = []
    for hg in range(NHG):
        for u in range(NU):
            for name, (at, unit) in STEPS.items():
                kind, half = name[:-1], int(name[-1])
                if unit == u and at in (None, hg):
                    if BANK_OF.get(kind) == bank:
                        jobs.append((kind, hg - 1 if name == "turn1" else hg, half))
                    elif BANK_OF.get(name) == bank:
                        jobs.append((kind, hg, half))
    return jobs


BANK_JOBS = [bank_jobs(bank) for bank in range(2)]
ROUTING = ("flip", "out", "turnx", "gate", "rank")
TAIL_JOBS = [[("turn", -1, 1) if j[0] == "turn" else j for j in BANK_JOBS[bank]
              if j[0] in ROUTING or j == ("turn", -1, 1)] for bank in range(2)]


def due(name, hg, u):
    at, unit = STEPS[name]
    return unit == u and at in (None, hg)


def counted(n):
    return not (isinstance(n, int) and n <= 0)


def tile_entry(table, r, c):
    return table[0:1, c:c + 1] if isinstance(r, int) else table[0:1, bass.ds(r * RING + c, 1)]


def mlp_loop(eng, steps):
    def exists(c):
        return 0 <= c < TILES

    steps(0, range(HEAD), exists)
    with eng.Fori(0, ROUNDS) as r:
        steps(r, range(HEAD, HEAD + RING), lambda c: True)
    steps(0, range(HEAD + ROUNDS * RING, TILES + STAGES), exists)


def build(nc, io):
    ctx = ExitStack()
    with ctx:
        def sb(name, shape, dt=F32):
            return ctx.enter_context(nc.sbuf_tensor(name, shape, dt))

        def ps(name, shape, dt=F32):
            return ctx.enter_context(nc.psum_tensor(name, shape, dt))

        def sem(name):
            return ctx.enter_context(nc.semaphore(name))

        scores = [ps(f"scores{i}", [P, QC]) for i in range(SCORE_SLOTS)]
        o_acc = [ps(f"o_acc{i}", [P, QC]) for i in range(2)]
        misc = [ps(f"misc{i}", [P, QC]) for i in range(2)]

        ident = sb("ident", [P, P])
        mask_hi = sb("mask_hi", [P, P])
        rope_cs = sb("rope_table", [P, S])
        const = sb("const", [P, CONST_W])
        upper = sb("upper", [P, P], BF16)
        ones = sb("ones", [P, P], BF16)
        dqT = sb("dqT", [LATENT, D])
        dkvT = sb("dkvT", [LATENT, D])
        up = sb("up", [LATENT, 4, P])
        kr = sb("kr", [D, DR])
        w_hg = sb("w_hg", [D, NHG, P])
        w_v = sb("w_v", [D, P])
        w_o = sb("w_o", [HEADS * DH, D])
        xT = sb("xT", [D, S])
        full = sb("full", [FROWS, S])
        rope_b = sb("rope_b", [ROPE_END, S])
        parts = sb("parts", [FROWS, SPLITS, S], BF16)
        rest = sb("rest", [FROWS, S])
        q_stack = [sb(f"q_stack{i}", [ROWS, HG, S], BF16) for i in range(2)]
        k_stack = [sb(f"k_stack{i}", [ROWS, HG, S], BF16) for i in range(2)]
        v_tok = sb("v_tok", [P, NKT, HEADS, DH])
        v_stat = [sb(f"v_stat{i}", [P, NKT, HG, VW]) for i in range(2)]
        prob = [sb(f"prob{i}", [P, 2 * QC]) for i in range(P_SLOTS)]
        o_sb = [sb(f"o_sb{i}", [P, QC]) for i in range(2)]
        rsum = sb("rsum", [P, QC // P * HG])
        attn = sb("attn", [P, NKT, D])
        xrow = [sb(f"xrow{i}", [P, QT, ROW]) for i in range(Q)]
        flipped = [sb(f"flipped{i}", [P, QT * P]) for i in range(Q)]
        stats = [sb(f"stats{i}", [P, QT, 6]) for i in range(Q)]
        mean_var = [sb(f"mean_var{i}", [P, QT, 2]) for i in range(Q)]
        var_eps = [sb(f"var_eps{i}", [P, QT]) for i in range(Q)]
        rstd = [sb(f"rstd{i}", [P, QT]) for i in range(Q)]
        gate_wT = sb("gate_wT", [D, E])
        gate_bias = sb("gate_bias", [P, 2, E])
        logits = sb("logits", [P, NKT, E])
        top = sb("top", [P, NKT])
        reach = sb("reach", [P, NKT, E])
        order = sb("order", [P, NKT, E])
        first = sb("first", [P, NKT])
        onehot = sb("onehot", [P, NKT + 1, E], BF16)
        place = sb("place", [P, NKT, E])
        chosen = sb("chosen", [P, NKT, E])
        place_of = sb("place_of", [P, NKT])
        index = sb("index", [P, NKT], U32)
        next_row = sb("next_row", [P, E])
        pad_row = sb("pad_row", [P, ROW])
        pad_at = sb("pad_at", [P, E], I32)
        tokens_of = sb("tokens_of", [P, E])
        begun = sb("begun", [P, E, N // P])
        tiles_of = sb("tiles_of", [P, E])
        below = sb("below", [P, E, E])
        end_of = sb("end_of", [P, E])
        skip_rows = sb("skip_rows", [P, E])
        passed = sb("passed", [P, TILES, E])
        jump = sb("jump", [P, TILES, E])
        tile_e = sb("tile_e", [P, TILES])
        tile_at = sb("tile_at", [P, TILES])
        tile_sum = sb("tile_sum", [P, TILES])
        expert_tab = sb("expert_tab", [P, TILES], I32)
        row_tab = sb("row_tab", [P, TILES], I32)
        w1 = sb("w1", [D, E * DFF])
        w2 = sb("w2", [P, E * DFF // P, D])
        b1T = sb("b1T", [P, E * DFF // P])
        b2 = sb("b2", [P, E * D])
        xs = [sb(f"xs{i}", [P, ROW]) for i in range(RING)]
        xsT = [sb(f"xsT{i}", [P, P]) for i in range(2)]
        hidden = [prob[0][:, i * DFF:(i + 1) * DFF] for i in range(2)]
        hiddenT = [prob[1][:, i * DFF:(i + 1) * DFF] for i in range(2)]
        x_b2 = [sb(f"x_b2{i}", [P, D]) for i in range(STAGES)]
        ids = [sb(f"ids{i}", [P, 1], U32) for i in range(RING)]
        ys = [sb(f"ys{i}", [P, D]) for i in range(2)]
        zs = [sb(f"zs{i}", [P, D]) for i in range(RING)]
        y_stats = [sb(f"y_stats{i}", [P, 6]) for i in range(2)]
        y_mean = [sb(f"y_mean{i}", [P, 2]) for i in range(2)]
        y_var = [sb(f"y_var{i}", [P, 1]) for i in range(2)]
        y_rstd = [sb(f"y_rstd{i}", [P, 1]) for i in range(2)]

        q_spill = [nc.dram_tensor(f"q_spill{i}", (SPLITS, DH + DR, HG, S), BF16, kind="Internal").ap() for i in range(2)]
        k_spill = [nc.dram_tensor(f"k_spill{i}", (SPLITS, DH + DR, HG, S), BF16, kind="Internal").ap() for i in range(2)]
        by_expert = nc.dram_tensor("by_expert", (DUMMY + P, ROW), F32, kind="Internal").ap()

        weights_in, up_in, const_in, tables_in = sem("weights_in"), sem("up_in"), sem("const_in"), sem("tables_in")
        out_w_in, gate_in, mlp_in, pad_in = sem("out_w_in"), sem("gate_in"), sem("mlp_in"), sem("pad_in")
        ident_ready, mask_ready, w_zero = sem("ident_ready"), sem("mask_ready"), sem("w_zero")
        ones_ready, onehot_zero, upper_ready = sem("ones_ready"), sem("onehot_zero"), sem("upper_ready")
        bias_ready, carried = sem("bias_ready"), sem("carried")
        fused_mm, fused = sem("fused_mm"), sem("fused")
        xT_in = sem("xT_in")
        projected, content_out, partner_out = sem("projected"), sem("content_out"), sem("partner_out")
        rope_mul, rope_out = sem("rope_mul"), sem("rope_out")
        part_ready = [sem(f"part{i}_ready") for i in range(SPLITS)]
        rest_ready = sem("rest_ready")
        spilled = sem("spilled")
        stack_in = [sem(f"stack_in{i}") for i in range(2)]
        v_mm, v_out, v_pad, v_ready = sem("v_mm"), sem("v_out"), sem("v_pad"), sem("v_ready")
        scored, exped, clipped, weighted = sem("scored"), sem("exped"), sem("clipped"), sem("weighted")
        o_out, turned, rsum_ready, attn_ready = sem("o_out"), sem("turned"), sem("rsum_ready"), sem("attn_ready")
        flip_mm, flip_out, out_mm, x_rows_in = sem("flip_mm"), sem("flip_out"), sem("out_mm"), sem("x_rows_in")
        added, stats_ready, mean_ready, var_ready = sem("added"), sem("stats_ready"), sem("mean_ready"), sem("var_ready")
        rstd_ready, normed, turnx_mm, turnx_out = sem("rstd_ready"), sem("normed"), sem("turnx_mm"), sem("turnx_out")
        gate_mm, logits_out, top_ready, reach_ready = sem("gate_mm"), sem("logits_out"), sem("top_ready"), sem("reach_ready")
        biased = sem("biased")
        order_ready, first_ready, onehot_ready = sem("order_ready"), sem("first_ready"), sem("onehot_ready")
        rank_mm, placed, chosen_ready, place_ready = sem("rank_mm"), sem("placed"), sem("chosen_ready"), sem("place_ready")
        index_ready, routed = sem("index_ready"), sem("routed")
        pad_ready, padded, dummy_out = sem("pad_ready"), sem("padded"), sem("dummy_out")
        plan, planned = sem("plan"), sem("planned")
        xs_in = [sem(f"xs_in{i}") for i in range(RING)]
        xs_turned, xsT_ready, up_mm = sem("xs_turned"), sem("xsT_ready"), sem("up_mm")
        hidden_ready, h_turned, hiddenT_ready = sem("hidden_ready"), sem("h_turned"), sem("hiddenT_ready")
        down_mm, y_out, y_stat, y_meaned = sem("down_mm"), sem("y_out"), sem("y_stat"), sem("y_meaned")
        y_vared, y_rstd_ready, z_ready, x_b2_ready, ids_ready = sem("y_vared"), sem("y_rstd_ready"), sem("z_ready"), sem("x_b2_ready"), sem("ids_ready")
        written = [sem(f"written{i}") for i in range(RING)]

        pool_seen, dve_seen, sp_seen = sem("pool_seen"), sem("dve_seen"), sem("sp_seen")

        block = ctx.enter_context(nc.Block())

        def score_ap(m):
            unit, _, heads = BANKS[m % NBK]
            w = UNITS[unit][3]
            return scores[m % SCORE_SLOTS][:, 0:heads * w].rearrange("p (h w) -> p h w", w=w)

        def prob_ap(n):
            _, _, heads, w = UNITS[n % NU]
            return prob[n % P_SLOTS][:, 0:len(heads) * w].rearrange("p (h w) -> p h w", w=w)

        def banks_up_to(b, n):
            return b * BB + (n // NU * NBK + BANKS_OF[n % NU][-1] + 1)

        def groups_up_to(b, n):
            return b * GB + (n // NU * NG + GROUP_OF[n % NU] + 1)

        def halves(b, hg, half):
            return b * (2 * NHG) + (2 * hg + half + 1)

        def routed_groups(b, q):
            return b * Q + (q - Q + 1)

        def reader_done(b, job):
            kind, hg, half = job
            return {
                "project": (partner_out, halves(b, hg + 2, half)),
                "v": (v_out, b * 2 + (2 + half + 1)),
                "turn": (attn_ready, halves(b, hg, half)),
                "flip": (flip_out, routed_groups(b, half)),
                "out": (added, routed_groups(b, half)),
                "turnx": (turnx_out, routed_groups(b, half)),
                "gate": (logits_out, b),
                "rank": (carried, b + 1),
            }[kind]

        def before(b, job):
            bank = BANK_OF[job[0]] if job[0] in BANK_OF else BANK_OF[f"{job[0]}{job[2]}"]
            tail = isinstance(b, int) and b == B
            jobs = TAIL_JOBS[bank] if tail else BANK_JOBS[bank]
            if isinstance(b, int) and b == 0:
                jobs = [j for j in jobs if j[0] not in ROUTING and j != ("turn", -1, 1)]
            i = jobs.index(job)
            return reader_done(b, jobs[i - 1]) if i else reader_done(b - 1, BANK_JOBS[bank][-1])

        def misc_of(kind, half):
            return misc[BANK_OF[kind] if kind in BANK_OF else BANK_OF[f"{kind}{half}"]]

        @block.sync
        def _(sp):
            sp.dma_start(dqT[:], io["W_DQ_T"]).then_inc(weights_in, 16)
            sp.dma_start(dkvT[:], io["W_DKV_T"]).then_inc(weights_in, 16)
            sp.dma_start(up[:, 0, :], io["W_UQ"]).then_inc(up_in, 16)
            sp.dma_start(up[:, 1, 0:HEADS * DR], io["W_QR"]).then_inc(up_in, 16)
            sp.dma_start(up[:, 2, :], io["W_UK"]).then_inc(up_in, 16)
            sp.dma_start(up[:, 3, :], io["W_UV"]).then_inc(up_in, 16)
            sp.dma_start(kr[:], io["W_KR"]).then_inc(weights_in, 16)
            sp.dma_start(xT[:], io["x_T"][0]).then_inc(xT_in, 16)
            sp.dma_start(rope_cs[:], io["rope_cs"]).then_inc(const_in, 16)
            sp.dma_start(const[:], io["const"]).then_inc(tables_in, 16)

            def spill(par, part, stacked):
                if stacked is not None:
                    sp.wait_ge(stack_in[par], stacked)
                    sp.sem_inc(sp_seen, 1)
                for s in range(SPLITS):
                    sp.wait_ge(part_ready[s], part)
                    sp.dma_start(q_spill[par][s].rearrange("r h s -> (r h) s"),
                                 parts[CONTQ:ROPEK, s, :]).then_inc(spilled, 16)
                    sp.dma_start(k_spill[par][s, 0:DH].rearrange("r h s -> (r h) s"),
                                 parts[CONTK:CONTK + HG * DH, s, :]).then_inc(spilled, 16)
                    sp.dma_start(k_spill[par][s, DH:DH + DR],
                                 parts[ROPEK:ROPEK + DR, s, :].unsqueeze(1).to_broadcast([DR, HG, S])
                                 ).then_inc(spilled, 16)

            def stack(par):
                qs = q_spill[par].rearrange("s r h t -> (s r) (h t)")
                ks = k_spill[par].rearrange("s r h t -> (s r) (h t)")
                block_rows, head_rows = SPLITS * (DH + DR), DH + DR
                qd = q_stack[par][:].rearrange("r h t -> r (h t)")
                kd = k_stack[par][:].rearrange("r h t -> r (h t)")
                for g in range(SPLITS):
                    r0 = g * block_rows
                    mid = r0 + (SPLITS - g) * head_rows
                    sp.dma_start(qd[r0:r0 + block_rows], qs).then_inc(stack_in[par], 16)
                    sp.dma_start(kd[r0:mid], ks[g * head_rows:]).then_inc(stack_in[par], 16)
                    if g:
                        sp.dma_start(kd[mid:r0 + block_rows], ks[0:g * head_rows]).then_inc(stack_in[par], 16)

            def load_rows(group, sent):
                if counted(sent):
                    sp.wait_ge(routed, sent)
                for q in range(Q):
                    sp.dma_start(xrow[q][:], io["x_rows"][group[q]].rearrange("(t p) w -> p t w", p=P)
                                 ).then_inc(x_rows_in, 16)

            def value(n):
                return n if isinstance(n, int) else sp.snap(n)

            def batch(b):
                for hg in range(NHG):
                    n_spilled = value(b * (NHG * SPILLS * 16) + (hg + 2) * (SPILLS * 16))
                    n_scored = value(b * BB + (hg * NBK + 1))
                    n_part = value(b * NHG + (hg + 3))
                    n_stacked = value(b * (2 * STACKS * 16) + (hg // 2 + 1) * (STACKS * 16))
                    n_sent = value(b * (Q * QT * 16))
                    n_projected = value(halves(b, NHG - 1, 1))
                    group = [value(b * Q + q) for q in range(Q)]
                    next_batch = value(b + 1)
                    sp.wait_ge(spilled, n_spilled)
                    sp.sem_inc(sp_seen, 1)
                    sp.wait_ge(scored, n_scored)
                    stack((hg + 1) % 2)
                    if hg == 1:
                        sp.wait_ge(projected, n_projected)
                        sp.dma_start(xT[:], io["x_T"][next_batch]).then_inc(xT_in, 16)
                    spill(hg % 2, n_part, n_stacked)
                    if hg == NHG - 1:
                        load_rows(group, n_sent)
                    if isinstance(b, int):
                        load_later(hg)

            def load_later(hg):
                if hg == 0:
                    sp.dma_start(w_o[:], io["W_O"]).then_inc(out_w_in, 16)
                    sp.dma_start(gate_wT[:], io["gate_w_T"]).then_inc(gate_in, 16)
                    sp.dma_start(gate_bias[:, 0, :], io["gate_b"].to_broadcast([P, E])).then_inc(gate_in, 16)
                    sp.dma_start(gate_bias[:, 1, :], io["expert_bias"].to_broadcast([P, E])).then_inc(gate_in, 16)
                    sp.dma_start(pad_row[:], io["pad_rows"]).then_inc(pad_in, 16)
                    sp.wait_ge(pad_in, 16)
                    sp.dma_start(by_expert[DUMMY:DUMMY + P, :], pad_row[:]).then_inc(dummy_out, 16)
                    sp.dma_start(b2[:], io["b2"].to_broadcast([P, E * D])).then_inc(mlp_in, 16)
                if hg == 1:
                    sp.dma_start(w1[:].rearrange("d (e f) -> d e f", e=E),
                                 io["w1"].rearrange("e d f -> d e f")).then_inc(mlp_in, 16)
                if hg == 2:
                    sp.dma_start(w2[:].rearrange("p (e c) d -> p e c d", e=E),
                                 io["w2"].rearrange("e (c p) d -> p e c d", p=P)).then_inc(mlp_in, 16)
                if hg == 3:
                    sp.dma_start(b1T[:], io["b1_T"]).then_inc(mlp_in, 16)

            spill(0, 1, None)
            sp.wait_ge(spilled, SPILLS * 16)
            stack(0)
            spill(1, 2, None)
            batch(0)
            with sp.Fori(1, B) as b:
                batch(b)
            sp.wait_ge(spilled, (B * NHG + 2) * SPILLS * 16)
            sp.wait_ge(stack_in[0], (B * NHG // 2 + 1) * STACKS * 16)
            sp.wait_ge(stack_in[1], B * NHG // 2 * STACKS * 16)
            sp.wait_ge(xT_in, (B + 1) * 16)
            sp.wait_ge(dummy_out, 16)

            sp.wait_ge(pad_ready, 1)
            for e in range(E):
                at = sp.value_load(pad_at[0:1, e:e + 1], min_val=0, max_val=DUMMY)
                sp.dma_start(by_expert[bass.ds(at, P), :], pad_row[:]).then_inc(padded, 16)
            sp.wait_ge(routed, N // P * 16)
            sp.wait_ge(padded, E * 16)
            sp.wait_ge(planned, 2)

            def load_tile(r, c):
                used = value(r * RING + (c - RING + 1))
                row = sp.value_load(tile_entry(row_tab, r, c), min_val=0, max_val=DUMMY)
                if counted(used):
                    sp.wait_ge(xs_turned, used)
                    sp.sem_inc(sp_seen, 1)
                    sp.wait_ge(ids_ready, used)
                sp.dma_start(xs[c % RING][:], by_expert[bass.ds(row, P), :]).then_inc(xs_in[c % RING], 16)

            for c in range(RING):
                load_tile(0, c)
            with sp.Fori(0, ROUNDS) as r:
                for c in range(RING, 2 * RING):
                    load_tile(r, c)
            for c in range((ROUNDS + 1) * RING, TILES):
                load_tile(0, c)

        @block.gpsimd
        def _(pool):
            pool.memset(ident[:], 0.0).then_inc(ident_ready, 1)
            pool.memset(mask_hi[:], P_HI).then_inc(mask_ready, 1)
            pool.wait_ge(ident_ready, 1)
            pool.affine_select(out=ident[:], in_=ident[:], compare_op=ALU.not_equal, fill=1.0, base=0,
                               pattern=[[-1, P]], channel_multiplier=1).then_inc(ident_ready, 1)
            pool.wait_ge(mask_ready, 1)
            pool.affine_select(out=mask_hi[:], in_=mask_hi[:], compare_op=ALU.is_ge, fill=0.0, base=0,
                               pattern=[[1, P]], channel_multiplier=-1).then_inc(mask_ready, 1)
            for i in range(2):
                pool.memset(v_stat[i][:], 0.0).then_inc(v_pad, 1)
            pool.wait_ge(v_pad, 2)
            for i in range(2):
                pool.memset(v_stat[i][:, :, :, DH:DH + 1], 1.0).then_inc(v_pad, 1)

            def v_slice(hg, par):
                pool.sem_inc(pool_seen, 1)
                pool.tensor_copy(v_stat[par][:, :, :, 0:DH],
                                 v_tok[:, :, hg * HG:(hg + 1) * HG, :]).then_inc(v_ready, 1)

            def rope(b, hg, c):
                n = halves(b, hg, c)
                t = slice(c * QC, (c + 1) * QC)
                pool.wait_ge(content_out, n)
                pool.tensor_tensor(full[0:ROPE_END, t], full[0:ROPE_END, t], rope_cs[0:ROPE_END, t],
                                   ALU.mult).then_inc(rope_mul, 1)
                pool.wait_ge(partner_out, n)
                pool.wait_ge(rope_mul, n)
                pool.tensor_tensor(full[0:ROPE_END, t], full[0:ROPE_END, t], rope_b[0:ROPE_END, t],
                                   ALU.add).then_inc(rope_out, 1)

            def rest0(k):
                pool.wait_ge(part_ready[0], k + 1)
                pool.tensor_tensor(rest[:], full[:], parts[:, 0, :], ALU.subtract).then_inc(rest_ready, 1)

            def part1(k):
                pool.tensor_tensor(parts[:, 1, :], full[:], parts[:, 0, :], ALU.subtract).then_inc(part_ready[1], 1)

            def part2(k):
                pool.wait_ge(rest_ready, k + 1)
                pool.wait_ge(part_ready[1], k + 1)
                pool.tensor_tensor(parts[:, 2, :], rest[:], parts[:, 1, :], ALU.subtract).then_inc(part_ready[2], 1)

            def inverse_std(b, q):
                pool.wait_ge(var_ready, routed_groups(b, q))
                pool.tensor_tensor(rstd[q][:], var_eps[q][:], const[:, CONST["half"]], ALU.pow).then_inc(rstd_ready, 1)

            def route(b, q):
                pool.wait_ge(index_ready, b)
                pool.sem_inc(pool_seen, 1)
                for t in range(q * QT, (q + 1) * QT):
                    pool.indirect_dma_start(by_expert, bass.IndirectOffsetOnAxis(ap=index[:, t:t + 1], axis=0),
                                            xrow[t // QT][:, t % QT, :], None).then_inc(routed, 16)

            def batch(b):
                for hg in range(NHG):
                    k = b * NHG + (hg + 2)
                    if hg == 2 and not isinstance(b, int):
                        inverse_std(b, 1)
                    rope(b, hg + 2, 0)
                    if hg < NHG - 1:
                        if counted(b * GB + hg * NG):
                            pool.wait_ge(weighted, b * GB + hg * NG)
                        v_slice(hg + 1, (hg + 1) % 2)
                    if hg == 1 and not isinstance(b, int):
                        inverse_std(b, 0)
                    if hg == NHG - 1 and not isinstance(b, int):
                        route(b, 0)
                    rope(b, hg + 2, 1)
                    if hg == NHG - 1 and not isinstance(b, int):
                        route(b, 1)
                    rest0(k)
                    part1(k)
                    part2(k)
                    if hg == NHG - 1:
                        pool.wait_ge(v_out, b * 2 + 4)
                        pool.wait_ge(weighted, b * GB + hg * NG)
                        v_slice(0, 0)

            pool.wait_ge(const_in, 16)
            pool.wait_ge(v_pad, 4)
            for k in range(2):
                rope(0, k, 0)
                rope(0, k, 1)
                rest0(k)
                part1(k)
                part2(k)
            pool.wait_ge(v_out, 2)
            v_slice(0, 0)
            pool.wait_ge(tables_in, 16)
            batch(0)
            with pool.Fori(1, B) as b:
                batch(b)
            for q in range(Q):
                inverse_std(B, q)
            for q in range(Q):
                route(B, q)
            pool.wait_ge(planned, 2)
            pool.wait_ge(mlp_in, 4 * 16)

            def residual(r, c):
                e = pool.value_load(tile_entry(expert_tab, r, c), min_val=0, max_val=E - 1)
                if counted(r * RING + (c - 2)):
                    pool.wait_ge(y_out, r * RING + (c - 2))
                if counted(r * 16 + (c // RING) * 16):
                    pool.wait_ge(written[c % RING], r * 16 + (c // RING) * 16)
                pool.wait_ge(xs_in[c % RING], r * 16 + (c // RING + 1) * 16)
                pool.tensor_tensor(x_b2[c % STAGES][:], xs[c % RING][:, 0:D], b2[:, bass.ds(e * D, D)],
                                   ALU.add).then_inc(x_b2_ready, 1)
                pool.tensor_copy(ids[c % RING][:], xs[c % RING][:, D:D + 1].bitcast(U32)).then_inc(ids_ready, 1)

            def y_inverse_std(r, c):
                pool.wait_ge(y_vared, r * RING + (c + 1))
                pool.tensor_tensor(y_rstd[c % 2][:], y_var[c % 2][:], const[:, CONST["half"]][:, 0:1],
                                   ALU.pow).then_inc(y_rstd_ready, 1)

            def write(r, c):
                pool.wait_ge(ids_ready, r * RING + (c + 1))
                pool.wait_ge(z_ready, r * RING + (c + 1))
                pool.sem_inc(pool_seen, 1)
                pool.indirect_dma_start(
                    io["out"], bass.IndirectOffsetOnAxis(ap=ids[c % RING][:], axis=0),
                    zs[c % RING][:], None, bounds_check=N - 1, oob_is_err=False).then_inc(written[c % RING], 16)

            def steps(r, cs, live):
                for c in cs:
                    step(r, c, live)

            def step(r, c, live):
                if live(c):
                    residual(r, c)
                if live(c - 3):
                    write(r, c - 3)
                if live(c - 2):
                    y_inverse_std(r, c - 2)

            mlp_loop(pool, steps)
            for i in range(RING):
                pool.wait_ge(written[i], len(range(i, TILES, RING)) * 16)

        @block.vector
        def _(dve):
            dve.memset(w_hg[:], 0.0).then_inc(w_zero, 1)
            dve.memset(ones[:], 1.0)
            dve.memset(rope_b[0:ROPEQ], 0.0)
            dve.memset(onehot[:], 0.0)
            dve.wait_ge(w_zero, 1)
            dve.wait_ge(fused_mm, 1)
            dve.wait_ge(weights_in, 48)

            def by_element(ap, per_head):
                return ap.rearrange("p (g h d) -> p g d h", g=NHG, d=per_head)

            def rows(start, n):
                return w_hg[:, :, start:start + n * HG].rearrange("p g (d h) -> p g d h", h=HG)

            qr = by_element(misc[0][:, 128:128 + HEADS * DR], DR)
            dve.tensor_copy(rows(CONTQ, DH), by_element(misc[0][:, 0:128], DH))
            dve.tensor_copy(rows(ROPEQ, DR), qr)
            dve.tensor_copy(rows(CONTK, DH), by_element(misc[0][:, 192:320], DH))
            for e in range(2):
                dve.tensor_copy(rows(ROT, DR)[:, :, e::2, :], qr[:, :, 1 - e::2, :])
            for hg in range(NHG):
                dve.tensor_copy(w_hg[:, hg, ROPEK:ROPEK + DR], kr[:])
                for e in range(2):
                    dve.tensor_copy(w_hg[:, hg, ROT + HG * DR + e:ROT + NROPE:2], kr[:, 1 - e::2])
            dve.tensor_copy(w_v[:], misc[0][:, 320:448]).then_inc(fused, 1)
            dve.wait_ge(const_in, 16)

            def take(b, hg, c):
                n = halves(b, hg, c)
                t = slice(c * QC, (c + 1) * QC)
                dve.wait_ge(projected, n)
                if counted(b * NHG + hg):
                    dve.wait_ge(rest_ready, b * NHG + hg)
                    dve.wait_ge(part_ready[1], b * NHG + hg)
                dve.tensor_copy(full[:, t], misc[0][0:FROWS]).then_inc(content_out, 1)
                dve.tensor_tensor(rope_b[ROPEQ:ROPE_END, t], misc[0][ROT:ROT + NROPE], rope_cs[ROT:ROT + NROPE, t],
                                  ALU.mult).then_inc(partner_out, 1)

            def normalize(b, hg, qc):
                n = halves(b, hg, qc)
                dve.wait_ge(turned, n)
                o = misc_of("turn", qc)[:].rearrange("p (t c) -> p t c", c=VW)
                dve.reciprocal(rsum[:], o[:, :, DH]).then_inc(rsum_ready, 1)
                if hg == 0 and counted(routed_groups(b, qc)):
                    dve.wait_ge(flip_mm, routed_groups(b, qc))
                dve.wait_ge(rsum_ready, n)
                tiles = QC // P
                cols = hg % NHG * HG * DH
                out = attn[:, qc * tiles:(qc + 1) * tiles, cols:cols + HG * DH]
                dve.tensor_tensor(out.rearrange("p t (h d) -> p t h d", d=DH),
                                  o[:, :, 0:DH].rearrange("p (t h) d -> p t h d", h=HG),
                                  rsum[:].rearrange("p (t h) -> p t h", h=HG).unsqueeze(3)
                                  .to_broadcast([P, tiles, HG, DH]),
                                  ALU.mult).then_inc(attn_ready, 1)

            def clip(b, n):
                w = UNITS[n % NU][3]
                diag = UNITS[n % NU][1] * P >= UNITS[n % NU][0] * QC
                p = prob_ap(n)
                dve.wait_ge(exped, banks_up_to(b, n))
                if not diag or w > P:
                    rest_ = p[:, :, P if diag else 0:w]
                    last = dve.tensor_scalar(rest_, rest_, P_HI, P_LO, ALU.min, ALU.max)
                if diag:
                    d_ = p[:, :, 0:P]
                    last = dve.scalar_tensor_tensor(
                        out=d_, in0=d_, scalar=P_LO,
                        in1=mask_hi[:].unsqueeze(1).to_broadcast([P, len(UNITS[n % NU][2]), P]),
                        op0=ALU.max, op1=ALU.min)
                last.then_inc(clipped, 1)

            def add_x(b, q):
                g = routed_groups(b, q)
                x = xrow[q][:, :, 0:D]
                dve.wait_ge(out_mm, g)
                dve.wait_ge(x_rows_in, b * (Q * 16))
                dve.tensor_tensor(x, misc_of("out", q)[:].rearrange("p (t d) -> p t d", d=D), x,
                                  ALU.add).then_inc(added, 1)

            def moments(b, q):
                g = routed_groups(b, q)
                dve.wait_ge(added, g)
                for t in range(QT):
                    last = dve.bn_stats(stats[q][:, t, :], xrow[q][:, t, 0:D])
                last.then_inc(stats_ready, 1)
                dve.wait_ge(stats_ready, g)
                dve.sem_inc(dve_seen, 1)
                for t in range(QT):
                    last = dve.bn_aggr(mean_var[q][:, t, :], stats[q][:, t, :])
                last.then_inc(mean_ready, 1)
                dve.wait_ge(mean_ready, g)
                dve.tensor_scalar(var_eps[q][:], mean_var[q][:, :, 1], EPS, None, ALU.add).then_inc(var_ready, 1)

            def layernorm(b, q):
                g = routed_groups(b, q)
                dve.wait_ge(rstd_ready, g)
                for t in range(QT):
                    x = xrow[q][:, t, 0:D]
                    last = dve.tensor_scalar(x, x, mean_var[q][:, t, 0:1], rstd[q][:, t:t + 1],
                                             ALU.subtract, ALU.mult)
                last.then_inc(normed, 1)

            def choose(b):
                def wide(ap):
                    return ap.unsqueeze(2).to_broadcast([P, NKT, E])

                dve.wait_ge(gate_mm, b)
                dve.tensor_tensor(logits[:], misc_of("gate", 0)[:, 0:NKT * E].rearrange("p (t e) -> p t e", e=E),
                                  gate_bias[:, 0, :].unsqueeze(1).to_broadcast([P, NKT, E]),
                                  ALU.add).then_inc(logits_out, 1)
                dve.wait_ge(logits_out, b)
                dve.tensor_reduce(top[:], logits[:], AX.X, ALU.max).then_inc(top_ready, 1)
                dve.wait_ge(top_ready, b)
                dve.tensor_tensor(reach[:], logits[:], wide(top[:]), ALU.is_ge).then_inc(reach_ready, 1)
                dve.wait_ge(reach_ready, b)
                dve.tensor_tensor(order[:], reach[:],
                                  const[:, CONST["descend"]].unsqueeze(1).to_broadcast([P, NKT, E]),
                                  ALU.mult).then_inc(order_ready, 1)
                dve.wait_ge(order_ready, b)
                dve.tensor_reduce(first[:], order[:], AX.X, ALU.max).then_inc(first_ready, 1)
                dve.wait_ge(first_ready, b)
                dve.tensor_tensor(onehot[:, 0:NKT, :], order[:], wide(first[:]),
                                  ALU.is_equal).then_inc(onehot_ready, 1)

            def assign(b):
                rank = misc_of("rank", 0)[:, 0:(NKT + 1) * E].rearrange("p (t e) -> p t e", e=E)
                dve.wait_ge(rank_mm, b)
                dve.wait_ge(carried, b)
                dve.tensor_tensor(place[:], rank[:, 0:NKT, :], next_row[:].unsqueeze(1).to_broadcast([P, NKT, E]),
                                  ALU.add).then_inc(placed, 1)
                dve.wait_ge(placed, b)
                dve.tensor_tensor(next_row[:], next_row[:], rank[:, NKT, :], ALU.add).then_inc(carried, 1)
                dve.tensor_tensor(chosen[:], place[:], onehot[:, 0:NKT, :], ALU.mult).then_inc(chosen_ready, 1)
                dve.wait_ge(chosen_ready, b)
                dve.tensor_reduce(place_of[:], chosen[:], AX.X, ALU.add).then_inc(place_ready, 1)
                dve.wait_ge(place_ready, b)
                dve.tensor_copy(index[:], place_of[:]).then_inc(index_ready, 1)

            def batch(b):
                later = not isinstance(b, int)
                for hg in range(NHG):
                    for u in range(NU):
                        clip(b, hg * NU + u)
                        for c in range(2):
                            if due(f"project{c}", hg, u):
                                take(b, hg + 2, c)
                        if due("turn1", hg, u) and (hg or later):
                            normalize(b, hg - 1, 1)
                        if due("turn0", hg, u):
                            normalize(b, hg, 0)
                        for q in range(Q):
                            if later and due(f"out{q}", hg, u):
                                add_x(b, q)
                            if later and due(f"moments{q}", hg, u):
                                moments(b, q)
                            if later and due(f"norm{q}", hg, u):
                                layernorm(b, q)
                        if later and due("gate0", hg, u):
                            choose(b)
                        if later and due("rank0", hg, u):
                            assign(b)

            for k in range(2):
                take(0, k, 0)
                take(0, k, 1)
            dve.wait_ge(tables_in, 16)
            dve.tensor_copy(upper[:], const[:, CONST["upper"]]).then_inc(upper_ready, 1)
            dve.tensor_copy(next_row[:], const[:, CONST["region"]]).then_inc(carried, 1)
            dve.wait_ge(mask_ready, 2)
            batch(0)
            dve.wait_ge(gate_in, 48)
            dve.tensor_tensor(gate_bias[:, 0, :], gate_bias[:, 0, :], gate_bias[:, 1, :], ALU.add).then_inc(bias_ready, 1)
            dve.wait_ge(bias_ready, 1)
            with dve.Fori(1, B) as b:
                batch(b)
            normalize(B, -1, 1)
            for q in range(Q):
                add_x(B, q)
                moments(B, q)
            for q in range(Q):
                layernorm(B, q)
            choose(B)
            assign(B)

            dve.wait_ge(carried, B + 1)
            dve.tensor_copy(pad_at[:], next_row[:]).then_inc(pad_ready, 1)
            dve.tensor_tensor(tokens_of[:], next_row[:], const[:, CONST["region"]], ALU.subtract).then_inc(plan, 1)
            dve.wait_ge(plan, 1)
            dve.tensor_tensor(begun[:], tokens_of[:].unsqueeze(2).to_broadcast([P, E, N // P]),
                              const[:, CONST["full_tiles"]].rearrange("p (e k) -> p e k", e=E),
                              ALU.is_gt).then_inc(plan, 1)
            dve.wait_ge(plan, 2)
            dve.tensor_reduce(tiles_of[:], begun[:], AX.X, ALU.add).then_inc(plan, 1)
            dve.wait_ge(plan, 3)
            dve.tensor_tensor(below[:], const[:, CONST["up_to"]].rearrange("p (e f) -> p e f", e=E),
                              tiles_of[:].unsqueeze(1).to_broadcast([P, E, E]), ALU.mult).then_inc(plan, 1)
            dve.tensor_scalar(skip_rows[:], tiles_of[:], -float(P), float(REGION), ALU.mult, ALU.add).then_inc(plan, 1)
            dve.wait_ge(plan, 5)
            dve.tensor_reduce(end_of[:], below[:], AX.X, ALU.add).then_inc(plan, 1)
            dve.wait_ge(plan, 6)
            dve.tensor_tensor(passed[:], const[:, CONST["tile"]].unsqueeze(2).to_broadcast([P, TILES, E]),
                              end_of[:].unsqueeze(1).to_broadcast([P, TILES, E]), ALU.is_ge).then_inc(plan, 1)
            dve.wait_ge(plan, 7)
            dve.tensor_reduce(tile_e[:], passed[:], AX.X, ALU.add).then_inc(plan, 1)
            dve.tensor_tensor(jump[:], passed[:], skip_rows[:].unsqueeze(1).to_broadcast([P, TILES, E]),
                              ALU.mult).then_inc(plan, 1)
            dve.wait_ge(plan, 9)
            dve.tensor_scalar(expert_tab[:], tile_e[:], float(E - 1), None, ALU.min).then_inc(planned, 1)
            dve.tensor_reduce(tile_sum[:], jump[:], AX.X, ALU.add).then_inc(plan, 1)
            dve.wait_ge(plan, 10)
            dve.tensor_tensor(tile_at[:], tile_sum[:], const[:, CONST["tile_row"]], ALU.add).then_inc(plan, 1)
            dve.wait_ge(plan, 11)
            dve.tensor_scalar(row_tab[:], tile_at[:], float(DUMMY), None, ALU.min).then_inc(planned, 1)

            def hidden_out(r, c):
                dve.wait_ge(up_mm, r * RING + (c + 1))
                if counted(r * RING + (c - 1)):
                    dve.wait_ge(h_turned, r * RING + (c - 1))
                dve.tensor_copy(hidden[c % 2], scores[2 + c % 2][:]).then_inc(hidden_ready, 1)

            def y_moments(r, c):
                n = r * RING + (c + 1)
                dve.wait_ge(down_mm, n)
                dve.wait_ge(x_b2_ready, n)
                dve.tensor_tensor(ys[c % 2][:], misc[c % 2][:, 0:D], x_b2[c % STAGES][:], ALU.add).then_inc(y_out, 1)
                dve.wait_ge(y_out, n)
                dve.bn_stats(y_stats[c % 2][:], ys[c % 2][:]).then_inc(y_stat, 1)
                dve.wait_ge(y_stat, n)
                dve.sem_inc(dve_seen, 1)
                dve.bn_aggr(y_mean[c % 2][:], y_stats[c % 2][:]).then_inc(y_meaned, 1)
                dve.wait_ge(y_meaned, n)
                dve.tensor_scalar(y_var[c % 2][:], y_mean[c % 2][:, 1:2], EPS, None, ALU.add).then_inc(y_vared, 1)

            def y_norm(r, c):
                dve.wait_ge(y_rstd_ready, r * RING + (c + 1))
                dve.tensor_scalar(zs[c % RING][:], ys[c % 2][:], y_mean[c % 2][:, 0:1], y_rstd[c % 2][:],
                                  ALU.subtract, ALU.mult).then_inc(z_ready, 1)

            def steps(r, cs, live):
                for c in cs:
                    step(r, c, live)

            def step(r, c, live):
                if live(c):
                    hidden_out(r, c)
                if live(c - 3):
                    y_norm(r, c - 3)
                if live(c - 2):
                    y_moments(r, c - 2)

            mlp_loop(dve, steps)

        @block.scalar
        def _(act):
            def part0(k, busy):
                act.wait_ge(rope_out, k * 2 + 2)
                if busy:
                    act.wait_ge(spilled, k * (SPILLS * 16))
                act.activation(parts[:, 0, :], full[:], ACT.Copy).then_inc(part_ready[0], 1)

            def v_evac(b, c):
                act.wait_ge(v_mm, b * 2 + (2 + c + 1))
                half = v_tok[:, c * (NKT // 2):(c + 1) * (NKT // 2)]
                act.activation(half.rearrange("p t h d -> p (t h d)"), misc_of("v", c)[:], ACT.Copy).then_inc(v_out, 1)

            def exp(b, n, m):
                act.wait_ge(scored, b * BB + (m + 1))
                if counted(groups_up_to(b, n - P_SLOTS)):
                    act.wait_ge(weighted, groups_up_to(b, n - P_SLOTS))
                _, start, heads = BANKS[m % NBK]
                act.activation(prob_ap(n)[:, start:start + heads], score_ap(m), ACT.Exp,
                               scale=SCALE).then_inc(exped, 1)

            def o_evac(b, hg, qc):
                act.wait_ge(weighted, b * GB + (hg * NG + QC_GROUPS[qc]))
                if counted(halves(b, hg - 1, qc)):
                    act.wait_ge(turned, halves(b, hg - 1, qc))
                act.activation(o_sb[qc][:], o_acc[qc][:], ACT.Copy).then_inc(o_out, 1)

            def flip_evac(kind, b, q):
                ready, done = {"flip": (flip_mm, flip_out), "turnx": (turnx_mm, turnx_out)}[kind]
                act.wait_ge(ready, routed_groups(b, q))
                act.activation(flipped[q][:], misc_of(kind, q)[:], ACT.Copy).then_inc(done, 1)

            def batch(b):
                later = not isinstance(b, int)
                for hg in range(NHG):
                    for u in range(NU):
                        for m in BANKS_OF[u]:
                            exp(b, hg * NU + u, hg * NBK + m)
                        if due("evac1", hg, u) and (hg or later):
                            o_evac(b, hg - 1, 1)
                        if due("part0", hg, u):
                            part0(b * NHG + (hg + 2), True)
                        if due("evac0", hg, u):
                            o_evac(b, hg, 0)
                        for c in range(2):
                            if due(f"v{c}", hg, u):
                                act.wait_ge(v_ready, b * NHG + NHG)
                                v_evac(b, c)
                        for q in range(Q):
                            for kind in ("flip", "turnx"):
                                if later and due(f"{kind}{q}", hg, u):
                                    flip_evac(kind, b, q)

            part0(0, False)
            part0(1, True)
            v_evac(-1, 0)
            v_evac(-1, 1)
            batch(0)
            with act.Fori(1, B) as b:
                batch(b)
            o_evac(B, -1, 1)
            for kind in ("flip", "turnx"):
                for q in range(Q):
                    flip_evac(kind, B, q)

            def xT_evac(r, c):
                act.wait_ge(xs_turned, r * RING + (c + 1))
                if counted(r * RING + (c - 1)):
                    act.wait_ge(up_mm, r * RING + (c - 1))
                act.activation(xsT[c % 2][:], scores[c % 2][:, 0:P], ACT.Copy).then_inc(xsT_ready, 1)

            def relu(r, c):
                e = act.value_load(tile_entry(expert_tab, r, c), min_val=0, max_val=E - 1)
                act.wait_ge(h_turned, r * RING + (c + 1))
                if counted(r * RING + (c - 1)):
                    act.wait_ge(down_mm, r * RING + (c - 1))
                for f in range(DFF // P):
                    t = slice(f * P, (f + 1) * P)
                    last = act.activation(hiddenT[c % 2][:, t], o_acc[c % 2][:, t], ACT.Relu,
                                          bias=b1T[:, bass.ds(e * (DFF // P) + f, 1)])
                last.then_inc(hiddenT_ready, 1)

            def steps(r, cs, live):
                for c in cs:
                    step(r, c, live)

            def step(r, c, live):
                if live(c + 1):
                    xT_evac(r, c + 1)
                if live(c - 1):
                    relu(r, c - 1)

            act.wait_ge(planned, 2)
            act.wait_ge(mlp_in, 4 * 16)
            xT_evac(0, 0)
            mlp_loop(act, steps)

        @block.tensor
        def _(pe):
            pe.wait_ge(weights_in, 48)
            pe.wait_ge(up_in, 64)
            pe.matmul(misc[0][:, 0:128], dqT[:], up[:, 0, :], start=True, stop=True)
            pe.matmul(misc[0][:, 128:192], dqT[:], up[:, 1, 0:64], start=True, stop=True)
            pe.matmul(misc[0][:, 192:320], dkvT[:], up[:, 2, :], start=True, stop=True)
            pe.matmul(misc[0][:, 320:448], dkvT[:], up[:, 3, :], start=True, stop=True).then_inc(fused_mm, 1)

            def project(c, hg):
                pe.matmul(misc_of("project", c)[:], w_hg[:, hg, :], xT[:, c * QC:(c + 1) * QC],
                          start=True, stop=True).then_inc(projected, 1)

            def v_rows(c):
                for t in range(QC // P):
                    last = pe.matmul(misc_of("v", c)[:, t * P:(t + 1) * P],
                                     xT[:, c * QC + t * P:c * QC + (t + 1) * P], w_v[:], start=True, stop=True)
                last.then_inc(v_mm, 1)

            def score(b, m):
                unit, start, count = BANKS[m % NBK]
                _, kt, heads, w = UNITS[unit]
                qc = UNITS[unit][0]
                par = m // NBK % 2
                old = m - SCORE_SLOTS if m >= SCORE_SLOTS else \
                    max(i for i in range(BB) if i % SCORE_SLOTS == m % SCORE_SLOTS) - BB
                if counted(b * BB + (old + 1)):
                    pe.wait_ge(exped, b * BB + (old + 1))
                out = score_ap(m)
                for i in range(count):
                    j = heads[start + i]
                    last = pe.matmul(out[:, i, :], k_stack[par][:, j, kt * P:(kt + 1) * P],
                                     q_stack[par][:, j, (qc + 1) * QC - w:(qc + 1) * QC], start=True, stop=True)
                last.then_inc(scored, 1)

            def weigh(b, n):
                if n % NU not in LAST_UNIT:
                    return
                g, hg = LAST_UNIT.index(n % NU), n // NU
                qc, kt = GROUPS[g]
                par = hg % 2
                pe.wait_ge(clipped, b * UB + (n + 1))
                if kt == 0:
                    if qc == 0:
                        pe.wait_ge(v_ready, b * NHG + (hg + 1))
                    if counted(halves(b, hg - 1, qc)):
                        pe.wait_ge(o_out, halves(b, hg - 1, qc))
                for u in range(NU):
                    if GROUP_OF[u] == g:
                        _, _, heads, w = UNITS[u]
                        p = prob_ap(hg * NU + u)
                        for i, j in enumerate(heads):
                            last = pe.matmul(o_acc[qc][j * VW:(j + 1) * VW, QC - w:QC], v_stat[par][:, kt, j, :],
                                             p[:, i, :], start=kt == 0, stop=g + 1 == QC_GROUPS[qc])
                last.then_inc(weighted, 1)

            def turn(b, hg, qc):
                pe.wait_ge(o_out, halves(b, hg, qc))
                free = before(b, ("turn", hg, qc))
                if counted(free[1]):
                    pe.wait_ge(*free)
                for t in range(QC // P):
                    last = pe.transpose(misc_of("turn", qc)[:, t * P:(t + 1) * P], o_sb[qc][:, t * P:(t + 1) * P],
                                        ident[:])
                last.then_inc(turned, 1)

            def routing(b, hg, kind, q):
                g = routed_groups(b, q)
                bank = misc_of(kind, q)
                pe.wait_ge(*before(b, (kind, hg, q)))
                if kind == "flip":
                    pe.wait_ge(attn_ready, halves(b, -1, 1))
                    for t in range(QT):
                        last = pe.transpose(bank[:, t * P:(t + 1) * P], attn[:, q * QT + t, :], ident[:])
                    last.then_inc(flip_mm, 1)
                elif kind == "out":
                    pe.wait_ge(flip_out, g)
                    pe.wait_ge(out_w_in, 16)
                    for t in range(QT):
                        last = pe.matmul(bank[:, t * D:(t + 1) * D], flipped[q][:, t * P:(t + 1) * P], w_o[:],
                                         start=True, stop=True)
                    last.then_inc(out_mm, 1)
                elif kind == "turnx":
                    pe.wait_ge(normed, g)
                    for t in range(QT):
                        last = pe.transpose(bank[:, t * P:(t + 1) * P], xrow[q][:, t, 0:D], ident[:])
                    last.then_inc(turnx_mm, 1)
                elif kind == "gate":
                    pe.wait_ge(turnx_out, routed_groups(b, Q - 1))
                    pe.wait_ge(gate_in, 48)
                    for t in range(NKT):
                        turned_x = flipped[t // QT][:, t % QT * P:(t % QT + 1) * P]
                        last = pe.matmul(bank[:, t * E:(t + 1) * E], turned_x, gate_wT[:], start=True, stop=True)
                    last.then_inc(gate_mm, 1)
                else:
                    pe.wait_ge(onehot_ready, b)
                    pe.wait_ge(upper_ready, 1)
                    hot = onehot[:].rearrange("p t e -> p (t e)")
                    width = (NKT + 1) * E
                    pe.matmul(bank[:, 0:width], upper[:], hot, start=True, stop=False, skip_group_check=True)
                    for s in range(1, NKT + 1):
                        last = pe.matmul(bank[:, s * E:width], ones[:], hot[:, 0:width - s * E],
                                         start=False, stop=s == NKT, skip_group_check=True)
                    last.then_inc(rank_mm, 1)

            def batch(b):
                later = not isinstance(b, int)
                for hg in range(NHG):
                    n_stack = STACKS * 16
                    pe.wait_ge(stack_in[hg % 2], b * (2 * n_stack) + (hg // 2 + 1) * n_stack)
                    for u in range(NU):
                        n = hg * NU + u
                        for m in BANKS_OF[u]:
                            score(b, hg * NBK + m)
                        if n >= LAG or later:
                            weigh(b, n - LAG)
                        for c in range(2):
                            if due(f"project{c}", hg, u):
                                if hg == 2 and c == 0:
                                    pe.wait_ge(xT_in, b * 16 + 32)
                                pe.wait_ge(*before(b, ("project", hg, c)))
                                project(c, (hg + 2) % NHG)
                            if due(f"v{c}", hg, u):
                                pe.wait_ge(*before(b, ("v", hg, c)))
                                v_rows(c)
                        if due("turn1", hg, u) and (hg or later):
                            turn(b, hg - 1, 1)
                        if due("turn0", hg, u):
                            turn(b, hg, 0)
                        for q in range(Q):
                            for kind in ROUTING:
                                if later and f"{kind}{q}" in STEPS and due(f"{kind}{q}", hg, u):
                                    routing(b, hg, kind, q)

            pe.wait_ge(fused, 1)
            pe.wait_ge(xT_in, 16)
            for k in range(2):
                for c in range(2):
                    if k or c:
                        pe.wait_ge(partner_out, 2 * k + c)
                    project(c, k)
            pe.wait_ge(partner_out, 4)
            v_rows(0)
            pe.wait_ge(v_out, 1)
            v_rows(1)
            pe.wait_ge(ident_ready, 2)
            batch(0)
            with pe.Fori(1, B) as b:
                batch(b)
            for n in range(-LAG, 0):
                weigh(B, n)
            turn(B, -1, 1)
            for kind in ROUTING[0:3]:
                for q in range(Q):
                    routing(B, STEPS[f"{kind}{q}"][0], kind, q)
            for kind in ROUTING[3:]:
                routing(B, STEPS[f"{kind}0"][0], kind, 0)

            pe.wait_ge(exped, B * BB)
            pe.wait_ge(carried, B + 1)
            pe.wait_ge(planned, 2)
            pe.wait_ge(mlp_in, 4 * 16)

            def turn_x(r, c):
                pe.wait_ge(xs_in[c % RING], r * 16 + (c // RING + 1) * 16)
                if counted(r * RING + (c - 1)):
                    pe.wait_ge(xsT_ready, r * RING + (c - 1))
                pe.transpose(scores[c % 2][:, 0:P], xs[c % RING][:, 0:D], ident[:]).then_inc(xs_turned, 1)

            def up_rows(r, c, e):
                pe.wait_ge(xsT_ready, r * RING + (c + 1))
                if counted(r * RING + (c - 1)):
                    pe.wait_ge(hidden_ready, r * RING + (c - 1))
                pe.matmul(scores[2 + c % 2][:], xsT[c % 2][:], w1[:, bass.ds(e * DFF, DFF)],
                          start=True, stop=True).then_inc(up_mm, 1)

            def turn_hidden(r, c):
                pe.wait_ge(hidden_ready, r * RING + (c + 1))
                if counted(r * RING + (c - 1)):
                    pe.wait_ge(hiddenT_ready, r * RING + (c - 1))
                for f in range(DFF // P):
                    last = pe.transpose(o_acc[c % 2][:, f * P:(f + 1) * P], hidden[c % 2][:, f * P:(f + 1) * P],
                                        ident[:])
                last.then_inc(h_turned, 1)

            def down_rows(r, c, e):
                pe.wait_ge(hiddenT_ready, r * RING + (c + 1))
                if counted(r * RING + (c - 1)):
                    pe.wait_ge(y_out, r * RING + (c - 1))
                w2_cols = w2[:].rearrange("p c d -> p (c d)")
                for f in range(DFF // P):
                    last = pe.matmul(misc[c % 2][:, 0:D], hiddenT[c % 2][:, f * P:(f + 1) * P],
                                     w2_cols[:, bass.ds(e * DFF + f * D, D)], start=f == 0, stop=f == DFF // P - 1)
                last.then_inc(down_mm, 1)

            def steps(r, cs, live):
                loaded = {}

                def expert(c):
                    if c not in loaded:
                        loaded[c] = pe.value_load(tile_entry(expert_tab, r, c), min_val=0, max_val=E - 1)
                    return loaded[c]

                for c in cs:
                    if live(c):
                        up_rows(r, c, expert(c))
                    if c + 1 in cs and live(c + 1):
                        expert(c + 1)
                    if live(c - 1):
                        turn_hidden(r, c - 1)
                    if live(c + 1):
                        turn_x(r, c + 1)
                    if live(c - 2):
                        down_rows(r, c - 2, expert(c - 2))

            turn_x(0, 0)
            mlp_loop(pe, steps)


def rope_table():
    inv = np.float32(THETA) ** (-np.arange(0, DR, 2, dtype=np.float32) / np.float32(DR))
    ang = np.arange(S, dtype=np.float32)[None, :] * inv.astype(np.float32)[:, None]
    table = np.zeros((P, S), np.float32)
    table[CONTQ:ROPEQ] = 1.0
    for r in range(NROPE):
        d = r // HG if r < HG * DR else r - HG * DR
        table[ROPEQ + r] = np.cos(ang[d // 2])
        table[ROT + r] = np.sin(ang[d // 2]) * (np.float32(1.0) if d % 2 else np.float32(-1.0))
    return table


def constants():
    p = np.arange(P, dtype=np.float32)
    table = np.zeros((P, CONST_W), np.float32)
    table[:, CONST["upper"]] = p[:, None] < p[None, :]
    table[:, CONST["descend"]] = E - np.arange(E)
    table[:, CONST["region"]] = REGION * np.arange(E)
    table[:, CONST["full_tiles"]] = np.tile(P * np.arange(N // P), E)
    table[:, CONST["up_to"]] = (np.arange(E)[:, None] >= np.arange(E)[None, :]).reshape(-1)
    table[:, CONST["tile"]] = np.arange(TILES)
    table[:, CONST["tile_row"]] = P * np.arange(TILES)
    table[:, CONST["half"]] = -0.5
    return table


def with_ids(rows, ids):
    out = np.zeros((rows.shape[0], ROW), np.int32)
    out[:, 0:D] = np.ascontiguousarray(rows).view(np.int32)
    out[:, D] = ids
    return out.view(np.float32)


def kernel(**inputs):
    import concourse.bacc as bacc
    from concourse.bass_utils import run_bass_kernel_spmd

    a = {k: np.asarray(v) for k, v in inputs.items()}
    x = a["L0_attn_x"]
    x_T = x.transpose(0, 2, 1)
    arrays = {
        "x_T": np.concatenate([x_T, x_T[:1]]),
        "x_rows": with_ids(x.reshape(N, D), np.arange(N)).reshape(2 * B, S // 2, ROW),
        "pad_rows": with_ids(np.zeros((P, D), np.float32), N + np.arange(P)),
        "W_DQ_T": np.ascontiguousarray(a["L0_attn_W_DQ"].T),
        "W_DKV_T": np.ascontiguousarray(a["L0_attn_W_DKV"].T),
        "W_UQ": a["L0_attn_W_UQ"], "W_QR": a["L0_attn_W_QR"], "W_UK": a["L0_attn_W_UK"],
        "W_UV": a["L0_attn_W_UV"], "W_KR": a["L0_attn_W_KR"], "W_O": a["L0_attn_W_O"],
        "gate_w_T": np.ascontiguousarray(a["L0_ffn_gate_w"].T),
        "gate_b": a["L0_ffn_gate_b"].reshape(1, E), "expert_bias": a["L0_ffn_expert_bias"].reshape(1, E),
        "w1": a["L0_ffn_w1"], "b1_T": np.ascontiguousarray(a["L0_ffn_b1"].reshape(E * DFF // P, P).T),
        "w2": a["L0_ffn_w2"], "b2": a["L0_ffn_b2"].reshape(1, E * D),
        "rope_cs": rope_table(),
        "const": constants(),
    }
    nc = bacc.Bacc("TRN2", target_bir_lowering=False, num_devices=1)
    io = {k: nc.dram_tensor("in_" + k, v.shape, mybir.dt.from_np(v.dtype), kind="ExternalInput").ap()
          for k, v in arrays.items()}
    io["out"] = nc.dram_tensor("out", (N, D), F32, kind="ExternalOutput").ap()
    build(nc, io)
    r = run_bass_kernel_spmd(nc, [{"in_" + k: v for k, v in arrays.items()}], core_ids=[0])
    return r.results[0]["out"].reshape(B, S, D)
```

```python
from contextlib import ExitStack

import numpy as np

import concourse.bass as bass
from concourse import mybir

F32, BF16 = mybir.dt.float32, mybir.dt.bfloat16
I32, U32 = mybir.dt.int32, mybir.dt.uint32
ALU = mybir.AluOpType
ACT = mybir.ActivationFunctionType
AX = mybir.AxisListType

P = 128
B, S, D = 4, 1024, 128
HEADS, DH, DR, LATENT = 16, 8, 4, 32
THETA = 10000.0
CLIP = 80.0
EPS = 1e-5
E, DFF = 8, 512
N = B * S

HG = 4
NHG = HEADS // HG
QC = 512
NKT = S // P
SPLITS = 3
TERMS = SPLITS * SPLITS
ROWS = TERMS * (DH + DR)
VW = 32
VS = DH + 1
CONTQ, ROPEQ, ROPEK, CONTK, ROT = 0, 32, 48, 64, 96
NROPE = HG * DR + DR
ROPE_END = ROPEQ + NROPE
FROWS = ROT
SCALE = 1.0 / float(np.sqrt(np.float32(DH + DR)))
P_LO, P_HI = float(np.exp(-CLIP * SCALE)), float(np.exp(CLIP * SCALE))


def unit_table():
    out = []
    for qc in range(S // QC):
        for kt in range((qc + 1) * QC // P):
            w = QC - max(0, kt * P - qc * QC)
            if w > QC // 2:
                out += [(qc, kt, (0, 1), w), (qc, kt, (2, 3), w)]
            else:
                out.append((qc, kt, (0, 1, 2, 3), w))
    return out


UNITS = unit_table()
NU = len(UNITS)
GROUPS = sorted({(qc, kt) for qc, kt, _, _ in UNITS})
NG = len(GROUPS)
GROUP_OF = [GROUPS.index((qc, kt)) for qc, kt, _, _ in UNITS]
LAST_UNIT = [max(n for n in range(NU) if GROUP_OF[n] == g) for g in range(NG)]
QC_GROUPS = [max(g for g in range(NG) if GROUPS[g][0] == qc) + 1 for qc in range(S // QC)]
UB, GB = NU * NHG, NG * NHG


def bank_table():
    out = []
    for n, (_, _, heads, w) in enumerate(UNITS):
        m = QC // w
        out += [(n, i, min(m, len(heads))) for i in range(0, len(heads), min(m, len(heads)))]
    return out


BANKS = bank_table()
NBK = len(BANKS)
BB = NBK * NHG
BANKS_OF = [[m for m in range(NBK) if BANKS[m][0] == n] for n in range(NU)]

SPILLS, STACKS = 3 * SPLITS, 3 * SPLITS - 1
SCORE_SLOTS = 4
P_SLOTS = 10
LAG = 6

Q = 2
QT = NKT // Q
ROW = D + 4
REGION = N + P
DUMMY = E * REGION
TILES = N // P + E - 1
RING = 6
BODY = 2
STAGES = 3
HEAD = RING
ROUNDS = (TILES - HEAD - 1) // (BODY * RING) * BODY

LATENT_COLS, LATENT_W = {}, 0
for _name, _w in (("W_DQ_T", D), ("W_DKV_T", D), ("W_UQ", HEADS * DH), ("W_QR", HEADS * DR), ("W_UK", HEADS * DH),
                  ("W_UV", HEADS * DH)):
    LATENT_COLS[_name] = slice(LATENT_W, LATENT_W + _w)
    LATENT_W += _w

CONST, CONST_W = {}, 0
for _name, _w in (("upper", P), ("descend", E), ("region", E), ("full_tiles", E * N // P), ("up_to", E * E),
                  ("tile", TILES), ("tile_row", TILES), ("half", QT)):
    CONST[_name] = slice(CONST_W, CONST_W + _w)
    CONST_W += _w

EACH, EVEN, ODD = range(NHG), range(0, NHG, 2), range(1, NHG, 2)
STEPS = {
    "project0": (EACH, 2), "project1": (EACH, 7), "part0": (EACH, 14), "evac0": (ODD, 14), "turn0": (ODD, 16),
    "evac1": (EVEN, 6), "turn1": (EVEN, 10), "v0": ([2], 8), "v1": ([3], 14), "flip0": ([0], 18),
    "flip1": ([1], 0), "out0": ([1], 2), "out1": ([1], 14), "moments0": ([1], 6), "norm0": ([1], 9),
    "moments1": ([1], 15), "norm1": ([2], 4), "turnx0": ([2], 4), "turnx1": ([2], 16), "gate0": ([2], 18),
    "rank0": ([3], 4),
}
BANK_OF = {"project": 0, "v0": 1, "v1": 0, "turn": 1, "flip0": 0, "flip1": 0, "out0": 1, "out1": 0,
           "turnx0": 1, "turnx1": 1, "gate0": 0, "rank0": 1}


def due(name, hg, u):
    return hg in STEPS[name][0] and u == STEPS[name][1]


def bank_jobs(bank):
    jobs = []
    for hg in range(NHG):
        for u in range(NU):
            for name in STEPS:
                kind, half = name[:-1], int(name[-1])
                if due(name, hg, u) and BANK_OF.get(kind, BANK_OF.get(name)) == bank:
                    jobs.append((kind, hg // 2 - (name == "turn1") if kind == "turn" else hg, half))
    return jobs


BANK_JOBS = [bank_jobs(bank) for bank in range(2)]
ROUTING = ("flip", "out", "turnx", "gate", "rank")
TAIL_JOBS = [[("turn", -1, 1) if j[0] == "turn" else j for j in BANK_JOBS[bank]
              if j[0] in ROUTING or j == ("turn", -1, 1)] for bank in range(2)]


def counted(n):
    return not (isinstance(n, int) and n <= 0)


def tile_entry(table, r, c):
    return table[0:1, c:c + 1] if isinstance(r, int) else table[0:1, bass.ds(r * RING + c, 1)]


def mlp_loop(eng, steps):
    def exists(c):
        return 0 <= c < TILES

    steps(0, range(HEAD), exists)
    with eng.Fori(0, ROUNDS, BODY) as r:
        steps(r, range(HEAD, HEAD + BODY * RING), lambda c: True)
    steps(0, range(HEAD + ROUNDS * RING, TILES + STAGES), exists)


def build(nc, io):
    ctx = ExitStack()
    with ctx:
        def sb(name, shape, dt=F32):
            return ctx.enter_context(nc.sbuf_tensor(name, shape, dt))

        def ps(name, shape, dt=F32):
            return ctx.enter_context(nc.psum_tensor(name, shape, dt))

        def sem(name):
            return ctx.enter_context(nc.semaphore(name))

        scores = [ps(f"scores{i}", [P, QC]) for i in range(SCORE_SLOTS)]
        o_acc = [ps(f"o_acc{i}", [P, QC]) for i in range(2)]
        misc = [ps(f"misc{i}", [P, QC]) for i in range(2)]

        ident = sb("ident", [P, P])
        mask_hi = sb("mask_hi", [P, P])
        rope_cs = sb("rope_table", [P, S])
        const = sb("const", [P, CONST_W])
        upper = sb("upper", [P, P], BF16)
        ones = sb("ones", [P, P], BF16)
        latent = sb("latent", [LATENT, LATENT_W])
        kr = sb("kr", [D, DR])
        w_hg = sb("w_hg", [D, NHG, P])
        w_v = sb("w_v", [D, P])
        w_o = sb("w_o", [HEADS * DH, D])
        xT = sb("xT", [D, S])
        full = sb("full", [FROWS, S])
        rope_b = sb("rope_b", [ROPE_END, S])
        parts = sb("parts", [FROWS, SPLITS, S], BF16)
        rest = sb("rest", [FROWS, S])
        q_stack = [sb(f"q_stack{i}", [ROWS, HG, S], BF16) for i in range(2)]
        k_stack = [sb(f"k_stack{i}", [ROWS, HG, S], BF16) for i in range(2)]
        v_tok = sb("v_tok", [P, NKT, HEADS, DH])
        v_stat = [sb(f"v_stat{i}", [P, NKT, HG, VW]) for i in range(2)]
        prob = [sb(f"prob{i}", [P, 2 * QC]) for i in range(P_SLOTS)]
        o_sb = [sb(f"o_sb{i}", [P, QC]) for i in range(2)]
        rsum = sb("rsum", [P, 2 * QC // P * HG])
        attn = sb("attn", [P, NKT, D])
        xrow = [sb(f"xrow{i}", [P, QT, ROW]) for i in range(Q)]
        flipped = [sb(f"flipped{i}", [P, QT * P]) for i in range(Q)]
        stats = [sb(f"stats{i}", [P, QT, 6]) for i in range(Q)]
        mean_var = [sb(f"mean_var{i}", [P, QT, 2]) for i in range(Q)]
        var_eps = [sb(f"var_eps{i}", [P, QT]) for i in range(Q)]
        rstd = [sb(f"rstd{i}", [P, QT]) for i in range(Q)]
        gate_wT = sb("gate_wT", [D, E])
        gate_bias = sb("gate_bias", [P, 2, E])
        logits = sb("logits", [P, NKT, E])
        top = sb("top", [P, NKT])
        reach = sb("reach", [P, NKT, E])
        order = sb("order", [P, NKT, E])
        first = sb("first", [P, NKT])
        onehot = sb("onehot", [P, NKT + 1, E], BF16)
        last_hot = [sb(f"last_hot{i}", [P, QT + 1, E], BF16) for i in range(Q)]
        place = sb("place", [P, NKT, E])
        chosen = sb("chosen", [P, NKT, E])
        place_of = sb("place_of", [P, NKT])
        index = sb("index", [P, NKT], U32)
        next_row = sb("next_row", [P, E])
        pad_row = sb("pad_row", [P, ROW])
        pad_at = sb("pad_at", [P, E], I32)
        tokens_of = sb("tokens_of", [P, E])
        begun = sb("begun", [P, E, N // P])
        tiles_of = sb("tiles_of", [P, E])
        below = sb("below", [P, E, E])
        end_of = sb("end_of", [P, E])
        skip_rows = sb("skip_rows", [P, E])
        passed = sb("passed", [P, TILES, E])
        jump = sb("jump", [P, TILES, E])
        tile_e = sb("tile_e", [P, TILES])
        tile_at = sb("tile_at", [P, TILES])
        tile_sum = sb("tile_sum", [P, TILES])
        expert_tab = sb("expert_tab", [P, TILES], I32)
        row_tab = sb("row_tab", [P, TILES], I32)
        w1 = sb("w1", [D, E * DFF])
        w2 = sb("w2", [P, E * DFF // P, D])
        b1T = sb("b1T", [P, E * DFF // P])
        b2 = sb("b2", [P, E * D])
        xs = [sb(f"xs{i}", [P, ROW]) for i in range(RING)]
        xsT = [sb(f"xsT{i}", [P, P]) for i in range(2)]
        hidden = [prob[0][:, i * DFF:(i + 1) * DFF] for i in range(2)]
        hiddenT = [prob[1][:, i * DFF:(i + 1) * DFF] for i in range(2)]
        x_b2 = [sb(f"x_b2{i}", [P, D]) for i in range(STAGES)]
        ids = [sb(f"ids{i}", [P, 1], U32) for i in range(RING)]
        ys = [sb(f"ys{i}", [P, D]) for i in range(2)]
        zs = [sb(f"zs{i}", [P, D]) for i in range(RING)]
        y_stats = [sb(f"y_stats{i}", [P, 6]) for i in range(2)]
        y_mean = [sb(f"y_mean{i}", [P, 2]) for i in range(2)]
        y_var = [sb(f"y_var{i}", [P, 1]) for i in range(2)]
        y_rstd = [sb(f"y_rstd{i}", [P, 1]) for i in range(2)]

        q_spill = [nc.dram_tensor(f"q_spill{i}", (SPLITS, DH + DR, HG, S), BF16, kind="Internal").ap() for i in range(2)]
        k_spill = [nc.dram_tensor(f"k_spill{i}", (SPLITS, DH + DR, HG, S), BF16, kind="Internal").ap() for i in range(2)]
        by_expert = nc.dram_tensor("by_expert", (DUMMY + P, ROW), F32, kind="Internal").ap()

        weights_in, kr_in, const_in, tables_in = sem("weights_in"), sem("kr_in"), sem("const_in"), sem("tables_in")
        out_w_in, gate_in, mlp_in, pad_in = sem("out_w_in"), sem("gate_in"), sem("mlp_in"), sem("pad_in")
        ident_ready, mask_ready, w_zero = sem("ident_ready"), sem("mask_ready"), sem("w_zero")
        upper_ready = sem("upper_ready")
        bias_ready, carried = sem("bias_ready"), sem("carried")
        first_mul, first_rope = sem("first_mul"), sem("first_rope")
        fused_mm, fused = sem("fused_mm"), sem("fused")
        xT_in = sem("xT_in")
        projected, content_out, partner_out = sem("projected"), sem("content_out"), sem("partner_out")
        rope_mul, rope_out = sem("rope_mul"), sem("rope_out")
        part_ready = [sem(f"part{i}_ready") for i in range(SPLITS)]
        rest_ready = sem("rest_ready")
        spilled = sem("spilled")
        stack_in = [sem(f"stack_in{i}") for i in range(2)]
        v_mm, v_out, v_pad, v_ready = sem("v_mm"), sem("v_out"), sem("v_pad"), sem("v_ready")
        scored, exped, clipped, weighted = sem("scored"), sem("exped"), sem("clipped"), sem("weighted")
        o_out, turned, rsum_ready, attn_ready = sem("o_out"), sem("turned"), sem("rsum_ready"), sem("attn_ready")
        flip_mm, flip_out, out_mm, x_rows_in = sem("flip_mm"), sem("flip_out"), sem("out_mm"), sem("x_rows_in")
        added, stats_ready, mean_ready, var_ready = sem("added"), sem("stats_ready"), sem("mean_ready"), sem("var_ready")
        rstd_ready, normed, turnx_mm, turnx_out = sem("rstd_ready"), sem("normed"), sem("turnx_mm"), sem("turnx_out")
        gate_mm, logits_out, top_ready, reach_ready = sem("gate_mm"), sem("logits_out"), sem("top_ready"), sem("reach_ready")
        order_ready, first_ready, onehot_ready = sem("order_ready"), sem("first_ready"), sem("onehot_ready")
        rank_mm, placed, chosen_ready, place_ready = sem("rank_mm"), sem("placed"), sem("chosen_ready"), sem("place_ready")
        index_ready, routed = sem("index_ready"), sem("routed")
        pad_ready, padded, dummy_out = sem("pad_ready"), sem("padded"), sem("dummy_out")
        plan, planned = sem("plan"), sem("planned")
        xs_in = [sem(f"xs_in{i}") for i in range(RING)]
        xs_turned, xsT_ready, up_mm = sem("xs_turned"), sem("xsT_ready"), sem("up_mm")
        hidden_ready, h_turned, hiddenT_ready = sem("hidden_ready"), sem("h_turned"), sem("hiddenT_ready")
        down_mm, y_out, y_stat, y_meaned = sem("down_mm"), sem("y_out"), sem("y_stat"), sem("y_meaned")
        y_vared, y_rstd_ready, z_ready, x_b2_ready, ids_ready = sem("y_vared"), sem("y_rstd_ready"), sem("z_ready"), sem("x_b2_ready"), sem("ids_ready")
        written = [sem(f"written{i}") for i in range(RING)]

        pool_seen, dve_seen, sp_seen = sem("pool_seen"), sem("dve_seen"), sem("sp_seen")

        block = ctx.enter_context(nc.Block())

        def score_ap(m):
            unit, _, heads = BANKS[m % NBK]
            w = UNITS[unit][3]
            return scores[m % SCORE_SLOTS][:, 0:heads * w].rearrange("p (h w) -> p h w", w=w)

        def prob_ap(n):
            _, _, heads, w = UNITS[n % NU]
            return prob[n % P_SLOTS][:, 0:len(heads) * w].rearrange("p (h w) -> p h w", w=w)

        def banks_up_to(b, n):
            return b * BB + (n // NU * NBK + BANKS_OF[n % NU][-1] + 1)

        def groups_up_to(b, n):
            return b * GB + (n // NU * NG + GROUP_OF[n % NU] + 1)

        def halves(b, hg, half):
            return b * (2 * NHG) + (2 * hg + half + 1)

        def sums(b, pair, half):
            return b * NHG + (2 * pair + half + 1)

        def routed_groups(b, q):
            return b * Q + (q - Q + 1)

        def reader_done(b, job):
            kind, hg, half = job
            return {
                "project": (partner_out, halves(b, hg + 2, half)),
                "v": (v_out, b * 2 + (2 + half + 1)),
                "turn": (attn_ready, sums(b, hg, half)),
                "flip": (flip_out, routed_groups(b, half)),
                "out": (added, routed_groups(b, half)),
                "turnx": (turnx_out, routed_groups(b, half)),
                "gate": (logits_out, b),
                "rank": (carried, b + 1),
            }[kind]

        def before(b, job):
            bank = BANK_OF[job[0]] if job[0] in BANK_OF else BANK_OF[f"{job[0]}{job[2]}"]
            tail = isinstance(b, int) and b == B
            jobs = TAIL_JOBS[bank] if tail else BANK_JOBS[bank]
            if isinstance(b, int) and b == 0:
                jobs = [j for j in jobs if j[0] not in ROUTING and j != ("turn", -1, 1)]
            i = jobs.index(job)
            return reader_done(b, jobs[i - 1]) if i else reader_done(b - 1, BANK_JOBS[bank][-1])

        def misc_of(kind, half):
            return misc[BANK_OF[kind] if kind in BANK_OF else BANK_OF[f"{kind}{half}"]]

        def pad(eng, experts):
            eng.wait_ge(pad_ready, 1)
            eng.wait_ge(pad_in, 16)
            for e in experts:
                at = eng.value_load(pad_at[0:1, e:e + 1], min_val=0, max_val=DUMMY)
                eng.dma_start(by_expert[bass.ds(at, P), :], pad_row[:]).then_inc(padded, 16)

        @block.sync
        def _(sp):
            sp.dma_start(latent[:], io["latent"]).then_inc(weights_in, 16)
            sp.dma_start(kr[:], io["W_KR"]).then_inc(kr_in, 16)
            sp.dma_start(xT[:], io["x_T"][0]).then_inc(xT_in, 16)
            sp.dma_start(rope_cs[:], io["rope_cs"]).then_inc(const_in, 16)
            sp.dma_start(const[:], io["const"]).then_inc(tables_in, 16)

            def spill(par, part, stacked):
                if stacked is not None:
                    sp.wait_ge(stack_in[par], stacked)
                    sp.sem_inc(sp_seen, 1)
                for s in range(SPLITS):
                    sp.wait_ge(part_ready[s], part)
                    sp.dma_start(q_spill[par][s].rearrange("r h s -> (r h) s"),
                                 parts[CONTQ:ROPEK, s, :]).then_inc(spilled, 16)
                    sp.dma_start(k_spill[par][s, 0:DH].rearrange("r h s -> (r h) s"),
                                 parts[CONTK:CONTK + HG * DH, s, :]).then_inc(spilled, 16)
                    sp.dma_start(k_spill[par][s, DH:DH + DR],
                                 parts[ROPEK:ROPEK + DR, s, :].unsqueeze(1).to_broadcast([DR, HG, S])
                                 ).then_inc(spilled, 16)

            def stack(par):
                qs = q_spill[par].rearrange("s r h t -> (s r) (h t)")
                ks = k_spill[par].rearrange("s r h t -> (s r) (h t)")
                block_rows, head_rows = SPLITS * (DH + DR), DH + DR
                qd = q_stack[par][:].rearrange("r h t -> r (h t)")
                kd = k_stack[par][:].rearrange("r h t -> r (h t)")
                for g in range(SPLITS):
                    r0 = g * block_rows
                    mid = r0 + (SPLITS - g) * head_rows
                    sp.dma_start(qd[r0:r0 + block_rows], qs).then_inc(stack_in[par], 16)
                    sp.dma_start(kd[r0:mid], ks[g * head_rows:]).then_inc(stack_in[par], 16)
                    if g:
                        sp.dma_start(kd[mid:r0 + block_rows], ks[0:g * head_rows]).then_inc(stack_in[par], 16)

            def load_rows(group, sent):
                if counted(sent):
                    sp.wait_ge(routed, sent)
                for q in range(Q):
                    sp.dma_start(xrow[q][:], io["x_rows"][group[q]].rearrange("(t p) w -> p t w", p=P)
                                 ).then_inc(x_rows_in, 16)

            def value(n):
                return n if isinstance(n, int) else sp.snap(n)

            def batch(b):
                for hg in range(NHG):
                    n_spilled = value(b * (NHG * SPILLS * 16) + (hg + 2) * (SPILLS * 16))
                    n_scored = value(b * BB + (hg * NBK + 1))
                    n_part = value(b * NHG + (hg + 3))
                    n_stacked = value(b * (2 * STACKS * 16) + (hg // 2 + 1) * (STACKS * 16))
                    n_sent = value(b * (Q * QT * 16))
                    n_projected = value(halves(b, NHG - 1, 1))
                    group = [value(b * Q + q) for q in range(Q)]
                    next_batch = value(b + 1)
                    sp.wait_ge(spilled, n_spilled)
                    sp.sem_inc(sp_seen, 1)
                    sp.wait_ge(scored, n_scored)
                    stack((hg + 1) % 2)
                    if hg == 1:
                        sp.wait_ge(projected, n_projected)
                        sp.dma_start(xT[:], io["x_T"][next_batch]).then_inc(xT_in, 16)
                    spill(hg % 2, n_part, n_stacked)
                    if hg == NHG - 1:
                        load_rows(group, n_sent)
                    if isinstance(b, int):
                        load_later(hg)

            def load_later(hg):
                if hg == 0:
                    sp.dma_start(w_o[:], io["W_O"]).then_inc(out_w_in, 16)
                    sp.dma_start(gate_wT[:], io["gate_w_T"]).then_inc(gate_in, 16)
                    sp.dma_start(gate_bias[:, 0, :], io["gate_b"].to_broadcast([P, E])).then_inc(gate_in, 16)
                    sp.dma_start(gate_bias[:, 1, :], io["expert_bias"].to_broadcast([P, E])).then_inc(gate_in, 16)
                    sp.dma_start(pad_row[:], io["pad_rows"]).then_inc(pad_in, 16)
                    sp.wait_ge(pad_in, 16)
                    sp.dma_start(by_expert[DUMMY:DUMMY + P, :], pad_row[:]).then_inc(dummy_out, 16)
                    sp.dma_start(b2[:], io["b2"].to_broadcast([P, E * D])).then_inc(mlp_in, 16)
                if hg == 1:
                    sp.dma_start(w1[:].rearrange("d (e f) -> d e f", e=E),
                                 io["w1"].rearrange("e d f -> d e f")).then_inc(mlp_in, 16)
                if hg == 2:
                    sp.dma_start(w2[:].rearrange("p (e c) d -> p e c d", e=E),
                                 io["w2"].rearrange("e (c p) d -> p e c d", p=P)).then_inc(mlp_in, 16)
                if hg == 3:
                    sp.dma_start(b1T[:], io["b1_T"]).then_inc(mlp_in, 16)

            spill(0, 1, None)
            sp.wait_ge(spilled, SPILLS * 16)
            stack(0)
            spill(1, 2, None)
            batch(0)
            with sp.Fori(1, B) as b:
                batch(b)
            sp.wait_ge(spilled, (B * NHG + 2) * SPILLS * 16)
            sp.wait_ge(stack_in[0], (B * NHG // 2 + 1) * STACKS * 16)
            sp.wait_ge(stack_in[1], B * NHG // 2 * STACKS * 16)
            sp.wait_ge(xT_in, (B + 1) * 16)
            sp.wait_ge(dummy_out, 16)

            pad(sp, range(E // 2))
            sp.wait_ge(routed, N // P * 16)
            sp.wait_ge(padded, E * 16)
            sp.wait_ge(planned, 2)

            def load_tile(r, c):
                used = value(r * RING + (c - RING + 1))
                row = sp.value_load(tile_entry(row_tab, r, c), min_val=0, max_val=DUMMY)
                if counted(used):
                    sp.wait_ge(xs_turned, used)
                    sp.sem_inc(sp_seen, 1)
                    sp.wait_ge(ids_ready, used)
                sp.dma_start(xs[c % RING][:], by_expert[bass.ds(row, P), :]).then_inc(xs_in[c % RING], 16)

            for c in range(RING):
                load_tile(0, c)
            rounds = (TILES - RING) // RING
            with sp.Fori(0, rounds) as r:
                for c in range(RING, 2 * RING):
                    load_tile(r, c)
            for c in range((rounds + 1) * RING, TILES):
                load_tile(0, c)

        @block.gpsimd
        def _(pool):
            pool.memset(ident[:], 0.0).then_inc(ident_ready, 1)
            pool.memset(mask_hi[:], P_HI).then_inc(mask_ready, 1)
            pool.wait_ge(ident_ready, 1)
            pool.affine_select(out=ident[:], in_=ident[:], compare_op=ALU.not_equal, fill=1.0, base=0,
                               pattern=[[-1, P]], channel_multiplier=1).then_inc(ident_ready, 1)
            pool.wait_ge(mask_ready, 1)
            pool.affine_select(out=mask_hi[:], in_=mask_hi[:], compare_op=ALU.is_ge, fill=0.0, base=0,
                               pattern=[[1, P]], channel_multiplier=-1).then_inc(mask_ready, 1)
            for i in range(2):
                pool.memset(v_stat[i][:], 0.0).then_inc(v_pad, 1)
            pool.wait_ge(v_pad, 2)
            for i in range(2):
                pool.memset(v_stat[i][:, :, :, i * VS + DH:(i + 1) * VS], 1.0).then_inc(v_pad, 1)

            def v_slice(hg, par):
                pool.sem_inc(pool_seen, 1)
                pool.tensor_copy(v_stat[par][:, :, :, par * VS:par * VS + DH],
                                 v_tok[:, :, hg * HG:(hg + 1) * HG, :]).then_inc(v_ready, 1)

            def rope(b, hg, c):
                n = halves(b, hg, c)
                t = slice(c * QC, (c + 1) * QC)
                pool.wait_ge(content_out, n)
                pool.tensor_tensor(full[0:ROPE_END, t], full[0:ROPE_END, t], rope_cs[0:ROPE_END, t],
                                   ALU.mult).then_inc(rope_mul, 1)
                pool.wait_ge(partner_out, n)
                pool.wait_ge(rope_mul, n if isinstance(n, int) and n < 2 else n - 1)
                pool.tensor_tensor(full[0:ROPE_END, t], full[0:ROPE_END, t], rope_b[0:ROPE_END, t],
                                   ALU.add).then_inc(rope_out, 1)

            def rest0(k):
                pool.wait_ge(part_ready[0], k + 1)
                if isinstance(k, int) and k == 1:
                    pool.wait_ge(part_ready[2], 1)
                pool.tensor_tensor(rest[:], full[:], parts[:, 0, :], ALU.subtract).then_inc(rest_ready, 1)

            def part1(k):
                pool.tensor_tensor(parts[:, 1, :], full[:], parts[:, 0, :], ALU.subtract).then_inc(part_ready[1], 1)

            def part2(k):
                pool.wait_ge(rest_ready, k + 1)
                pool.wait_ge(part_ready[1], k + 1)
                pool.tensor_tensor(parts[:, 2, :], rest[:], parts[:, 1, :], ALU.subtract).then_inc(part_ready[2], 1)

            def inverse_std(b, q):
                pool.wait_ge(var_ready, routed_groups(b, q))
                pool.tensor_tensor(rstd[q][:], var_eps[q][:], const[:, CONST["half"]], ALU.pow).then_inc(rstd_ready, 1)

            def route(b, q):
                pool.wait_ge(index_ready, b + q if isinstance(b, int) else b)
                pool.sem_inc(pool_seen, 1)
                for t in range(q * QT, (q + 1) * QT):
                    pool.indirect_dma_start(by_expert, bass.IndirectOffsetOnAxis(ap=index[:, t:t + 1], axis=0),
                                            xrow[t // QT][:, t % QT, :], None).then_inc(routed, 16)

            def batch(b):
                for hg in range(NHG):
                    k = b * NHG + (hg + 2)
                    if hg == 2 and not isinstance(b, int):
                        inverse_std(b, 1)
                    rope(b, hg + 2, 0)
                    if hg < NHG - 1:
                        if counted(b * GB + hg * NG):
                            pool.wait_ge(weighted, b * GB + hg * NG)
                        v_slice(hg + 1, (hg + 1) % 2)
                    if hg == 1 and not isinstance(b, int):
                        inverse_std(b, 0)
                    if hg == NHG - 1 and not isinstance(b, int):
                        route(b, 0)
                    rope(b, hg + 2, 1)
                    if hg == NHG - 1 and not isinstance(b, int):
                        route(b, 1)
                    rest0(k)
                    part1(k)
                    part2(k)
                    if hg == NHG - 1:
                        pool.wait_ge(v_out, b * 2 + 4)
                        pool.wait_ge(weighted, b * GB + hg * NG)
                        v_slice(0, 0)

            pool.wait_ge(const_in, 16)
            pool.wait_ge(v_pad, 4)
            rope(0, 0, 0)
            pool.wait_ge(part_ready[0], 1)
            part1(0)
            rope(0, 1, 0)
            rope(0, 1, 1)
            rest0(1)
            part1(1)
            part2(1)
            pool.wait_ge(v_out, 2)
            v_slice(0, 0)
            pool.wait_ge(tables_in, 16)
            batch(0)
            with pool.Fori(1, B) as b:
                batch(b)
            for q in range(Q):
                inverse_std(B, q)
            for q in range(Q):
                route(B, q)
            pool.wait_ge(planned, 2)
            pool.wait_ge(mlp_in, 4 * 16)

            def residual(r, c):
                e = pool.value_load(tile_entry(expert_tab, r, c), min_val=0, max_val=E - 1)
                if counted(r * RING + (c - 2)):
                    pool.wait_ge(y_out, r * RING + (c - 2))
                if counted(r * 16 + (c // RING) * 16):
                    pool.wait_ge(written[c % RING], r * 16 + (c // RING) * 16)
                pool.wait_ge(xs_in[c % RING], r * 16 + (c // RING + 1) * 16)
                pool.tensor_tensor(x_b2[c % STAGES][:], xs[c % RING][:, 0:D], b2[:, bass.ds(e * D, D)],
                                   ALU.add).then_inc(x_b2_ready, 1)
                pool.tensor_copy(ids[c % RING][:], xs[c % RING][:, D:D + 1].bitcast(U32)).then_inc(ids_ready, 1)

            def y_inverse_std(r, c):
                pool.wait_ge(y_vared, r * RING + (c + 1))
                pool.tensor_tensor(y_rstd[c % 2][:], y_var[c % 2][:], const[:, CONST["half"]][:, 0:1],
                                   ALU.pow).then_inc(y_rstd_ready, 1)

            def write(r, c):
                pool.wait_ge(ids_ready, r * RING + (c + 1))
                pool.wait_ge(z_ready, r * RING + (c + 1))
                pool.sem_inc(pool_seen, 1)
                pool.indirect_dma_start(
                    io["out"], bass.IndirectOffsetOnAxis(ap=ids[c % RING][:], axis=0),
                    zs[c % RING][:], None, bounds_check=N - 1, oob_is_err=False).then_inc(written[c % RING], 16)

            def steps(r, cs, live):
                for c in cs:
                    step(r, c, live)

            def step(r, c, live):
                if live(c):
                    residual(r, c)
                if live(c - 3):
                    write(r, c - 3)
                if live(c - 2):
                    y_inverse_std(r, c - 2)

            mlp_loop(pool, steps)
            for i in range(RING):
                pool.wait_ge(written[i], len(range(i, TILES, RING)) * 16)

        @block.vector
        def _(dve):
            dve.memset(w_hg[:], 0.0).then_inc(w_zero, 1)
            dve.memset(ones[:], 1.0)
            dve.memset(rope_b[0:ROPEQ], 0.0)
            dve.memset(onehot[:], 0.0)
            for q in range(Q):
                dve.memset(last_hot[q][:], 0.0)
            dve.wait_ge(w_zero, 1)
            dve.wait_ge(fused_mm, 1)
            dve.wait_ge(kr_in, 16)

            def by_element(ap, per_head):
                return ap.rearrange("p (g h d) -> p g d h", g=NHG, d=per_head)

            def rows(start, n):
                return w_hg[:, :, start:start + n * HG].rearrange("p g (d h) -> p g d h", h=HG)

            qr = by_element(misc[0][:, 128:128 + HEADS * DR], DR)
            dve.tensor_copy(rows(CONTQ, DH), by_element(misc[0][:, 0:128], DH))
            dve.tensor_copy(rows(ROPEQ, DR), qr)
            dve.tensor_copy(rows(CONTK, DH), by_element(misc[0][:, 192:320], DH))
            for e in range(2):
                dve.tensor_copy(rows(ROT, DR)[:, :, e::2, :], qr[:, :, 1 - e::2, :])
            dve.tensor_copy(w_hg[:, :, ROPEK:ROPEK + DR], kr[:].unsqueeze(1).to_broadcast([P, NHG, DR]))
            for e in range(2):
                dve.tensor_copy(w_hg[:, :, ROT + HG * DR + e:ROT + NROPE:2],
                                kr[:, 1 - e::2].unsqueeze(1).to_broadcast([P, NHG, DR // 2]))
            dve.tensor_copy(w_v[:], misc[0][:, 320:448]).then_inc(fused, 1)
            dve.wait_ge(const_in, 16)

            def take(b, hg, c, bank=misc[0]):
                n = halves(b, hg, c)
                t = slice(c * QC, (c + 1) * QC)
                dve.wait_ge(projected, n)
                if counted(b * NHG + hg):
                    dve.wait_ge(rest_ready, b * NHG + hg)
                    dve.wait_ge(part_ready[1], b * NHG + hg)
                dve.tensor_copy(full[:, t], bank[0:FROWS]).then_inc(content_out, 1)
                dve.tensor_tensor(rope_b[ROPEQ:ROPE_END, t], bank[ROT:ROT + NROPE], rope_cs[ROT:ROT + NROPE, t],
                                  ALU.mult).then_inc(partner_out, 1)

            def part0(k):
                dve.wait_ge(rope_out, k * 2 + 1)
                dve.wait_ge(spilled, k * (SPILLS * 16))
                dve.tensor_copy(parts[:, 0, :], full[:]).then_inc(part_ready[0], 1)

            def normalize(b, pair, qc):
                n = sums(b, pair, qc)
                dve.wait_ge(turned, n)
                o = misc_of("turn", qc)[:].rearrange("p (t h c) -> p t h c", h=HG, c=VW)
                inverse = rsum[:].rearrange("p (g t h) -> p g t h", g=2, h=HG)
                for g in range(2):
                    last = dve.reciprocal(inverse[:, g], o[:, :, :, g * VS + DH])
                last.then_inc(rsum_ready, 1)
                if pair == 0 and counted(routed_groups(b, qc)):
                    dve.wait_ge(flip_mm, routed_groups(b, qc))
                dve.wait_ge(rsum_ready, n)
                tiles = QC // P
                for g in range(2):
                    first_col = (pair % (NHG // 2) * 2 + g) * HG * DH
                    out = attn[:, qc * tiles:(qc + 1) * tiles, first_col:first_col + HG * DH]
                    last = dve.tensor_tensor(out.rearrange("p t (h d) -> p t h d", d=DH),
                                             o[:, :, :, g * VS:g * VS + DH],
                                             inverse[:, g].unsqueeze(3).to_broadcast([P, tiles, HG, DH]), ALU.mult)
                last.then_inc(attn_ready, 1)

            def clip(b, n):
                w = UNITS[n % NU][3]
                diag = UNITS[n % NU][1] * P >= UNITS[n % NU][0] * QC
                p = prob_ap(n)
                dve.wait_ge(exped, banks_up_to(b, n))
                if not diag or w > P:
                    rest_ = p[:, :, P if diag else 0:w]
                    last = dve.tensor_scalar(rest_, rest_, P_HI, P_LO, ALU.min, ALU.max)
                if diag:
                    d_ = p[:, :, 0:P]
                    last = dve.scalar_tensor_tensor(
                        out=d_, in0=d_, scalar=P_LO,
                        in1=mask_hi[:].unsqueeze(1).to_broadcast([P, len(UNITS[n % NU][2]), P]),
                        op0=ALU.max, op1=ALU.min)
                last.then_inc(clipped, 1)

            def add_x(b, q):
                g = routed_groups(b, q)
                x = xrow[q][:, :, 0:D]
                dve.wait_ge(out_mm, g)
                dve.wait_ge(x_rows_in, b * (Q * 16))
                dve.tensor_tensor(x, misc_of("out", q)[:].rearrange("p (t d) -> p t d", d=D), x,
                                  ALU.add).then_inc(added, 1)

            def moments(b, q):
                g = routed_groups(b, q)
                dve.wait_ge(added, g)
                for t in range(QT):
                    last = dve.bn_stats(stats[q][:, t, :], xrow[q][:, t, 0:D])
                last.then_inc(stats_ready, 1)
                dve.wait_ge(stats_ready, g)
                dve.sem_inc(dve_seen, 1)
                for t in range(QT):
                    last = dve.bn_aggr(mean_var[q][:, t, :], stats[q][:, t, :])
                last.then_inc(mean_ready, 1)
                dve.wait_ge(mean_ready, g)
                dve.tensor_scalar(var_eps[q][:], mean_var[q][:, :, 1], EPS, None, ALU.add).then_inc(var_ready, 1)

            def layernorm(b, q):
                g = routed_groups(b, q)
                dve.wait_ge(rstd_ready, g)
                for t in range(QT):
                    x = xrow[q][:, t, 0:D]
                    last = dve.tensor_scalar(x, x, mean_var[q][:, t, 0:1], rstd[q][:, t:t + 1],
                                             ALU.subtract, ALU.mult)
                last.then_inc(normed, 1)

            def choose(n, tiles, hot):
                count = len(tiles)

                def wide(ap):
                    return ap.unsqueeze(2).to_broadcast([P, count, E])

                def of(ap):
                    return ap[:, tiles[0]:tiles[0] + count]

                dve.wait_ge(gate_mm, n)
                dve.tensor_tensor(of(logits), misc_of("gate", 0)[:, 0:count * E].rearrange("p (t e) -> p t e", e=E),
                                  gate_bias[:, 0, :].unsqueeze(1).to_broadcast([P, count, E]),
                                  ALU.add).then_inc(logits_out, 1)
                dve.wait_ge(logits_out, n)
                dve.tensor_reduce(of(top), of(logits), AX.X, ALU.max).then_inc(top_ready, 1)
                dve.wait_ge(top_ready, n)
                dve.tensor_tensor(of(reach), of(logits), wide(of(top)), ALU.is_ge).then_inc(reach_ready, 1)
                dve.wait_ge(reach_ready, n)
                dve.tensor_tensor(of(order), of(reach),
                                  const[:, CONST["descend"]].unsqueeze(1).to_broadcast([P, count, E]),
                                  ALU.mult).then_inc(order_ready, 1)
                dve.wait_ge(order_ready, n)
                dve.tensor_reduce(of(first), of(order), AX.X, ALU.max).then_inc(first_ready, 1)
                dve.wait_ge(first_ready, n)
                dve.tensor_tensor(hot[:, 0:count, :], of(order), wide(of(first)),
                                  ALU.is_equal).then_inc(onehot_ready, 1)

            def assign(n, tiles, hot):
                count = len(tiles)

                def of(ap):
                    return ap[:, tiles[0]:tiles[0] + count]

                rank = misc_of("rank", 0)[:, 0:(count + 1) * E].rearrange("p (t e) -> p t e", e=E)
                dve.wait_ge(rank_mm, n)
                dve.wait_ge(carried, n)
                dve.tensor_tensor(of(place), rank[:, 0:count, :], next_row[:].unsqueeze(1).to_broadcast([P, count, E]),
                                  ALU.add).then_inc(placed, 1)
                dve.wait_ge(placed, n)
                dve.tensor_tensor(next_row[:], next_row[:], rank[:, count, :], ALU.add).then_inc(carried, 1)
                dve.tensor_tensor(of(chosen), of(place), hot[:, 0:count, :], ALU.mult).then_inc(chosen_ready, 1)
                dve.wait_ge(chosen_ready, n)
                dve.tensor_reduce(of(place_of), of(chosen), AX.X, ALU.add).then_inc(place_ready, 1)
                dve.wait_ge(place_ready, n)
                dve.tensor_copy(of(index), of(place_of)).then_inc(index_ready, 1)

            def batch(b):
                later = not isinstance(b, int)
                for hg in range(NHG):
                    for u in range(NU):
                        clip(b, hg * NU + u)
                        for c in range(2):
                            if due(f"project{c}", hg, u):
                                take(b, hg + 2, c)
                        if due("part0", hg, u):
                            part0(b * NHG + (hg + 2))
                        if due("turn1", hg, u) and (hg or later):
                            normalize(b, hg // 2 - 1, 1)
                        if due("turn0", hg, u):
                            normalize(b, hg // 2, 0)
                        for q in range(Q):
                            if later and due(f"out{q}", hg, u):
                                add_x(b, q)
                            if later and due(f"moments{q}", hg, u):
                                moments(b, q)
                            if later and due(f"norm{q}", hg, u):
                                layernorm(b, q)
                        if later and due("gate0", hg, u):
                            choose(b, range(NKT), onehot)
                        if later and due("rank0", hg, u):
                            assign(b, range(NKT), onehot)

            take(0, 0, 0, misc[0])
            take(0, 0, 1, misc[1])
            t = slice(QC, 2 * QC)
            dve.wait_ge(content_out, 2)
            dve.tensor_tensor(full[ROPEQ:ROPE_END, t], full[ROPEQ:ROPE_END, t], rope_cs[ROPEQ:ROPE_END, t],
                              ALU.mult).then_inc(first_mul, 1)
            dve.wait_ge(first_mul, 1)
            dve.wait_ge(partner_out, 2)
            dve.tensor_tensor(full[ROPEQ:ROPE_END, t], full[ROPEQ:ROPE_END, t], rope_b[ROPEQ:ROPE_END, t],
                              ALU.add).then_inc(first_rope, 1)
            dve.wait_ge(part_ready[0], 1)
            dve.tensor_tensor(rest[:], full[:], parts[:, 0, :], ALU.subtract).then_inc(rest_ready, 1)
            dve.wait_ge(part_ready[1], 1)
            dve.wait_ge(rest_ready, 1)
            dve.tensor_tensor(parts[:, 2, :], rest[:], parts[:, 1, :], ALU.subtract).then_inc(part_ready[2], 1)
            for c in range(2):
                take(0, 1, c, misc[c])
            part0(1)
            dve.wait_ge(tables_in, 16)
            dve.tensor_copy(upper[:], const[:, CONST["upper"]]).then_inc(upper_ready, 1)
            dve.tensor_copy(next_row[:], const[:, CONST["region"]]).then_inc(carried, 1)
            dve.wait_ge(mask_ready, 2)
            batch(0)
            dve.wait_ge(gate_in, 48)
            dve.tensor_tensor(gate_bias[:, 0, :], gate_bias[:, 0, :], gate_bias[:, 1, :], ALU.add).then_inc(bias_ready, 1)
            dve.wait_ge(bias_ready, 1)
            with dve.Fori(1, B) as b:
                batch(b)
            normalize(B, -1, 1)
            add_x(B, 0)
            moments(B, 0)
            add_x(B, 1)
            layernorm(B, 0)
            moments(B, 1)
            layernorm(B, 1)
            for q in range(Q):
                choose(B + q, range(q * QT, (q + 1) * QT), last_hot[q])
                assign(B + q, range(q * QT, (q + 1) * QT), last_hot[q])

            dve.wait_ge(carried, B + Q)
            dve.tensor_copy(pad_at[:], next_row[:]).then_inc(pad_ready, 1)
            dve.tensor_tensor(tokens_of[:], next_row[:], const[:, CONST["region"]], ALU.subtract).then_inc(plan, 1)
            dve.wait_ge(plan, 1)
            dve.tensor_tensor(begun[:], tokens_of[:].unsqueeze(2).to_broadcast([P, E, N // P]),
                              const[:, CONST["full_tiles"]].rearrange("p (e k) -> p e k", e=E),
                              ALU.is_gt).then_inc(plan, 1)
            dve.wait_ge(plan, 2)
            dve.tensor_reduce(tiles_of[:], begun[:], AX.X, ALU.add).then_inc(plan, 1)
            dve.wait_ge(plan, 3)
            dve.tensor_tensor(below[:], const[:, CONST["up_to"]].rearrange("p (e f) -> p e f", e=E),
                              tiles_of[:].unsqueeze(1).to_broadcast([P, E, E]), ALU.mult).then_inc(plan, 1)
            dve.tensor_scalar(skip_rows[:], tiles_of[:], -float(P), float(REGION), ALU.mult, ALU.add).then_inc(plan, 1)
            dve.wait_ge(plan, 5)
            dve.tensor_reduce(end_of[:], below[:], AX.X, ALU.add).then_inc(plan, 1)
            dve.wait_ge(plan, 6)
            dve.tensor_tensor(passed[:], const[:, CONST["tile"]].unsqueeze(2).to_broadcast([P, TILES, E]),
                              end_of[:].unsqueeze(1).to_broadcast([P, TILES, E]), ALU.is_ge).then_inc(plan, 1)
            dve.wait_ge(plan, 7)
            dve.tensor_reduce(tile_e[:], passed[:], AX.X, ALU.add).then_inc(plan, 1)
            dve.tensor_tensor(jump[:], passed[:], skip_rows[:].unsqueeze(1).to_broadcast([P, TILES, E]),
                              ALU.mult).then_inc(plan, 1)
            dve.wait_ge(plan, 9)
            dve.tensor_scalar(expert_tab[:], tile_e[:], float(E - 1), None, ALU.min).then_inc(planned, 1)
            dve.tensor_reduce(tile_sum[:], jump[:], AX.X, ALU.add).then_inc(plan, 1)
            dve.wait_ge(plan, 10)
            dve.tensor_tensor(tile_at[:], tile_sum[:], const[:, CONST["tile_row"]], ALU.add).then_inc(plan, 1)
            dve.wait_ge(plan, 11)
            dve.tensor_scalar(row_tab[:], tile_at[:], float(DUMMY), None, ALU.min).then_inc(planned, 1)

            def hidden_out(r, c):
                dve.wait_ge(up_mm, r * RING + (c + 1))
                if counted(r * RING + (c - 1)):
                    dve.wait_ge(h_turned, r * RING + (c - 1))
                dve.tensor_copy(hidden[c % 2], scores[2 + c % 2][:]).then_inc(hidden_ready, 1)

            def y_moments(r, c):
                n = r * RING + (c + 1)
                dve.wait_ge(down_mm, n)
                dve.wait_ge(x_b2_ready, n)
                dve.tensor_tensor(ys[c % 2][:], misc[c % 2][:, 0:D], x_b2[c % STAGES][:], ALU.add).then_inc(y_out, 1)
                dve.wait_ge(y_out, n)
                dve.bn_stats(y_stats[c % 2][:], ys[c % 2][:]).then_inc(y_stat, 1)
                dve.wait_ge(y_stat, n)
                dve.sem_inc(dve_seen, 1)
                dve.bn_aggr(y_mean[c % 2][:], y_stats[c % 2][:]).then_inc(y_meaned, 1)
                dve.wait_ge(y_meaned, n)
                dve.tensor_scalar(y_var[c % 2][:], y_mean[c % 2][:, 1:2], EPS, None, ALU.add).then_inc(y_vared, 1)

            def y_norm(r, c):
                dve.wait_ge(y_rstd_ready, r * RING + (c + 1))
                dve.tensor_scalar(zs[c % RING][:], ys[c % 2][:], y_mean[c % 2][:, 0:1], y_rstd[c % 2][:],
                                  ALU.subtract, ALU.mult).then_inc(z_ready, 1)

            def steps(r, cs, live):
                for c in cs:
                    step(r, c, live)

            def step(r, c, live):
                if live(c):
                    hidden_out(r, c)
                if live(c - 3):
                    y_norm(r, c - 3)
                if live(c - 2):
                    y_moments(r, c - 2)

            mlp_loop(dve, steps)

        @block.scalar
        def _(act):
            def v_evac(b, c):
                act.wait_ge(v_mm, b * 2 + (2 + c + 1))
                half = v_tok[:, c * (NKT // 2):(c + 1) * (NKT // 2)]
                act.activation(half.rearrange("p t h d -> p (t h d)"), misc_of("v", c)[:], ACT.Copy).then_inc(v_out, 1)

            def exp(b, n, m):
                act.wait_ge(scored, b * BB + (m + 1))
                if counted(groups_up_to(b, n - P_SLOTS)):
                    act.wait_ge(weighted, groups_up_to(b, n - P_SLOTS))
                _, start, heads = BANKS[m % NBK]
                act.activation(prob_ap(n)[:, start:start + heads], score_ap(m), ACT.Exp,
                               scale=SCALE).then_inc(exped, 1)

            def o_evac(b, pair, qc):
                act.wait_ge(weighted, b * GB + ((2 * pair + 1) * NG + QC_GROUPS[qc]))
                if counted(sums(b, pair - 1, qc)):
                    act.wait_ge(turned, sums(b, pair - 1, qc))
                act.activation(o_sb[qc][:], o_acc[qc][:], ACT.Copy).then_inc(o_out, 1)

            def flip_evac(kind, b, q):
                ready, done = {"flip": (flip_mm, flip_out), "turnx": (turnx_mm, turnx_out)}[kind]
                act.wait_ge(ready, routed_groups(b, q))
                act.activation(flipped[q][:], misc_of(kind, q)[:], ACT.Copy).then_inc(done, 1)

            def batch(b):
                later = not isinstance(b, int)
                for hg in range(NHG):
                    for u in range(NU):
                        for m in BANKS_OF[u]:
                            exp(b, hg * NU + u, hg * NBK + m)
                        if due("evac1", hg, u) and (hg or later):
                            o_evac(b, hg // 2 - 1, 1)
                        if due("evac0", hg, u):
                            o_evac(b, hg // 2, 0)
                        for c in range(2):
                            if due(f"v{c}", hg, u):
                                act.wait_ge(v_ready, b * NHG + NHG)
                                v_evac(b, c)
                        for q in range(Q):
                            for kind in ("flip", "turnx"):
                                if later and due(f"{kind}{q}", hg, u):
                                    flip_evac(kind, b, q)

            act.wait_ge(first_rope, 1)
            act.wait_ge(rope_out, 1)
            act.activation(parts[:, 0, :], full[:], ACT.Copy).then_inc(part_ready[0], 1)
            v_evac(-1, 0)
            v_evac(-1, 1)
            batch(0)
            with act.Fori(1, B) as b:
                batch(b)
            o_evac(B, -1, 1)
            for kind in ("flip", "turnx"):
                for q in range(Q):
                    flip_evac(kind, B, q)

            def xT_evac(r, c):
                act.wait_ge(xs_turned, r * RING + (c + 1))
                if counted(r * RING + (c - 1)):
                    act.wait_ge(up_mm, r * RING + (c - 1))
                act.activation(xsT[c % 2][:], scores[c % 2][:, 0:P], ACT.Copy).then_inc(xsT_ready, 1)

            def relu(r, c):
                e = act.value_load(tile_entry(expert_tab, r, c), min_val=0, max_val=E - 1)
                act.wait_ge(h_turned, r * RING + (c + 1))
                if counted(r * RING + (c - 1)):
                    act.wait_ge(down_mm, r * RING + (c - 1))
                for f in range(DFF // P):
                    t = slice(f * P, (f + 1) * P)
                    last = act.activation(hiddenT[c % 2][:, t], o_acc[c % 2][:, t], ACT.Relu,
                                          bias=b1T[:, bass.ds(e * (DFF // P) + f, 1)])
                last.then_inc(hiddenT_ready, 1)

            def steps(r, cs, live):
                for c in cs:
                    step(r, c, live)

            def step(r, c, live):
                if live(c + 1):
                    xT_evac(r, c + 1)
                if live(c - 1):
                    relu(r, c - 1)

            pad(act, range(E // 2, E))
            act.wait_ge(planned, 2)
            act.wait_ge(mlp_in, 4 * 16)
            xT_evac(0, 0)
            mlp_loop(act, steps)

        @block.tensor
        def _(pe):
            def weight(name):
                return latent[:, LATENT_COLS[name]]

            pe.wait_ge(weights_in, 16)
            pe.matmul(misc[0][:, 0:128], weight("W_DQ_T"), weight("W_UQ"), start=True, stop=True)
            pe.matmul(misc[0][:, 128:192], weight("W_DQ_T"), weight("W_QR"), start=True, stop=True)
            pe.matmul(misc[0][:, 192:320], weight("W_DKV_T"), weight("W_UK"), start=True, stop=True)
            pe.matmul(misc[0][:, 320:448], weight("W_DKV_T"), weight("W_UV"), start=True, stop=True).then_inc(fused_mm, 1)

            def project(c, hg, bank):
                pe.matmul(bank[:], w_hg[:, hg, :], xT[:, c * QC:(c + 1) * QC],
                          start=True, stop=True).then_inc(projected, 1)

            def v_rows(c):
                for t in range(QC // P):
                    last = pe.matmul(misc_of("v", c)[:, t * P:(t + 1) * P],
                                     xT[:, c * QC + t * P:c * QC + (t + 1) * P], w_v[:], start=True, stop=True)
                last.then_inc(v_mm, 1)

            def score(b, m):
                unit, start, count = BANKS[m % NBK]
                _, kt, heads, w = UNITS[unit]
                qc = UNITS[unit][0]
                par = m // NBK % 2
                old = m - SCORE_SLOTS if m >= SCORE_SLOTS else \
                    max(i for i in range(BB) if i % SCORE_SLOTS == m % SCORE_SLOTS) - BB
                if counted(b * BB + (old + 1)):
                    pe.wait_ge(exped, b * BB + (old + 1))
                out = score_ap(m)
                for i in range(count):
                    j = heads[start + i]
                    last = pe.matmul(out[:, i, :], k_stack[par][:, j, kt * P:(kt + 1) * P],
                                     q_stack[par][:, j, (qc + 1) * QC - w:(qc + 1) * QC], start=True, stop=True)
                last.then_inc(scored, 1)

            def weigh(b, n):
                if n % NU not in LAST_UNIT:
                    return
                g, hg = LAST_UNIT.index(n % NU), n // NU
                qc, kt = GROUPS[g]
                par = hg % 2
                pe.wait_ge(clipped, b * UB + (n + 1))
                if kt == 0:
                    if qc == 0:
                        pe.wait_ge(v_ready, b * NHG + (hg + 1))
                    if hg % 2 == 0 and counted(sums(b, hg // 2 - 1, qc)):
                        pe.wait_ge(o_out, sums(b, hg // 2 - 1, qc))
                for u in range(NU):
                    if GROUP_OF[u] == g:
                        _, _, heads, w = UNITS[u]
                        p = prob_ap(hg * NU + u)
                        for i, j in enumerate(heads):
                            last = pe.matmul(o_acc[qc][j * VW:(j + 1) * VW, QC - w:QC], v_stat[par][:, kt, j, :],
                                             p[:, i, :], start=kt == 0 and hg % 2 == 0,
                                             stop=g + 1 == QC_GROUPS[qc] and hg % 2 == 1,
                                             skip_group_check=True)
                last.then_inc(weighted, 1)

            def turn(b, pair, qc):
                pe.wait_ge(o_out, sums(b, pair, qc))
                free = before(b, ("turn", pair, qc))
                if counted(free[1]):
                    pe.wait_ge(*free)
                for t in range(QC // P):
                    last = pe.transpose(misc_of("turn", qc)[:, t * P:(t + 1) * P], o_sb[qc][:, t * P:(t + 1) * P],
                                        ident[:])
                last.then_inc(turned, 1)

            def routing(b, hg, kind, q):
                g = routed_groups(b, q)
                bank = misc_of(kind, q)
                pe.wait_ge(*before(b, (kind, hg, q)))
                if kind == "flip":
                    pe.wait_ge(attn_ready, sums(b, -1, 1))
                    for t in range(QT):
                        last = pe.transpose(bank[:, t * P:(t + 1) * P], attn[:, q * QT + t, :], ident[:])
                    last.then_inc(flip_mm, 1)
                elif kind == "out":
                    pe.wait_ge(flip_out, g)
                    pe.wait_ge(out_w_in, 16)
                    for t in range(QT):
                        last = pe.matmul(bank[:, t * D:(t + 1) * D], flipped[q][:, t * P:(t + 1) * P], w_o[:],
                                         start=True, stop=True)
                    last.then_inc(out_mm, 1)
                elif kind == "turnx":
                    pe.wait_ge(normed, g)
                    for t in range(QT):
                        last = pe.transpose(bank[:, t * P:(t + 1) * P], xrow[q][:, t, 0:D], ident[:])
                    last.then_inc(turnx_mm, 1)
                elif kind == "gate":
                    gate(b, range(NKT), bank)
                else:
                    rank(b, range(NKT), bank, onehot)

            def gate(b, tiles, bank):
                pe.wait_ge(gate_in, 48)
                for i, t in enumerate(tiles):
                    if t % QT == 0:
                        pe.wait_ge(turnx_out, routed_groups(b, t // QT))
                    turned_x = flipped[t // QT][:, t % QT * P:(t % QT + 1) * P]
                    last = pe.matmul(bank[:, i * E:(i + 1) * E], turned_x, gate_wT[:], start=True, stop=True)
                last.then_inc(gate_mm, 1)

            def rank(n, tiles, bank, hot):
                pe.wait_ge(onehot_ready, n)
                pe.wait_ge(upper_ready, 1)
                count = len(tiles)
                rows = hot[:].rearrange("p t e -> p (t e)")
                width = (count + 1) * E
                pe.matmul(bank[:, 0:width], upper[:], rows, start=True, stop=False, skip_group_check=True)
                for s in range(1, count + 1):
                    last = pe.matmul(bank[:, s * E:width], ones[:], rows[:, 0:width - s * E],
                                     start=False, stop=s == count, skip_group_check=True)
                last.then_inc(rank_mm, 1)

            def batch(b):
                later = not isinstance(b, int)
                for hg in range(NHG):
                    n_stack = STACKS * 16
                    pe.wait_ge(stack_in[hg % 2], b * (2 * n_stack) + (hg // 2 + 1) * n_stack)
                    for u in range(NU):
                        n = hg * NU + u
                        for m in BANKS_OF[u]:
                            score(b, hg * NBK + m)
                        if n >= LAG or later:
                            weigh(b, n - LAG)
                        for c in range(2):
                            if due(f"project{c}", hg, u):
                                if hg == 2 and c == 0:
                                    pe.wait_ge(xT_in, b * 16 + 32)
                                pe.wait_ge(*before(b, ("project", hg, c)))
                                project(c, (hg + 2) % NHG, misc_of("project", c))
                            if due(f"v{c}", hg, u):
                                pe.wait_ge(*before(b, ("v", hg, c)))
                                v_rows(c)
                        if due("turn1", hg, u) and (hg or later):
                            turn(b, hg // 2 - 1, 1)
                        if due("turn0", hg, u):
                            turn(b, hg // 2, 0)
                        for q in range(Q):
                            for kind in ROUTING:
                                if later and f"{kind}{q}" in STEPS and due(f"{kind}{q}", hg, u):
                                    routing(b, hg, kind, q)

            pe.wait_ge(fused, 1)
            pe.wait_ge(xT_in, 16)
            project(0, 0, misc[0])
            project(1, 0, misc[1])
            for c in range(2):
                pe.wait_ge(partner_out, c + 1)
                project(c, 1, misc[c])
            pe.wait_ge(partner_out, 4)
            v_rows(0)
            v_rows(1)
            pe.wait_ge(ident_ready, 2)
            batch(0)
            with pe.Fori(1, B) as b:
                batch(b)
            for n in range(-LAG, 0):
                weigh(B, n)
            turn(B, -1, 1)
            for kind in ("flip", "out"):
                for q in range(Q):
                    routing(B, STEPS[f"{kind}{q}"][0][0], kind, q)
            first_tiles, last_tiles = range(QT), range(QT, NKT)
            routing(B, STEPS["turnx0"][0][0], "turnx", 0)
            pe.wait_ge(added, B * Q)
            gate(B, first_tiles, misc_of("gate", 0))
            routing(B, STEPS["turnx1"][0][0], "turnx", 1)
            pe.wait_ge(turnx_out, B * Q)
            rank(B, first_tiles, misc_of("rank", 0), last_hot[0])
            pe.wait_ge(logits_out, B)
            gate(B, last_tiles, misc_of("gate", 0))
            pe.wait_ge(carried, B + 1)
            rank(B + 1, last_tiles, misc_of("rank", 0), last_hot[1])

            pe.wait_ge(exped, B * BB)
            pe.wait_ge(carried, B + Q)
            pe.wait_ge(planned, 2)
            pe.wait_ge(mlp_in, 4 * 16)

            def turn_x(r, c):
                pe.wait_ge(xs_in[c % RING], r * 16 + (c // RING + 1) * 16)
                if counted(r * RING + (c - 1)):
                    pe.wait_ge(xsT_ready, r * RING + (c - 1))
                pe.transpose(scores[c % 2][:, 0:P], xs[c % RING][:, 0:D], ident[:]).then_inc(xs_turned, 1)

            def up_rows(r, c, e):
                pe.wait_ge(xsT_ready, r * RING + (c + 1))
                if counted(r * RING + (c - 1)):
                    pe.wait_ge(hidden_ready, r * RING + (c - 1))
                pe.matmul(scores[2 + c % 2][:], xsT[c % 2][:], w1[:, bass.ds(e * DFF, DFF)],
                          start=True, stop=True).then_inc(up_mm, 1)

            def turn_hidden(r, c):
                pe.wait_ge(hidden_ready, r * RING + (c + 1))
                if counted(r * RING + (c - 1)):
                    pe.wait_ge(hiddenT_ready, r * RING + (c - 1))
                for f in range(DFF // P):
                    last = pe.transpose(o_acc[c % 2][:, f * P:(f + 1) * P], hidden[c % 2][:, f * P:(f + 1) * P],
                                        ident[:])
                last.then_inc(h_turned, 1)

            def down_rows(r, c, e):
                pe.wait_ge(hiddenT_ready, r * RING + (c + 1))
                if counted(r * RING + (c - 1)):
                    pe.wait_ge(y_out, r * RING + (c - 1))
                w2_cols = w2[:].rearrange("p c d -> p (c d)")
                for f in range(DFF // P):
                    last = pe.matmul(misc[c % 2][:, 0:D], hiddenT[c % 2][:, f * P:(f + 1) * P],
                                     w2_cols[:, bass.ds(e * DFF + f * D, D)], start=f == 0, stop=f == DFF // P - 1)
                last.then_inc(down_mm, 1)

            def steps(r, cs, live):
                loaded = {}

                def expert(c):
                    if c not in loaded:
                        loaded[c] = pe.value_load(tile_entry(expert_tab, r, c), min_val=0, max_val=E - 1)
                    return loaded[c]

                for c in cs:
                    if live(c):
                        up_rows(r, c, expert(c))
                    if c + 1 in cs and live(c + 1):
                        expert(c + 1)
                    if live(c - 1):
                        turn_hidden(r, c - 1)
                    if live(c + 1):
                        turn_x(r, c + 1)
                    if live(c - 2):
                        down_rows(r, c - 2, expert(c - 2))

            turn_x(0, 0)
            mlp_loop(pe, steps)


def rope_table():
    inv = np.float32(THETA) ** (-np.arange(0, DR, 2, dtype=np.float32) / np.float32(DR))
    ang = np.arange(S, dtype=np.float32)[None, :] * inv.astype(np.float32)[:, None]
    table = np.zeros((P, S), np.float32)
    table[CONTQ:ROPEQ] = 1.0
    for r in range(NROPE):
        d = r // HG if r < HG * DR else r - HG * DR
        table[ROPEQ + r] = np.cos(ang[d // 2])
        table[ROT + r] = np.sin(ang[d // 2]) * (np.float32(1.0) if d % 2 else np.float32(-1.0))
    return table


def constants():
    p = np.arange(P, dtype=np.float32)
    table = np.zeros((P, CONST_W), np.float32)
    table[:, CONST["upper"]] = p[:, None] < p[None, :]
    table[:, CONST["descend"]] = E - np.arange(E)
    table[:, CONST["region"]] = REGION * np.arange(E)
    table[:, CONST["full_tiles"]] = np.tile(P * np.arange(N // P), E)
    table[:, CONST["up_to"]] = (np.arange(E)[:, None] >= np.arange(E)[None, :]).reshape(-1)
    table[:, CONST["tile"]] = np.arange(TILES)
    table[:, CONST["tile_row"]] = P * np.arange(TILES)
    table[:, CONST["half"]] = -0.5
    return table


def with_ids(rows, ids):
    out = np.zeros((rows.shape[0], ROW), np.int32)
    out[:, 0:D] = np.ascontiguousarray(rows).view(np.int32)
    out[:, D] = ids
    return out.view(np.float32)


def kernel(**inputs):
    import concourse.bacc as bacc
    from concourse.bass_utils import run_bass_kernel_spmd

    a = {k: np.asarray(v) for k, v in inputs.items()}
    x = a["L0_attn_x"]
    x_T = x.transpose(0, 2, 1)
    latent = {"W_DQ_T": a["L0_attn_W_DQ"].T, "W_DKV_T": a["L0_attn_W_DKV"].T,
              **{name: a["L0_attn_" + name] for name in ("W_UQ", "W_QR", "W_UK", "W_UV")}}
    arrays = {
        "x_T": np.concatenate([x_T, x_T[:1]]),
        "x_rows": with_ids(x.reshape(N, D), np.arange(N)).reshape(2 * B, S // 2, ROW),
        "pad_rows": with_ids(np.zeros((P, D), np.float32), N + np.arange(P)),
        "latent": np.concatenate([latent[name] for name in LATENT_COLS], axis=1),
        "W_KR": a["L0_attn_W_KR"], "W_O": a["L0_attn_W_O"],
        "gate_w_T": np.ascontiguousarray(a["L0_ffn_gate_w"].T),
        "gate_b": a["L0_ffn_gate_b"].reshape(1, E), "expert_bias": a["L0_ffn_expert_bias"].reshape(1, E),
        "w1": a["L0_ffn_w1"], "b1_T": np.ascontiguousarray(a["L0_ffn_b1"].reshape(E * DFF // P, P).T),
        "w2": a["L0_ffn_w2"], "b2": a["L0_ffn_b2"].reshape(1, E * D),
        "rope_cs": rope_table(),
        "const": constants(),
    }
    nc = bacc.Bacc("TRN2", target_bir_lowering=False, num_devices=1)
    io = {k: nc.dram_tensor("in_" + k, v.shape, mybir.dt.from_np(v.dtype), kind="ExternalInput").ap()
          for k, v in arrays.items()}
    io["out"] = nc.dram_tensor("out", (N, D), F32, kind="ExternalOutput").ap()
    build(nc, io)
    r = run_bass_kernel_spmd(nc, [{"in_" + k: v for k, v in arrays.items()}], core_ids=[0])
    return r.results[0]["out"].reshape(B, S, D)
```
